# Optimizing a Trainium2 kernel written in Bass

```python
import numpy as np
import jax
import jax.numpy as jnp

def _softmax(x, axis=-1):
    return jax.nn.softmax(x, axis=axis)

def _gelu(x):
    return jax.nn.gelu(x, approximate=True)

def _silu(x):
    return jax.nn.silu(x)

def _sigmoid(x):
    return jax.nn.sigmoid(x)

def _layernorm(x, axis=-1, eps=1e-05):
    m = jnp.mean(x, axis=axis, keepdims=True)
    v = jnp.var(x, axis=axis, keepdims=True)
    return (x - m) / jnp.sqrt(v + eps)

def _scatter_add(tgt, idx, src, axis=0):
    return tgt.at[idx].add(src)

def _segment_sum(src, seg, n):
    return jax.ops.segment_sum(src, seg, n)
kernel_name = 'mk_sandwich_d1_jaxref_r8_a1e629'

def setup_inputs(seed: int=0):
    np.random.seed(seed)
    _w = jnp.asarray

    def _L0_attn_setup():
        import jax, jax.numpy as jnp
        import numpy as np
        D_MODEL = 256
        N_HEADS = 16
        D_HEAD = D_MODEL // N_HEADS
        key = jax.random.key(seed)
        ks = jax.random.split(key, 5)
        s = 0.02
        return {'x': jax.random.normal(ks[0], (4, 256, D_MODEL), dtype=jnp.float32), 'Wq': jax.random.normal(ks[1], (D_MODEL, D_MODEL), dtype=jnp.float32) * s, 'Wk': jax.random.normal(ks[2], (D_MODEL, D_MODEL), dtype=jnp.float32) * s, 'Wv': jax.random.normal(ks[3], (D_MODEL, D_MODEL), dtype=jnp.float32) * s, 'Wo': jax.random.normal(ks[4], (D_MODEL, D_MODEL), dtype=jnp.float32) * s}
    _L0_attn_in = _L0_attn_setup()

    def _L0_ffn_setup():
        import jax, jax.numpy as jnp
        import numpy as np
        H = 256
        NH = 32
        KVH = 4
        HD = 128
        E = 32
        TOPK = 8
        I = 128
        EPS = 1e-05
        THETA = 10000.0

        def _rmsnorm(x, w, eps=EPS):
            xf = x.astype(jnp.float32)
            var = jnp.mean(xf * xf, axis=-1, keepdims=True)
            return (w * (xf * jax.lax.rsqrt(var + eps))).astype(x.dtype)

        def _rope(x, pos):
            d = x.shape[-1]
            inv_freq = 1.0 / THETA ** (jnp.arange(0, d, 2, dtype=jnp.float32) / d)
            ang = pos.astype(jnp.float32)[:, None] * inv_freq[None, :]
            cos = jnp.cos(ang)[None, :, None, :]
            sin = jnp.sin(ang)[None, :, None, :]
            x1, x2 = jnp.split(x, 2, axis=-1)
            return jnp.concatenate([x1 * cos - x2 * sin, x1 * sin + x2 * cos], axis=-1)
        key = jax.random.key(seed)
        ks = jax.random.split(key, 16)
        s = 0.02
        n = lambda k, shape: jax.random.normal(k, shape, dtype=jnp.float32) * s
        return {'hidden_states': jax.random.normal(ks[0], (1, 64, H), dtype=jnp.float32), 'ln1_w': jnp.ones((H,), jnp.float32), 'ln2_w': jnp.ones((H,), jnp.float32), 'Wq': n(ks[1], (H, NH * HD)), 'Wk': n(ks[2], (H, KVH * HD)), 'Wv': n(ks[3], (H, KVH * HD)), 'Wo': n(ks[4], (NH * HD, H)), 'Wr': n(ks[5], (H, E)), 'expert_bias': jax.random.normal(ks[6], (E,), dtype=jnp.float32) * 0.1, 'Wg': n(ks[7], (E, H, I)), 'Wu': n(ks[8], (E, H, I)), 'Wd': n(ks[9], (E, I, H)), 'Wsg': n(ks[10], (H, I)), 'Wsu': n(ks[11], (H, I)), 'Wsd': n(ks[12], (I, H))}
    _L0_ffn_in = _L0_ffn_setup()
    _d = {'L0_attn_x': _L0_attn_in['x'], 'L0_attn_Wq': _L0_attn_in['Wq'], 'L0_attn_Wk': _L0_attn_in['Wk'], 'L0_attn_Wv': _L0_attn_in['Wv'], 'L0_attn_Wo': _L0_attn_in['Wo'], 'L0_ffn_ln1_w': _L0_ffn_in['ln1_w'], 'L0_ffn_ln2_w': _L0_ffn_in['ln2_w'], 'L0_ffn_Wq': _L0_ffn_in['Wq'], 'L0_ffn_Wk': _L0_ffn_in['Wk'], 'L0_ffn_Wv': _L0_ffn_in['Wv'], 'L0_ffn_Wo': _L0_ffn_in['Wo'], 'L0_ffn_Wr': _L0_ffn_in['Wr'], 'L0_ffn_expert_bias': _L0_ffn_in['expert_bias'], 'L0_ffn_Wg': _L0_ffn_in['Wg'], 'L0_ffn_Wu': _L0_ffn_in['Wu'], 'L0_ffn_Wd': _L0_ffn_in['Wd'], 'L0_ffn_Wsg': _L0_ffn_in['Wsg'], 'L0_ffn_Wsu': _L0_ffn_in['Wsu'], 'L0_ffn_Wsd': _L0_ffn_in['Wsd']}
    _x0 = _d['L0_attn_x']
    _d['L0_attn_x'] = jax.random.normal(jax.random.fold_in(jax.random.key(seed), 1), (4, 256, 256), dtype=_x0.dtype)
    del _x0
    return _d

def reference(L0_attn_x, L0_attn_Wq, L0_attn_Wk, L0_attn_Wv, L0_attn_Wo, L0_ffn_ln1_w, L0_ffn_ln2_w, L0_ffn_Wq, L0_ffn_Wk, L0_ffn_Wv, L0_ffn_Wo, L0_ffn_Wr, L0_ffn_expert_bias, L0_ffn_Wg, L0_ffn_Wu, L0_ffn_Wd, L0_ffn_Wsg, L0_ffn_Wsu, L0_ffn_Wsd):

    def _L0_attn_ref(x, Wq, Wk, Wv, Wo):
        import jax, jax.numpy as jnp
        import numpy as np
        D_MODEL = 256
        N_HEADS = 16
        D_HEAD = D_MODEL // N_HEADS
        B, T, D = x.shape
        H, Dh = (N_HEADS, D_HEAD)
        q = (x @ Wq.T).reshape(B, T, H, Dh).transpose(0, 2, 1, 3)
        k = (x @ Wk.T).reshape(B, T, H, Dh).transpose(0, 2, 1, 3)
        v = (x @ Wv.T).reshape(B, T, H, Dh).transpose(0, 2, 1, 3)
        scale = Dh ** (-0.5)
        scores = jnp.einsum('bhqd,bhkd->bhqk', q, k) * scale
        causal = jnp.tril(jnp.ones((T, T), dtype=bool))
        scores = jnp.where(causal, scores, -jnp.inf)
        attn = jax.nn.softmax(scores, axis=-1)
        out = jnp.einsum('bhqk,bhkd->bhqd', attn, v)
        out = out.transpose(0, 2, 1, 3).reshape(B, T, D)
        return out @ Wo.T

    def _L0_ffn_ref(hidden_states, ln1_w, ln2_w, Wq, Wk, Wv, Wo, Wr, expert_bias, Wg, Wu, Wd, Wsg, Wsu, Wsd):
        import jax, jax.numpy as jnp
        import numpy as np
        H = 256
        NH = 32
        KVH = 4
        HD = 128
        E = 32
        TOPK = 8
        I = 128
        EPS = 1e-05
        THETA = 10000.0

        def _rmsnorm(x, w, eps=EPS):
            xf = x.astype(jnp.float32)
            var = jnp.mean(xf * xf, axis=-1, keepdims=True)
            return (w * (xf * jax.lax.rsqrt(var + eps))).astype(x.dtype)

        def _rope(x, pos):
            d = x.shape[-1]
            inv_freq = 1.0 / THETA ** (jnp.arange(0, d, 2, dtype=jnp.float32) / d)
            ang = pos.astype(jnp.float32)[:, None] * inv_freq[None, :]
            cos = jnp.cos(ang)[None, :, None, :]
            sin = jnp.sin(ang)[None, :, None, :]
            x1, x2 = jnp.split(x, 2, axis=-1)
            return jnp.concatenate([x1 * cos - x2 * sin, x1 * sin + x2 * cos], axis=-1)
        B, S, _ = hidden_states.shape
        resid = hidden_states
        h = _rmsnorm(hidden_states, ln1_w)
        pos = jnp.arange(S)
        q = (h @ Wq).reshape(B, S, NH, HD)
        k = (h @ Wk).reshape(B, S, KVH, HD)
        v = (h @ Wv).reshape(B, S, KVH, HD)
        q = _rope(q, pos)
        k = _rope(k, pos)
        rep = NH // KVH
        k = jnp.repeat(k, rep, axis=2)
        v = jnp.repeat(v, rep, axis=2)
        scores = jnp.einsum('bqhd,bkhd->bhqk', q, k) / jnp.sqrt(jnp.float32(HD))
        causal = jnp.tril(jnp.ones((S, S), dtype=bool))
        scores = jnp.where(causal[None, None], scores, jnp.float32(-1000000000.0))
        attn = jax.nn.softmax(scores, axis=-1)
        o = jnp.einsum('bhqk,bkhd->bqhd', attn, v).reshape(B, S, NH * HD) @ Wo
        x = resid + o
        resid = x
        h = _rmsnorm(x, ln2_w)
        t = h.reshape(-1, H)
        T = t.shape[0]
        router_scores = jax.nn.sigmoid(t @ Wr)
        _, idx = jax.lax.top_k(router_scores + expert_bias[None, :], TOPK)
        w = jnp.take_along_axis(router_scores, idx, axis=1)
        w = w / jnp.sum(w, axis=-1, keepdims=True)
        wfull = jnp.zeros((T, E), jnp.float32).at[jnp.arange(T)[:, None], idx].set(w)
        g = jnp.einsum('th,ehi->tei', t, Wg)
        u = jnp.einsum('th,ehi->tei', t, Wu)
        act = jax.nn.silu(g) * u
        moe = jnp.einsum('tei,te,eih->th', act, wfull, Wd)
        shared = jax.nn.silu(t @ Wsg) * (t @ Wsu) @ Wsd
        return resid + (moe + shared).reshape(B, S, H)
    x = L0_attn_x
    x = x + _layernorm(_L0_attn_ref(_layernorm(x, axis=-1), L0_attn_Wq, L0_attn_Wk, L0_attn_Wv, L0_attn_Wo), axis=-1)
    x = x + _layernorm(_L0_ffn_ref(_layernorm(x, axis=-1), L0_ffn_ln1_w, L0_ffn_ln2_w, L0_ffn_Wq, L0_ffn_Wk, L0_ffn_Wv, L0_ffn_Wo, L0_ffn_Wr, L0_ffn_expert_bias, L0_ffn_Wg, L0_ffn_Wu, L0_ffn_Wd, L0_ffn_Wsg, L0_ffn_Wsu, L0_ffn_Wsd), axis=-1)
    return x

_drawn_inputs = setup_inputs


def setup_inputs(seed=0):
    import zlib

    import numpy as np

    out = dict(_drawn_inputs(seed))
    spreads = {'L0_ffn_ln1_w': (1.0, 0.6), 'L0_ffn_ln2_w': (1.0, 0.6)}
    factors = {'L0_ffn_Wq': 8.0,
     'L0_ffn_Wk': 8.0,
     'L0_ffn_Wr': 8.0,
     'L0_ffn_expert_bias': 8.0,
     'L0_ffn_Wg': 8.0,
     'L0_ffn_Wu': 8.0,
     'L0_ffn_Wd': 8.0,
     'L0_ffn_Wsg': 8.0,
     'L0_ffn_Wsu': 8.0,
     'L0_ffn_Wsd': 8.0}
    for name, (base, spread) in spreads.items():
        noise = np.random.default_rng([zlib.crc32(name.encode()), seed]).standard_normal(out[name].shape)
        drawn = base * np.exp(spread * noise) if base else spread * noise
        out[name] = jnp.asarray(drawn.astype(out[name].dtype))
    for name, factor in factors.items():
        out[name] = (out[name] * factor).astype(out[name].dtype)
    return out
```

```python
from contextlib import ExitStack

import numpy as np
import concourse.bass as bass
from concourse import mybir

F32 = mybir.dt.float32
F32R = mybir.dt.float32r
BF16 = mybir.dt.bfloat16
ALU = mybir.AluOpType
ACT = mybir.ActivationFunctionType
AX = mybir.AxisListType.X

PART = 128
NB, SEQ, D = 4, 256, 256
NC = D // PART
NTT = SEQ // PART
NT = NB * NTT
SLOT = 2 * NC * SEQ
EPS = 1e-5
NEG = -1e30
HPI, PAIRS = 8, 4
PCOLS = PART + SEQ

A_HEADS, A_DH = 16, 16
A_ITS = NB * A_HEADS // HPI
A_QKV = 3 * HPI * A_DH
STACK = 64
KV, DH = 4, 128
B_ITS = NB * KV
B_QKV = HPI * DH + 2 * DH
B_WQ = NC * B_QKV
B_WO = HPI * D
B_W = B_WQ + B_WO
WQUART = B_W // 4

NE, TOPK, FF = 32, 8, 128
EW = 2 * NC * FF + D


def wait(eng, sem, value):
    if isinstance(value, int) and value <= 0:
        return
    eng.wait_ge(sem, value)


def three(nc, out, w_hi, w_lo, m_hi, m_lo, start, stop, skip=False):
    nc.tensor.matmul(out, w_lo, m_hi, start=start, stop=False, skip_group_check=skip)
    nc.tensor.matmul(out, w_hi, m_lo, start=False, stop=False, skip_group_check=skip)
    return nc.tensor.matmul(out, w_hi, m_hi, start=False, stop=stop, skip_group_check=skip)


class Machine:

    def __init__(self, nc, ctx):
        self.nc = nc
        self.ctx = ctx
        self.tag = ""

    def sb(self, name, shape, dt=F32, ctx=None):
        return (ctx or self.ctx).enter_context(self.nc.sbuf_tensor(self.tag + name, shape, dt))

    def sem(self, name, ctx=None):
        return (ctx or self.ctx).enter_context(self.nc.semaphore(self.tag + name))




class Norm:

    def __init__(self, m, ctx, name, rms=False):
        self.m, self.rms = m, rms
        self.stats = m.sb(name + "_stats", [PART, NT, 6], ctx=ctx)
        self.mv = m.sb(name + "_mv", [PART, NT, 2], ctx=ctx)
        self.den = m.sb(name + "_den", [PART, NT], ctx=ctx)
        self.rstd = m.sb(name + "_rstd", [PART, NT], ctx=ctx)
        self.step = m.sem(name + "_step", ctx=ctx)
        self.var_ready = m.sem(name + "_var_ready", ctx=ctx)
        self.root_ready = m.sem(name + "_root_ready", ctx=ctx)

    def vector(self, dve, tile, arrived=None):
        nc = self.m.nc
        for t in range(NT):
            if arrived:
                arrived(t)
            nc.vector.bn_stats(self.stats[:, t, :], tile(t)).then_inc(self.step, 1)
        for t in range(NT):
            dve.wait_ge(self.step, t + 1)
            nc.vector.bn_aggr(self.mv[:, t, :], self.stats[:, t, :]).then_inc(self.step, 1)
        n = 2 * NT
        dve.wait_ge(self.step, n)
        var = self.mv[:, :, 1]
        if self.rms:
            nc.vector.tensor_tensor(self.den[:], self.mv[:, :, 0], self.mv[:, :, 0],
                                    ALU.mult).then_inc(self.step, 1)
            dve.wait_ge(self.step, n + 1)
            nc.vector.tensor_tensor(self.rstd[:], self.den[:], var, ALU.add).then_inc(self.step, 1)
            dve.wait_ge(self.step, n + 2)
            var = self.rstd[:]
            n += 2
        nc.vector.tensor_scalar(self.den[:], var, EPS, None, ALU.add).then_inc(self.var_ready, 1)
        dve.wait_ge(self.root_ready, 1)
        nc.vector.reciprocal(self.rstd[:], self.den[:]).then_inc(self.step, 1)
        dve.wait_ge(self.step, n + 1)

    def scalar(self, act):
        act.wait_ge(self.var_ready, 1)
        self.m.nc.scalar.activation(self.den[:], self.den[:], ACT.Sqrt).then_inc(self.root_ready, 1)

    def apply(self, out, src, t):
        r = self.rstd[:, t:t + 1]
        if self.rms:
            return self.m.nc.vector.tensor_scalar(out, src, r, None, ALU.mult)
        return self.m.nc.vector.tensor_scalar(out, src, self.mv[:, t, 0:1], r, ALU.subtract, ALU.mult)


class Turn:

    def __init__(self, m, ctx, name, src, dst, weight=None):
        self.m, self.src, self.dst, self.weight = m, src, dst, weight
        self.rows_ready = m.sem(name + "_rows_ready", ctx=ctx)
        self.turned = m.sem(name + "_turned", ctx=ctx)
        self.hi_done = m.sem(name + "_hi_done", ctx=ctx)
        self.lo_done = m.sem(name + "_lo_done", ctx=ctx)

    def bank(self, b):
        return self.m.s_ps[:, b % 2, :].rearrange("p (c t) -> p c t", c=NC)

    def slot(self, b, part, c):
        at = b * SLOT + part * NC * SEQ + c * SEQ
        return self.dst[:, at:at + SEQ]

    def tensor(self, pe):
        nc = self.m.nc
        for b in range(NB):
            wait(pe, self.rows_ready, NTT * (b + 1))
            wait(pe, self.lo_done, b - 1)
            for t in range(NTT):
                for c in range(NC):
                    last = nc.tensor.transpose(self.bank(b)[:, c, t * PART:(t + 1) * PART],
                                               self.src[:, NTT * b + t, c * PART:(c + 1) * PART],
                                               self.m.ident[:])
            last.then_inc(self.turned, 1)

    def scalar(self, act):
        nc = self.m.nc
        for b in range(NB):
            act.wait_ge(self.turned, b + 1)
            for c in range(NC):
                scale = 1.0 if self.weight is None else self.weight[:, c:c + 1]
                last = nc.scalar.activation(self.slot(b, 0, c), self.bank(b)[:, c, :], ACT.Copy,
                                            scale=scale)
            last.then_inc(self.hi_done, 1)

    def vector(self, dve, b):
        nc = self.m.nc
        dve.wait_ge(self.hi_done, b + 1)
        for c in range(NC):
            scale = 1.0 if self.weight is None else self.weight[:, c:c + 1]
            last = nc.vector.scalar_tensor_tensor(
                out=self.slot(b, 1, c), in0=self.bank(b)[:, c, :], scalar=scale,
                in1=self.slot(b, 0, c).bitcast(F32), op0=ALU.mult, op1=ALU.subtract)
        last.then_inc(self.lo_done, 1)




def prepare(m, dram):
    nc = m.nc
    m.tag = "pre_"
    with ExitStack() as ctx:
        w_nat = m.sb("w_nat", [PART, 4, NC, D], ctx=ctx)
        norm = Norm(m, ctx, "ln_x")
        turn = Turn(m, ctx, "x", m.rows, m.act_t)
        sem = lambda name: m.sem(name, ctx=ctx)
        x_loaded = [sem(f"x_loaded{t}") for t in range(NT)]
        w_loaded, tables_loaded = sem("w_loaded"), sem("tables_loaded")
        zeroed, const_ready = sem("zeroed"), sem("const_ready")
        w_turned, w_hi, w_lo = sem("w_turned"), sem("w_hi"), sem("w_lo")
        block = ctx.enter_context(nc.Block())

        def w_bank(i):
            return (m.qt_ps, m.pj_ps)[i % 2][:].rearrange("p (c n) -> p c n", c=NC)

        def w_slot(i, part):
            if i == 3:
                at = part * NC * D
                return m.a_wo[:, at:at + NC * D].rearrange("p (c n) -> p c n", c=NC)
            at = part * 2 * NC * A_QKV
            half = m.a_wqkv[:, at:at + 2 * NC * A_QKV]
            return half.rearrange("p (g c n) -> p c g n", g=2, c=NC)[:, :, :, i * PART:(i + 1) * PART]

        @block.sync
        def _(sp):
            x = dram["x"].rearrange("b (t p) d -> p (b t) d", p=PART)
            for t in range(NT):
                sp.dma_start(m.x[:, t, :], x[:, t, :]).then_inc(x_loaded[t], 16)
            sp.dma_start(m.rope[:], dram["rope"]).then_inc(tables_loaded, 16)
            for i, name in enumerate(("ln1_w", "ln2_w")):
                sp.dma_start(m.lnw[:, i, :], dram[name].rearrange("(c p) -> p c", p=PART),
                             allow_slow_non_contiguous=True).then_inc(tables_loaded, 16)
            for dst, src in group_weights(m, dram, 0):
                sp.dma_start(dst, src).then_inc(tables_loaded, 16)
            sp.wait_ge(tables_loaded, 16 * (3 + W_DMAS))

        @block.gpsimd
        def _(pool):
            for buf in (m.ident, m.ident16, m.mask):
                nc.gpsimd.memset(buf[:], 0.0).then_inc(zeroed, 1)
            pool.wait_ge(zeroed, 3)
            for buf in (m.ident, m.ident16):
                nc.gpsimd.affine_select(out=buf[:], in_=buf[:], compare_op=ALU.not_equal, fill=1.0,
                                        base=0, pattern=[[-1, PART]],
                                        channel_multiplier=1).then_inc(const_ready, 1)
            nc.gpsimd.affine_select(out=m.mask[:], in_=m.mask[:], compare_op=ALU.is_ge, fill=NEG,
                                    base=0, pattern=[[-1, PART]],
                                    channel_multiplier=1).then_inc(const_ready, 1)
            nc.gpsimd.memset(m.b_w[:, 2 * B_W:4 * B_W].bitcast(F32), 0.0)

        @block.tensor
        def _(pe):
            pe.wait_ge(const_ready, 3)
            for i in range(4):
                pe.wait_ge(w_loaded, 64)
                wait(pe, w_lo, i - 1)
                for r in range(NC):
                    for c in range(NC):
                        last = nc.tensor.transpose(w_bank(i)[:, c, r * PART:(r + 1) * PART],
                                                   w_nat[:, i, r, c * PART:(c + 1) * PART], m.ident[:])
                last.then_inc(w_turned, 1)
            turn.tensor(pe)

        def w_views(i, part):
            src = w_bank(i)
            if i < 3:
                src = src.rearrange("p c (g n) -> p c g n", g=2)
            return w_slot(i, part), src

        w_scale = [float(A_DH) ** -0.5, 1.0, 1.0, 1.0]

        @block.scalar
        def _(act):
            for i, name in enumerate(("a_wq", "a_wk", "a_wv", "a_wo")):
                act.dma_start(w_nat[:, i, :, :], dram[name].rearrange("(r p) n -> p r n", p=PART),
                              ).then_inc(w_loaded, 16)
            norm.scalar(act)
            for i in range(4):
                act.wait_ge(w_turned, i + 1)
                dst, src = w_views(i, 0)
                nc.scalar.activation(dst, src, ACT.Copy, scale=w_scale[i]).then_inc(w_hi, 1)
            turn.scalar(act)

        @block.vector
        def _(dve):
            nc.vector.memset(m.acc[:], 0.0)
            norm.vector(dve, lambda t: m.x[:, t, :], lambda t: dve.wait_ge(x_loaded[t], 16))
            for t in range(NT):
                norm.apply(m.rows[:, t, :], m.x[:, t, :], t).then_inc(turn.rows_ready, 1)
            for i in range(4):
                dve.wait_ge(w_hi, i + 1)
                dst, src = w_views(i, 1)
                hi, _ = w_views(i, 0)
                for c in range(NC):
                    last = nc.vector.scalar_tensor_tensor(
                        out=dst[:, c], in0=src[:, c], scalar=w_scale[i], in1=hi[:, c].bitcast(F32),
                        op0=ALU.mult, op1=ALU.subtract)
                last.then_inc(w_lo, 1)
            for b in range(NB):
                turn.vector(dve, b)




class Attention:

    DRAIN = 5

    ITS = UNITS = 0
    LATE_NEXT = False
    QUERIES_LATE = None
    POOL_NORMALISES = False

    def __init__(self, m, ctx, tag):
        self.m, self.ctx = m, ctx
        m.tag = tag
        sb, sem = self.sb, self.sem
        self.src_t = sb("src_t", [PART, SLOT], F32R)
        self.qt = sb("qt", [PART, 2, 2, 2 * SEQ], F32R)
        self.prob = sb("prob", [PART, PAIRS, 2, PCOLS])
        self.prob_t = sb("prob_t", [PART, 2, 2, 2 * PCOLS], F32R)
        self.negmax = sb("negmax", [PART, 2, 2, NTT])
        self.sums = sb("sums", [PART, PAIRS, 2 * NTT])
        self.rsum = sb("rsum", [PART, PAIRS, 2 * NTT])
        self.src_loaded = sem("src_loaded")
        self.unit_full = sem("unit_full")
        self.unit_free = sem("unit_free")
        self.qt_full = sem("qt_full")
        self.qt_hi = sem("qt_hi")
        self.qt_ready = sem("qt_ready")
        self.s_full = sem("s_full")
        self.max_ready = sem("max_ready")
        self.exp_done = sem("exp_done")
        self.rsum_ready = sem("rsum_ready")
        self.prob_ready = sem("prob_ready")
        self.pt_full = sem("pt_full")
        self.pt_hi = sem("pt_hi")
        self.pt_ready = sem("pt_ready")
        self.pv_done = sem("pv_done")
        self.o_hi = sem("o_hi")
        self.o_ready = sem("o_ready")
        self.w_done = sem("w_done")
        self.y_added = sem("y_added")
        self.v_raw = sem("v_raw")
        self.v_hi = sem("v_hi")
        self.v_ready = sem("v_ready")
        self.kt_ready = sem("kt_ready")

    def sb(self, name, shape, dt=F32):
        return self.m.sb(name, shape, dt, ctx=self.ctx)

    def sem(self, name):
        return self.m.sem(name, ctx=self.ctx)


    COPIED = 3

    def src(self, it, part, c, t):
        at = part * NC * SEQ + c * SEQ + t * PART
        if isinstance(it, int) and it < self.COPIED:
            at += self.batch(it) * SLOT
            return self.m.act_t[:, at:at + PART]
        return self.src_t[:, at:at + PART]

    def wait_src(self, pe, it):
        if not (isinstance(it, int) and it < self.COPIED):
            pe.wait_ge(self.src_loaded, 16 * (it - self.COPIED + 1))

    def pe_scores(self, pe, it, p, P):
        nc, m = self.m.nc, self.m
        wait(pe, self.qt_ready, P + 1)
        self.pe_wait_keys(pe, it, p)
        for h in range(2):
            wait(pe, self.exp_done, 2 * P - 1 + h)
            for t in range(NTT):
                lo, width = t * PART, (t + 1) * PART
                out = m.s_ps[:, h, lo:lo + width]
                diagonal = m.s_ps[:, h, lo + width - PART:lo + width]
                self.pe_score(out, it, p, h, t, width)
                last = nc.tensor.matmul(diagonal, m.ident16[:], m.mask[:], start=False, stop=True)
            last.then_inc(self.s_full, 1)

    def pe_prob_t(self, pe, p, P):
        nc, m = self.m.nc, self.m
        wait(pe, self.prob_ready, P + 1)
        wait(pe, self.pt_ready, P)
        for h in range(2):
            for at, col in ((h * SEQ, 0), (h * SEQ + PART, PART), (2 * SEQ + h * PART, 2 * PART)):
                last = nc.tensor.transpose(m.pt_ps[:, at:at + PART],
                                           self.prob[:, p, h, col:col + PART], m.ident[:])
        last.then_inc(self.pt_full, 1)

    def stage(self, it, p, lag):
        P = PAIRS * it + p - lag
        if isinstance(P, int) and not 0 <= P < PAIRS * self.ITS:
            return None
        return it + (p - lag) // PAIRS, (p - lag) % PAIRS, P

    def early_unit(self, p, units):
        return self.schedule[p][0] if units and self.schedule[p] else None

    def late_unit(self, it, p, units):
        if p == 0:
            known = isinstance(it, int) and not 0 < it < self.ITS
            return None if known or len(self.schedule[-1]) < 2 else (it, self.schedule[-1][1])
        return (it + 1, self.schedule[p - 1][1]) if units and len(self.schedule[p - 1]) > 1 else None

    def slot_pe(self, pe, it, p, units=True):
        if now := self.stage(it, p, 0):
            self.pe_scores(pe, *now)
        if self.LATE_NEXT and (late := self.late_unit(it, p, units)):
            self.pe_unit(pe, *late)
        ahead = self.stage(it, p, -1)
        if ahead and p != self.QUERIES_LATE:
            self.pe_queries_t(pe, *ahead)
        if out := self.stage(it, p, 5):
            self.pe_project(pe, *out)
        if values := self.stage(it, p, 4):
            self.pe_values(pe, *values)
        u = self.early_unit(p, units)
        if u is not None and p != self.QUERIES_LATE:
            self.pe_unit(pe, it + 1, u)
        if prob := self.stage(it, p, 2):
            self.pe_prob_t(pe, *prob[1:])
        if ahead and p == self.QUERIES_LATE:
            self.pe_queries_t(pe, *ahead)
            if u is not None:
                self.pe_unit(pe, it + 1, u)
        if not self.LATE_NEXT and u is not None and len(self.schedule[p]) > 1:
            self.pe_unit(pe, it + 1, self.schedule[p][1])


    def act_exp(self, act, p, P):
        nc, m = self.m.nc, self.m
        wait(act, self.pt_full, P - PAIRS + 1)
        for h in range(2):
            wait(act, self.max_ready, 2 * P + 1 + h)
            for t in range(NTT):
                lo, width = t * PART, (t + 1) * PART
                k = 2 * h + t
                last = nc.scalar.activation(self.prob[:, p, h, lo:lo + width],
                                            m.s_ps[:, h, lo:lo + width], ACT.Exp,
                                            bias=self.negmax[:, p % 2, t, h:h + 1],
                                            accum_out=self.sums[:, p, k:k + 1])
            last.then_inc(self.exp_done, 1)

    def act_prob_t(self, act, p, P):
        wait(act, self.pt_full, P + 1)
        wait(act, self.pv_done, P - 1)
        self.m.nc.scalar.activation(self.prob_t[:, p % 2, 0, :], self.m.pt_ps[:, 0:2 * PCOLS],
                                    ACT.Copy).then_inc(self.pt_hi, 1)

    def slot_act(self, act, it, p, units=True):
        if prob := self.stage(it, p, 3):
            self.act_prob_t(act, *prob[1:])
        if late := self.late_unit(it, p, units):
            self.act_unit(act, *late)
        ahead = self.stage(it, p, -1)
        if ahead and p != self.QUERIES_LATE:
            self.act_queries(act, *ahead)
        if now := self.stage(it, p, 0):
            self.act_exp(act, *now[1:])
        if ahead and p == self.QUERIES_LATE:
            self.act_queries(act, *ahead)
        if out := self.stage(it, p, 4):
            self.act_outputs(act, *out)
        u = self.early_unit(p, units)
        if u is not None:
            self.act_unit(act, it + 1, u)
        if now and p == PAIRS - 1:
            self.act_values(act, it)
        if now and p == PAIRS - 2:
            self.act_weights(act, it)


    def dve_max(self, dve, p, P):
        nc, m = self.m.nc, self.m
        wait(dve, self.exp_done, 2 * P - 2)
        for h in range(2):
            wait(dve, self.s_full, 2 * P + 1 + h)
            for t in range(NTT):
                lo, width = t * PART, (t + 1) * PART
                last = nc.vector.tensor_reduce(self.negmax[:, p % 2, t, h:h + 1],
                                               m.s_ps[:, h, lo:lo + width], AX, ALU.max, negate=True)
            last.then_inc(self.max_ready, 1)

    def dve_normalise(self, dve, p, P):
        nc = self.m.nc
        wait(dve, self.exp_done, 2 * P + 2)
        nc.vector.reciprocal(self.rsum[:, p, :], self.sums[:, p, :]).then_inc(self.rsum_ready, 1)
        if self.POOL_NORMALISES:
            return
        wait(dve, self.rsum_ready, P + 1)
        for h in range(2):
            for t in range(NTT):
                lo, width = t * PART, (t + 1) * PART
                k = 2 * h + t
                row = self.prob[:, p, h, lo:lo + width]
                last = nc.vector.tensor_scalar(row, row, self.rsum[:, p, k:k + 1], None, ALU.mult)
        last.then_inc(self.prob_ready, 1)

    def pool_normalise(self, pool, p, P):
        wait(pool, self.rsum_ready, P + 1)
        rsum = self.rsum[:, p, :].rearrange("p (h t) -> p h t", h=2)
        for t in range(NTT):
            lo, width = t * PART, (t + 1) * PART
            rows = self.prob[:, p, :, lo:lo + width]
            last = self.m.nc.gpsimd.tensor_tensor(
                rows, rows, rsum[:, :, t:t + 1].to_broadcast([PART, 2, width]), ALU.mult)
        last.then_inc(self.prob_ready, 1)

    def dve_prob_t(self, dve, p, P):
        wait(dve, self.pt_hi, P + 1)
        self.m.nc.vector.tensor_tensor(self.prob_t[:, p % 2, 1, :], self.m.pt_ps[:, 0:2 * PCOLS],
                                       self.prob_t[:, p % 2, 0, :].bitcast(F32),
                                       ALU.subtract).then_inc(self.pt_ready, 1)

    def dve_add(self, dve, it):
        into = self.m.acc[:, bass.ds(self.batch(it) * (NTT * D), NTT * D)]
        wait(dve, self.w_done, self.projected(it))
        wait(dve, self.y_added, it)
        self.m.nc.vector.tensor_tensor(into, self.m.y_ps[:], into, ALU.add).then_inc(self.y_added, 1)

    def slot_dve(self, dve, it, p, units=True):
        if now := self.stage(it, p, 0):
            self.dve_max(dve, *now[1:])
        if ahead := self.stage(it, p, -1):
            self.dve_queries(dve, *ahead)
        late = self.late_unit(it, p, units)
        if late and self.LATE_NEXT:
            self.dve_unit(dve, *late)
        if prob := self.stage(it, p, 3):
            self.dve_prob_t(dve, *prob[1:])
        if late and not self.LATE_NEXT:
            self.dve_unit(dve, *late)
        if before := self.stage(it, p, 1):
            self.dve_normalise(dve, *before[1:])
        if out := self.stage(it, p, 4):
            self.dve_outputs(dve, *out)
        u = self.early_unit(p, units)
        if u is not None:
            self.dve_unit(dve, it + 1, u)
        if now and p == PAIRS - 1:
            self.dve_values(dve, it)
        if p == 0 and not (isinstance(it, int) and it < 2):
            self.dve_add(dve, it - 2)


    def run(self, eng, slot, middles):
        for it in range(2):
            for p in range(PAIRS):
                slot(eng, it, p)
        for first, last in middles:
            self.splitting = last <= self.ITS - NB
            with eng.Fori(first, last) as it:
                for p in range(PAIRS):
                    slot(eng, it, p)
        for p in range(PAIRS):
            slot(eng, self.ITS - 1, p, units=False)
        for P in range(PAIRS * self.ITS, PAIRS * self.ITS + self.DRAIN):
            slot(eng, P // PAIRS, P % PAIRS, units=False)


class AttentionA(Attention):

    ITS, UNITS = A_ITS, 4
    LATE_NEXT = True
    QUERIES_LATE = PAIRS - 1
    POOL_NORMALISES = True
    schedule = ((), (), (0, 1), (2, 3))

    def __init__(self, m, ctx):
        super().__init__(m, ctx, "a_")
        sb, sem = self.sb, self.sem
        rest = m.b_w[:, 2 * B_W:4 * B_W]

        def place(n, pattern, **sizes):
            nonlocal rest
            rest, taken = rest[:, n:], rest[:, 0:n]
            return taken.rearrange(pattern, **sizes)

        self.v = place(2 * NTT * HPI * PART, "p (a t h n) -> p a t h n", a=2, t=NTT, h=HPI)
        self.q_stack = place(NTT * HPI * PART, "p (t n) -> p t n", t=NTT)
        self.k_stack = place(NTT * HPI * STACK, "p (t n) -> p t n", t=NTT)
        self.kt = place(2 * PAIRS * SEQ, "p n -> p n")
        self.v_row = sb("v_row", [PART, 2 * NTT * HPI * A_DH])
        self.ot = sb("ot", [PART, 2, SEQ], F32R)
        self.w_raw_hi = sem("w_raw_hi")
        self.stack_hi = sem("stack_hi")
        self.stack_ready = sem("stack_ready")

    def slot_pool(self, pool, it, p, units=True):
        if before := self.stage(it, p, 1):
            self.pool_normalise(pool, *before[1:])

    @staticmethod
    def batch(it):
        return it // 2

    @staticmethod
    def projected(it):
        return it + 1

    def weights(self, part, c, group):
        at = part * 2 * NC * A_QKV + c * A_QKV
        return self.m.a_wqkv[:, bass.ds(group * (NC * A_QKV) + at, A_QKV)]

    def pe_unit(self, pe, it, u):
        nc, m = self.m.nc, self.m
        n = self.UNITS * it + u
        if u < NTT:
            self.wait_src(pe, it)
            wait(pe, self.unit_free, n)
            for c in range(NC):
                last = three(nc, m.pj_ps[:, 0:A_QKV], self.src(it, 0, c, u), self.src(it, 1, c, u),
                             self.weights(0, c, it % 2), self.weights(1, c, it % 2),
                             c == 0, c == NC - 1)
        else:
            wait(pe, self.stack_ready, NTT * (it + 1))
            wait(pe, self.unit_free, n)
            for q in range(2):
                pair = 2 * (u - NTT) + q
                for t in range(NTT):
                    at = q * SEQ + t * PART
                    last = nc.tensor.transpose(
                        m.pj_ps[:, at:at + PART],
                        self.k_stack[:, t, pair * PART:(pair + 1) * PART].bitcast(F32), m.ident[:])
        last.then_inc(self.unit_full, 1)

    def pe_queries_t(self, pe, it, p, P):
        nc, m = self.m.nc, self.m
        wait(pe, self.stack_ready, NTT * (it + 1))
        wait(pe, self.qt_ready, P)
        for h in range(2):
            at = (2 * p + h) * PART - (STACK if h else 0)
            for t in range(NTT):
                last = nc.tensor.transpose(m.qt_ps[:, h * SEQ + t * PART:h * SEQ + (t + 1) * PART],
                                           self.q_stack[:, t, at:at + PART].bitcast(F32), m.ident[:])
        last.then_inc(self.qt_full, 1)

    def pe_wait_keys(self, pe, it, p):
        if p % 2 == 0:
            wait(pe, self.kt_ready, 2 * it + p // 2 + 1)

    def keys(self, it, p, n):
        return self.kt[:, bass.ds((it % 2) * (PAIRS * SEQ) + p * SEQ, n)]

    def pe_score(self, out, it, p, h, t, width):
        at = h * SEQ + t * PART
        self.m.nc.tensor.matmul(out, self.qt[:, p % 2, 0, at:at + PART], self.keys(it, p, width),
                                start=True, stop=False)

    def pe_values(self, pe, it, p, P):
        nc, m = self.m.nc, self.m
        wait(pe, self.pt_ready, P + 1)
        if p == 0:
            wait(pe, self.v_ready, it + 1)
            wait(pe, self.o_ready, it)
        par = p % 2
        for h in range(2):
            head = 2 * p + h
            for k in range(NTT):
                width = SEQ - k * PART
                at = h * SEQ if k == 0 else 2 * SEQ + h * PART
                last = three(nc, m.o_ps[:, k * PART:SEQ],
                             self.v[:, 0, k, head, :], self.v[:, 1, k, head, :],
                             self.prob_t[:, par, 0, at:at + width], self.prob_t[:, par, 1, at:at + width],
                             head == 0 and k == 0, head == HPI - 1 and k == NTT - 1)
        last.then_inc(self.pv_done, 1)

    def pe_project(self, pe, it, p, P):
        if p != PAIRS - 1:
            return
        nc, m = self.m.nc, self.m
        wait(pe, self.o_ready, it + 1)
        wait(pe, self.y_added, it)
        at = (it % 2) * D
        for t in range(NTT):
            last = three(nc, m.y_ps[:, t * D:(t + 1) * D],
                         self.ot[:, 0, t * PART:(t + 1) * PART], self.ot[:, 1, t * PART:(t + 1) * PART],
                         m.a_wo[:, bass.ds(at, D)], m.a_wo[:, bass.ds(at + NC * D, D)], True, True)
        last.then_inc(self.w_done, 1)

    def act_outputs(self, act, it, p, P):
        if p != PAIRS - 1:
            return
        wait(act, self.pv_done, P + 1)
        wait(act, self.w_done, it)
        self.m.nc.scalar.activation(self.ot[:, 0, :], self.m.o_ps[:, 0:SEQ],
                                    ACT.Copy).then_inc(self.o_hi, 1)

    def dve_outputs(self, dve, it, p, P):
        if p != PAIRS - 1:
            return
        wait(dve, self.o_hi, it + 1)
        self.m.nc.vector.tensor_tensor(self.ot[:, 1, :], self.m.o_ps[:, 0:SEQ],
                                       self.ot[:, 0, :].bitcast(F32),
                                       ALU.subtract).then_inc(self.o_ready, 1)

    def values(self, it, t):
        n = HPI * A_DH
        return self.v_row[:, bass.ds((it % 2) * (NTT * n) + t * n, n)]

    def v_view(self, part, t):
        base = self.v[:, part, t, 0, 0:A_DH]
        return bass.AP(tensor=base.tensor, offset=base.offset,
                       ap=[list(base.ap[0]), [PART + A_DH, HPI], [1, A_DH]])

    def act_values(self, act, it):
        nc = self.m.nc
        wait(act, self.v_raw, NTT * (it + 1))
        wait(act, self.pv_done, PAIRS * it)
        for t in range(NTT):
            row = self.values(it, t).rearrange("p (h d) -> p h d", h=HPI)
            last = nc.scalar.activation(self.v_view(0, t), row, ACT.Copy)
        last.then_inc(self.v_hi, 1)

    def dve_values(self, dve, it):
        nc = self.m.nc
        wait(dve, self.v_hi, it + 1)
        for t in range(NTT):
            row = self.values(it, t).rearrange("p (h d) -> p h d", h=HPI)
            last = nc.vector.tensor_tensor(self.v_view(1, t), row, self.v_view(0, t).bitcast(F32),
                                           ALU.subtract)
        last.then_inc(self.v_ready, 1)

    def act_queries(self, act, it, p, P):
        wait(act, self.qt_full, P + 1)
        wait(act, self.s_full, 2 * P - 2)
        self.m.nc.scalar.activation(self.qt[:, p % 2, 0, :], self.m.qt_ps[:],
                                    ACT.Copy).then_inc(self.qt_ready, 1)

    def dve_queries(self, dve, it, p, P):
        pass

    def act_weights(self, act, it):
        pass

    def stack_views(self, u):
        heads = lambda x, n: x.rearrange("p (h n) -> p h n", h=n)
        pj = self.m.pj_ps
        q, k, v = (pj[:, i * PART:(i + 1) * PART] for i in range(3))
        qs = heads(self.q_stack[:, u, :], HPI)[:, :, 0:STACK].rearrange("p h (s d) -> p h s d", d=A_DH)
        ks = heads(self.k_stack[:, u, :], HPI).rearrange("p h (s d) -> p h s d", d=A_DH)
        return heads(q, HPI), heads(k, HPI), v, qs, ks

    def act_unit(self, act, it, u):
        nc, m = self.m.nc, self.m
        n = self.UNITS * it + u
        wait(act, self.unit_full, n + 1)
        if u < NTT:
            wait(act, self.qt_full, PAIRS * it)
            wait(act, self.unit_free, self.UNITS * it)
            q, k, _, qs, ks = self.stack_views(u)
            for src, dst in ((q, qs[:, :, 0:2, :]), (k, ks[:, :, 0:3:2, :])):
                twice = src.unsqueeze(2).to_broadcast([PART, HPI, 2, A_DH])
                last = nc.scalar.activation(dst, twice, ACT.Copy)
            last.then_inc(self.stack_hi, 1)
        else:
            wait(act, self.s_full, 2 * PAIRS * (it - 1))
            nc.scalar.activation(self.keys(it, 2 * (u - NTT), 2 * SEQ), m.pj_ps[:],
                                 ACT.Copy).then_inc(self.kt_ready, 1)
            act.wait_ge(self.kt_ready, 2 * it + u - NTT + 1)
            act.sem_inc(self.unit_free, 1)

    def dve_unit(self, dve, it, u):
        if u >= NTT:
            return
        nc = self.m.nc
        wait(dve, self.stack_hi, NTT * it + u + 1)
        q, k, v, qs, ks = self.stack_views(u)
        nc.vector.tensor_tensor(qs[:, :, 2, :], q, qs[:, :, 0, :].bitcast(F32), ALU.subtract)
        nc.vector.tensor_tensor(ks[:, :, 1, :], k, ks[:, :, 0, :].bitcast(F32),
                                ALU.subtract).then_inc(self.stack_ready, 1)
        wait(dve, self.v_ready, it - 1)
        nc.vector.tensor_copy(self.values(it, u), v).then_inc(self.v_raw, 1)
        dve.wait_ge(self.v_raw, NTT * it + u + 1)
        dve.sem_inc(self.unit_free, 1)

    def build(self, dram):
        nc, m = self.m.nc, self.m
        middles = ((2, self.ITS - 1),)
        block = self.ctx.enter_context(nc.Block())

        @block.sync
        def _(sp):
            def load(it, b):
                if not isinstance(it, int):
                    sp.wait_ge(self.unit_full, self.UNITS * (it - 1) + NTT)
                sp.dma_start(self.src_t[:].bitcast(F32), self.m.act_t[:, bass.ds(b * SLOT, SLOT)].bitcast(F32),
                             ).then_inc(self.src_loaded, 16)
            load(self.COPIED, 1)
            with sp.Fori(2, NB) as b:
                load(2 * b, b)
                load(2 * b + 1, b)
            sp.wait_ge(self.src_loaded, 16 * (self.ITS - self.COPIED))

        @block.gpsimd
        def _(pool):
            for q in range(4):
                pool.wait_ge(self.w_raw_hi, q + 1)
                at = slice(q * WQUART, (q + 1) * WQUART)
                nc.gpsimd.tensor_tensor(m.b_w[:, B_W:2 * B_W][:, at], m.b_w_raw[:, at],
                                        m.b_w[:, at].bitcast(F32), ALU.subtract)
            self.run(pool, self.slot_pool, middles)

        @block.tensor
        def _(pe):
            for u in range(NTT):
                self.pe_unit(pe, 0, u)
            self.pe_queries_t(pe, 0, 0, 0)
            for u in range(NTT, self.UNITS):
                self.pe_unit(pe, 0, u)
            self.run(pe, self.slot_pe, middles)

        @block.scalar
        def _(act):
            def split_weights(q):
                at = slice(q * WQUART, (q + 1) * WQUART)
                nc.scalar.activation(m.b_w[:, at], m.b_w_raw[:, at], ACT.Copy).then_inc(self.w_raw_hi, 1)
            for u in range(NTT):
                split_weights(u)
                self.act_unit(act, 0, u)
            self.act_queries(act, 0, 0, 0)
            for u in range(NTT, self.UNITS):
                split_weights(u)
                self.act_unit(act, 0, u)
            self.run(act, self.slot_act, middles)

        @block.vector
        def _(dve):
            for u in range(self.UNITS):
                self.dve_unit(dve, 0, u)
            self.run(dve, self.slot_dve, middles)


W_DMAS = 4


def group_weights(m, dram, g):
    q = HPI * DH
    raw_in = m.b_w_raw[:, 0:B_WQ].rearrange("p (c n) -> p c n", c=NC)
    raw_out = m.b_w_raw[:, B_WQ:B_W].rearrange("p (h n) -> p h n", h=HPI)
    wq, wk, wv = (dram[n].rearrange("(c p) n -> p c n", p=PART) for n in ("b_wq", "b_wk", "b_wv"))
    wo = dram["b_wo"].rearrange("(h p) n -> p h n", p=DH)
    return [(raw_in[:, :, 0:q], wq[:, :, bass.ds(g * q, q)]),
            (raw_in[:, :, q:q + DH], wk[:, :, bass.ds(g * DH, DH)]),
            (raw_in[:, :, q + DH:q + 2 * DH], wv[:, :, bass.ds(g * DH, DH)]),
            (raw_out, wo[:, bass.ds(g * HPI, HPI), :])]


class AttentionB(Attention):

    ITS, UNITS = B_ITS, 7
    KV0, KV1, Q00, Q01, KT, Q10, Q11 = range(7)
    schedule = ((KV0, KV1), (Q00, Q01), (KT,), (Q10, Q11))
    Q_OF = {Q00: (0, 0), Q01: (0, 1), Q10: (1, 0), Q11: (1, 1)}
    KV_OF = {KV0: 0, KV1: 1}
    ROT = {KV0: 0, KV1: 1, Q00: 2, Q01: 3, Q10: 4, Q11: 5}
    NROT = len(ROT)

    def __init__(self, m, ctx):
        super().__init__(m, ctx, "b_")
        sb, sem = self.sb, self.sem
        self.w, self.w_raw = m.b_w, m.b_w_raw
        self.raw = sb("raw", [PART, 2, 4 * DH])
        self.cos_part = sb("cos_part", [PART, 2, 4 * DH])
        self.sin_part = sb("sin_part", [PART, 2, 4 * DH])
        self.q_row = sb("q_row", [PART, 2, NTT, 4 * DH])
        self.k_row = sb("k_row", [PART, NTT, DH])
        self.v_row = sb("v_row", [PART, 2 * NTT * DH])
        self.kt = sb("kt", [PART, 2 * 2 * SEQ], F32R)
        self.v = sb("v", [PART, 2, NTT, DH], F32R)
        self.ot = sb("ot", [PART, 2, 2, 2 * SEQ], F32R)
        self.w_loaded = sem("w_loaded")
        self.w_hi = sem("w_hi")
        self.w_ready = sem("w_ready")
        self.raw_ready = sem("raw_ready")
        self.cos_ready = sem("cos_ready")
        self.sin_ready = sem("sin_ready")
        self.rotated = sem("rotated")
        self.kt_hi = sem("kt_hi")

    @staticmethod
    def batch(it):
        return it % NB

    @staticmethod
    def projected(it):
        return PAIRS * (it + 1)

    def w_at(self, it, part, offset, n):
        group = it // NB
        return self.w[:, bass.ds((group % 2) * (2 * B_W) + (part * B_W + offset), n)]

    def pe_unit(self, pe, it, u):
        nc, m = self.m.nc, self.m
        n = self.UNITS * it + u
        if u == self.KT:
            wait(pe, self.rotated, self.NROT * it + self.ROT[self.KV1] + 1)
            wait(pe, self.unit_free, n)
            for t in range(NTT):
                last = nc.tensor.transpose(m.pj_ps[:, t * PART:(t + 1) * PART], self.k_row[:, t, :],
                                           m.ident[:])
            last.then_inc(self.unit_full, 1)
            return
        self.wait_src(pe, it)
        wait(pe, self.w_ready, 4 * (it // NB) + 3)
        wait(pe, self.unit_free, n)
        if u in self.Q_OF:
            half, t = self.Q_OF[u]
            col, width = half * 4 * DH, 4 * DH
        else:
            t = self.KV_OF[u]
            col, width = HPI * DH, 2 * DH
        for c in range(NC):
            last = three(nc, m.pj_ps[:, 0:width], self.src(it, 0, c, t), self.src(it, 1, c, t),
                         self.w_at(it, 0, c * B_QKV + col, width),
                         self.w_at(it, 1, c * B_QKV + col, width), c == 0, c == NC - 1)
        last.then_inc(self.unit_full, 1)

    def pe_queries_t(self, pe, it, p, P):
        nc, m = self.m.nc, self.m
        half = p // 2
        unit = self.Q01 if half == 0 else self.Q11
        wait(pe, self.rotated, self.NROT * it + self.ROT[unit] + 1)
        wait(pe, self.qt_ready, P)
        for h in range(2):
            head = 2 * (p % 2) + h
            for t in range(NTT):
                at = h * SEQ + t * PART
                last = nc.tensor.transpose(m.qt_ps[:, at:at + PART],
                                           self.q_row[:, half, t, head * DH:(head + 1) * DH], m.ident[:])
        last.then_inc(self.qt_full, 1)

    def pe_wait_keys(self, pe, it, p):
        if p == 0:
            wait(pe, self.kt_ready, it + 1)

    def keys(self, it, part, n):
        return self.kt[:, bass.ds((it % 2) * (2 * SEQ) + part * SEQ, n)]

    def pe_score(self, out, it, p, h, t, width):
        at = h * SEQ + t * PART
        q = lambda part: self.qt[:, p % 2, part, at:at + PART]
        three(self.m.nc, out, q(0), q(1), self.keys(it, 0, width), self.keys(it, 1, width), True, False)

    def pe_values(self, pe, it, p, P):
        nc, m = self.m.nc, self.m
        wait(pe, self.pt_ready, P + 1)
        if p == 0:
            wait(pe, self.v_ready, it + 1)
        wait(pe, self.o_ready, P)
        pt = lambda part: self.prob_t[:, p % 2, part, :]
        three(nc, m.o_ps[:], self.v[:, 0, 0, :], self.v[:, 1, 0, :],
              pt(0)[:, 0:2 * SEQ], pt(1)[:, 0:2 * SEQ], True, False)
        later = m.o_ps[:].rearrange("p (h q) -> p h q", h=2)[:, :, PART:SEQ]
        tail = lambda part: pt(part)[:, 2 * SEQ:2 * PCOLS].rearrange("p (h q) -> p h q", h=2)
        last = three(nc, later, self.v[:, 0, 1, :], self.v[:, 1, 1, :], tail(0), tail(1), False, True)
        last.then_inc(self.pv_done, 1)

    def pe_project(self, pe, it, p, P):
        nc, m = self.m.nc, self.m
        wait(pe, self.o_ready, P + 1)
        if p == 0:
            wait(pe, self.y_added, it)
            wait(pe, self.w_ready, 4 * (it // NB) + 4)
        for h in range(2):
            for t in range(NTT):
                at = h * SEQ + t * PART
                o = lambda part: self.ot[:, p % 2, part, at:at + PART]
                row = B_WQ + (2 * p + h) * D
                last = three(nc, m.y_ps[:, t * D:(t + 1) * D], o(0), o(1), self.w_at(it, 0, row, D),
                             self.w_at(it, 1, row, D), p == 0 and h == 0 and t == 0,
                             p == PAIRS - 1 and h == 1 and t == NTT - 1, skip=True)
        last.then_inc(self.w_done, 1)

    def act_outputs(self, act, it, p, P):
        wait(act, self.pv_done, P + 1)
        wait(act, self.w_done, P - 1)
        self.m.nc.scalar.activation(self.ot[:, p % 2, 0, :], self.m.o_ps[:],
                                    ACT.Copy).then_inc(self.o_hi, 1)

    def dve_outputs(self, dve, it, p, P):
        wait(dve, self.o_hi, P + 1)
        self.m.nc.vector.tensor_tensor(self.ot[:, p % 2, 1, :], self.m.o_ps[:],
                                       self.ot[:, p % 2, 0, :].bitcast(F32),
                                       ALU.subtract).then_inc(self.o_ready, 1)

    def act_values(self, act, it):
        wait(act, self.v_raw, NTT * (it + 1))
        wait(act, self.pv_done, PAIRS * it)
        self.m.nc.scalar.activation(self.v[:, 0, :, :].rearrange("p t n -> p (t n)"),
                                    self.values(it, 0, NTT), ACT.Copy).then_inc(self.v_hi, 1)

    def values(self, it, t, n):
        return self.v_row[:, bass.ds((it % 2) * (NTT * DH) + t * DH, n * DH)]

    def dve_values(self, dve, it):
        wait(dve, self.v_hi, it + 1)
        self.m.nc.vector.tensor_tensor(self.v[:, 1, :, :].rearrange("p t n -> p (t n)"),
                                       self.values(it, 0, NTT),
                                       self.v[:, 0, :, :].rearrange("p t n -> p (t n)").bitcast(F32),
                                       ALU.subtract).then_inc(self.v_ready, 1)

    def act_queries(self, act, it, p, P):
        wait(act, self.qt_full, P + 1)
        wait(act, self.s_full, 2 * P - 2)
        self.m.nc.scalar.activation(self.qt[:, p % 2, 0, :], self.m.qt_ps[:],
                                    ACT.Copy).then_inc(self.qt_hi, 1)

    def dve_queries(self, dve, it, p, P):
        wait(dve, self.qt_hi, P + 1)
        self.m.nc.vector.tensor_tensor(self.qt[:, p % 2, 1, :], self.m.qt_ps[:],
                                       self.qt[:, p % 2, 0, :].bitcast(F32),
                                       ALU.subtract).then_inc(self.qt_ready, 1)

    def act_unit(self, act, it, u):
        nc, m = self.m.nc, self.m
        wait(act, self.unit_full, self.UNITS * it + u + 1)
        if u == self.KT:
            wait(act, self.s_full, 2 * PAIRS * (it - 1))
            nc.scalar.activation(self.keys(it, 0, SEQ), m.pj_ps[:, 0:SEQ],
                                 ACT.Copy).then_inc(self.kt_hi, 1)
            return
        r = self.NROT * it + self.ROT[u]
        wait(act, self.rotated, r - 1)
        n = 4 * DH if u in self.Q_OF else DH
        if u in self.KV_OF:
            wait(act, self.v_ready, it - 1)
            nc.scalar.activation(self.values(it, self.KV_OF[u], 1), m.pj_ps[:, DH:2 * DH],
                                 ACT.Copy).then_inc(self.v_raw, 1)
        nc.scalar.activation(self.raw[:, self.ROT[u] % 2, 0:n], m.pj_ps[:, 0:n],
                             ACT.Copy).then_inc(self.raw_ready, 1)
        act.wait_ge(self.raw_ready, r + 1)
        act.sem_inc(self.unit_free, 1)

    def dve_unit(self, dve, it, u):
        nc, m = self.m.nc, self.m
        if u == self.KT:
            wait(dve, self.kt_hi, it + 1)
            nc.vector.tensor_tensor(self.keys(it, 1, SEQ), m.pj_ps[:, 0:SEQ],
                                    self.keys(it, 0, SEQ).bitcast(F32),
                                    ALU.subtract).then_inc(self.kt_ready, 1)
            wait(dve, self.kt_ready, it + 1)
            dve.sem_inc(self.unit_free, 1)
            return
        r = self.NROT * it + self.ROT[u]
        wait(dve, self.raw_ready, r + 1)
        wait(dve, self.rotated, r - 1)
        out, x, factor = self.rotation(u, self.cos_part, 0)
        nc.vector.tensor_tensor(out, x, factor, ALU.mult).then_inc(self.cos_ready, 1)

    def rotation(self, u, product, kind):
        par = self.ROT[u] % 2
        if u in self.Q_OF:
            (_, t), heads, table = self.Q_OF[u], 4, 0
        else:
            t, heads, table = self.KV_OF[u], 1, 2
        halves = lambda x: x[:, par, 0:heads * DH].rearrange("p (h a d) -> p h a d", h=heads, a=2)
        factor = self.m.rope[:, table + kind, t, :].rearrange("p (a d) -> p a d", a=2)
        factor = factor.unsqueeze(1).to_broadcast([PART, heads, 2, DH // 2])
        x = halves(self.raw)
        return halves(product), x[:, :, ::-1, :] if kind else x, factor

    def pool_unit(self, pool, it, u):
        if u == self.KT:
            return
        nc = self.m.nc
        r = self.NROT * it + self.ROT[u]
        par = self.ROT[u] % 2
        wait(pool, self.raw_ready, r + 1)
        wait(pool, self.rotated, r - 1)
        out, x, factor = self.rotation(u, self.sin_part, 1)
        nc.gpsimd.tensor_tensor(out, x, factor, ALU.mult).then_inc(self.sin_ready, 1)
        wait(pool, self.cos_ready, r + 1)
        wait(pool, self.sin_ready, r + 1)
        if u in self.Q_OF:
            half, t = self.Q_OF[u]
            wait(pool, self.qt_full, PAIRS * (it - 1) + 2 * half + 2)
            out, n = self.q_row[:, half, t, :], 4 * DH
        else:
            t = self.KV_OF[u]
            wait(pool, self.unit_full, self.UNITS * (it - 1) + self.KT + 1)
            out, n = self.k_row[:, t, :], DH
        nc.gpsimd.tensor_tensor(out, self.cos_part[:, par, 0:n], self.sin_part[:, par, 0:n],
                                ALU.add).then_inc(self.rotated, 1)

    def quarter(self, it, part=None):
        q = (it % NB) * WQUART
        if part is None:
            return self.w_raw[:, bass.ds(q, WQUART)]
        group = it // NB + 1
        return self.w[:, bass.ds((group % 2) * (2 * B_W) + q + part * B_W, WQUART)]

    def act_weights(self, act, it):
        if not self.more_weights(it):
            return
        wait(act, self.w_loaded, 16 * W_DMAS * (it // NB + 1))
        wait(act, self.w_done, PAIRS * (it - 2))
        self.m.nc.scalar.activation(self.quarter(it, 0), self.quarter(it), ACT.Copy).then_inc(self.w_hi, 1)

    def slot_pool(self, pool, it, p, units=True):
        if not self.stage(it, p, 0):
            return
        if units:
            for u in self.schedule[p]:
                self.pool_unit(pool, it + 1, u)
        if p == PAIRS - 2 and self.more_weights(it):
            wait(pool, self.w_hi, it + 1)
            self.m.nc.gpsimd.tensor_tensor(self.quarter(it, 1), self.quarter(it),
                                           self.quarter(it, 0).bitcast(F32),
                                           ALU.subtract).then_inc(self.w_ready, 1)

    def more_weights(self, it):
        return it < B_ITS - NB if isinstance(it, int) else self.splitting

    def build(self, dram):
        nc, m = self.m.nc, self.m
        middles = ((2, self.ITS - NB), (self.ITS - NB, self.ITS - 1))
        block = self.ctx.enter_context(nc.Block())

        @block.sync
        def _(sp):
            def load_weights(g):
                wait(sp, self.w_ready, 4 * g)
                for dst, src in group_weights(m, dram, g):
                    sp.dma_start(dst, src).then_inc(self.w_loaded, 16)

            def load_batch(it, b):
                if not (isinstance(it, int) and it == self.COPIED):
                    sp.wait_ge(self.unit_full, self.UNITS * it)
                sp.dma_start(self.src_t[:].bitcast(F32), m.act_t[:, b * SLOT:(b + 1) * SLOT].bitcast(F32),
                             ).then_inc(self.src_loaded, 16)

            load_weights(1)
            load_batch(3, 3)
            with sp.Fori(1, KV - 1) as g:
                load_batch(NB * g, 0)
                load_batch(NB * g + 1, 1)
                load_weights(g + 1)
                load_batch(NB * g + 2, 2)
                load_batch(NB * g + 3, 3)
            for b in range(NB):
                load_batch(NB * (KV - 1) + b, b)
            sp.wait_ge(self.src_loaded, 16 * (self.ITS - self.COPIED))

        @block.gpsimd
        def _(pool):
            pool.sem_inc(self.w_ready, 4)
            for u in range(self.UNITS):
                self.pool_unit(pool, 0, u)
            self.run(pool, self.slot_pool, middles)

        @block.tensor
        def _(pe):
            for u in range(self.UNITS):
                self.pe_unit(pe, 0, u)
            self.pe_queries_t(pe, 0, 0, 0)
            self.run(pe, self.slot_pe, middles)

        @block.scalar
        def _(act):
            for u in range(self.UNITS):
                self.act_unit(act, 0, u)
            self.act_queries(act, 0, 0, 0)
            self.run(act, self.slot_act, middles)

        @block.vector
        def _(dve):
            for u in range(self.UNITS):
                self.dve_unit(dve, 0, u)
            self.dve_queries(dve, 0, 0, 0)
            self.run(dve, self.slot_dve, middles)




def join(m):
    nc = m.nc
    m.tag = "join_"
    with ExitStack() as ctx:
        norms = [Norm(m, ctx, "ln_a"), Norm(m, ctx, "ln_f"), Norm(m, ctx, "rms", rms=True)]
        turn = Turn(m, ctx, "h", m.rows, m.act_t, m.lnw[:, 0, :])
        acc = m.acc[:].rearrange("p (t d) -> p t d", t=NT)
        done = m.sem("done", ctx=ctx)
        block = ctx.enter_context(nc.Block())

        @block.vector
        def _(dve):
            norms[0].vector(dve, lambda t: acc[:, t, :])
            for t in range(NT):
                norms[0].apply(m.rows[:, t, :], acc[:, t, :], t).then_inc(done, 1)
            for t in range(NT):
                dve.wait_ge(done, t + 1)
                nc.vector.tensor_tensor(m.x[:, t, :], m.x[:, t, :], m.rows[:, t, :],
                                        ALU.add).then_inc(done, 1)
            norms[1].vector(dve, lambda t: m.x[:, t, :], lambda t: dve.wait_ge(done, NT + t + 1))
            for t in range(NT):
                norms[1].apply(acc[:, t, :], m.x[:, t, :], t).then_inc(done, 1)
            norms[2].vector(dve, lambda t: acc[:, t, :], lambda t: dve.wait_ge(done, 2 * NT + t + 1))
            for t in range(NT):
                norms[2].apply(m.rows[:, t, :], acc[:, t, :], t).then_inc(turn.rows_ready, 1)
            for b in range(NB):
                turn.vector(dve, b)

        @block.scalar
        def _(act):
            for norm in norms:
                norm.scalar(act)
            turn.scalar(act)

        @block.tensor
        def _(pe):
            turn.tensor(pe)


def norm_two(m):
    nc = m.nc
    m.tag = "two_"
    with ExitStack() as ctx:
        norm = Norm(m, ctx, "rms", rms=True)
        turn = Turn(m, ctx, "h", m.rows, m.act_t, m.lnw[:, 1, :])
        acc = m.acc[:].rearrange("p (t d) -> p t d", t=NT)
        block = ctx.enter_context(nc.Block())

        @block.vector
        def _(dve):
            norm.vector(dve, lambda t: acc[:, t, :])
            for t in range(NT):
                norm.apply(m.rows[:, t, :], acc[:, t, :], t).then_inc(turn.rows_ready, 1)
            for b in range(NB):
                turn.vector(dve, b)

        @block.scalar
        def _(act):
            norm.scalar(act)
            turn.scalar(act)

        @block.tensor
        def _(pe):
            turn.tensor(pe)




def experts(m, dram):
    nc = m.nc
    m.tag = "moe_"
    half = NT * PART // 2
    steps = 2 * (NE + 1)
    with ExitStack() as ctx:
        sb = lambda name, shape, dt=F32: m.sb(name, shape, dt, ctx=ctx)
        sem = lambda name: m.sem(name, ctx=ctx)
        wr_raw = sb("wr_raw", [PART, NC, NE])
        wr = sb("wr", [PART, 2, NC, NE], F32R)
        bias = sb("bias", [PART, NE])
        score = sb("score", [PART, NT, NE])
        biased = sb("biased", [PART, NT, NE])
        best = sb("best", [PART, NT, TOPK])
        struck = sb("struck", [PART, NT, NE])
        gate = sb("gate", [PART, NT, NE])
        gsum = sb("gsum", [PART, NT])
        gate_t = sb("gate_t", [NE, NT * PART])
        w_raw = [sb(f"w_raw{i}", [PART, EW]) for i in range(2)]
        w = [sb(f"w{i}", [PART, 2, EW], F32R) for i in range(2)]
        share = [sb(f"share{i}", [PART, NT * PART]) for i in range(2)]
        silu = [sb(f"silu{i}", [PART, half]) for i in range(2)]
        scaled = [sb(f"scaled{i}", [PART, half]) for i in range(2)]
        hidden = [sb(f"hidden{i}", [PART, half]) for i in range(2)]
        hid = [sb(f"hid{i}", [PART, 2, half], F32R) for i in range(2)]
        final = Norm(m, ctx, "ln_o")

        wr_loaded, wr_hi, wr_ready = sem("wr_loaded"), sem("wr_hi"), sem("wr_ready")
        routed, sigmoid_done, route = sem("routed"), sem("sigmoid_done"), sem("route")
        gates_ready = sem("gates_ready")
        gate_turned, gate_copied, gate_out = sem("gate_turned"), sem("gate_copied"), sem("gate_out")
        w_loaded = [sem(f"w_loaded{i}") for i in range(2)]
        share_loaded = [sem(f"share_loaded{i}") for i in range(2)]
        ones_ready = sem("ones_ready")
        up_hi, up_ready = sem("up_hi"), sem("up_ready")
        dn_hi, dn_ready = sem("dn_hi"), sem("dn_ready")
        gu_full = sem("gu_full")
        silu_done = sem("silu_done")
        scaled_done = sem("scaled_done")
        hidden_done = sem("hidden_done")
        hid_hi = sem("hid_hi")
        hid_ready = sem("hid_ready")
        down_done = sem("down_done")
        ended, ln_done, added, out_done = sem("ended"), sem("ln_done"), sem("added"), sem("out_done")

        acc = m.acc[:].rearrange("p (t d) -> p t d", t=NT)
        gu = [[m.banks[:, 2 * i + j, :] for j in range(2)] for i in range(2)]
        sums = m.banks[:, 4:8, :].rearrange("p k (a d) -> p (k a) d", a=2)
        act_b = m.act_t[:].rearrange("p (b n) -> p b n", b=NB)
        UP = 2 * NC * FF

        def tokens(part, c, t):
            at = part * NC * SEQ + c * SEQ + (t % NTT) * PART
            return act_b[:, t // NTT, at:at + PART]

        def half_tokens(part, c, n):
            at = part * NC * SEQ + c * SEQ
            return act_b[:, NB // 2 * n:NB // 2 * (n + 1), at:at + SEQ]

        def loads(e, par):
            raw = w_raw[par][:]
            gu_view = raw[:, 0:UP].rearrange("p (j c i) -> p j c i", j=2, c=NC)
            if isinstance(e, int) and e == 0:
                src = [dram[n].rearrange("(c p) i -> p c i", p=PART) for n in ("wsg", "wsu")]
                down = dram["wsd"]
            else:
                src = [dram[n][bass.ds(e - 1, 1), :, :].rearrange("e (c p) i -> p (e c) i", p=PART)
                       for n in ("wg", "wu")]
                down = dram["wd"][bass.ds(e - 1, 1), :, :].rearrange("e p d -> p (e d)")
            return [(gu_view[:, 0, :, :], src[0]), (gu_view[:, 1, :, :], src[1]), (raw[:, UP:EW], down)]

        block = ctx.enter_context(nc.Block())

        @block.sync
        def _(sp):
            def load(e, par):
                wait(sp, dn_ready, e - 1)
                for dst, src in loads(e, par):
                    sp.dma_start(dst, src).then_inc(w_loaded[par], 16)

            def load_share(e, par):
                wait(sp, scaled_done, 2 * (e - 1))
                row = dram["gates"][bass.ds(e - 1, 1), :].to_broadcast([PART, NT * PART])
                sp.dma_start(share[par][:], row).then_inc(share_loaded[par], 16)

            load(0, 0)
            load(1, 1)
            sp.wait_ge(gate_copied, 1)
            sp.dma_start(dram["gates"], gate_t[:]).then_inc(gate_out, 16)
            sp.wait_ge(gate_out, 16)
            load_share(1, 1)
            load(2, 0)
            with sp.Fori(0, NE // 2 - 1) as j:
                for k in range(2):
                    load_share(2 * j + 2 + k, k)
                    load(2 * j + 3 + k, 1 - k)
            load_share(NE, 0)
            sp.wait_ge(share_loaded[0], 16 * (NE // 2))
            for t in range(NT):
                sp.wait_ge(added, t + 1)
                sp.dma_start(dram["out"].rearrange("b (t p) d -> p (b t) d", p=PART)[:, t, :],
                             m.rows[:, t, :]).then_inc(out_done, 16)
            sp.wait_ge(out_done, 16 * NT)


        def pe_up(pe, e, n, par):
            H = 2 * e + n
            if n == 0:
                wait(pe, up_ready, e + 1)
            wait(pe, hidden_done, H - 1)
            for j in range(2):
                for c in range(NC):
                    at = (j * NC + c) * FF
                    last = three(nc, gu[n][j], w[par][:, 0, at:at + FF], w[par][:, 1, at:at + FF],
                                 half_tokens(0, c, n), half_tokens(1, c, n), c == 0, c == NC - 1)
            last.then_inc(gu_full, 1)

        def pe_down(pe, e, n, par, first=False, end=False):
            H = 2 * e + n
            wait(pe, dn_ready, e + 1)
            wait(pe, hid_ready, H + 1)
            for t in range(NT // 2):
                last = three(nc, sums[:, n * (NT // 2) + t, :],
                             hid[n][:, 0, t * PART:(t + 1) * PART], hid[n][:, 1, t * PART:(t + 1) * PART],
                             w[par][:, 0, UP:EW], w[par][:, 1, UP:EW],
                             first and t % 2 == 0, end and t % 2 == 1, skip=True)
            last.then_inc(down_done, 1)

        @block.tensor
        def _(pe):
            pe.wait_ge(wr_ready, 1)
            for t in range(NT):
                for c in range(NC):
                    last = three(nc, gu[1][1][:, t * NE:(t + 1) * NE], tokens(0, c, t), tokens(1, c, t),
                                 wr[:, 0, c, :], wr[:, 1, c, :], c == 0, c == NC - 1)
            last.then_inc(routed, 1)
            pe_up(pe, 0, 0, 0)
            pe.wait_ge(sigmoid_done, 1)
            pe_up(pe, 0, 1, 0)
            pe.wait_ge(gates_ready, 1)
            for t in range(NT):
                last = nc.tensor.transpose(m.banks[0:NE, 4 + t // 4, (t % 4) * PART:(t % 4 + 1) * PART],
                                           gate[:, t, :], m.ident[:])
            last.then_inc(gate_turned, 1)
            for n in range(2):
                pe_up(pe, 1, n, 1)
                pe.wait_ge(gate_copied, 1)
                pe_down(pe, 0, n, 0, first=True)
            with pe.Fori(0, NE // 2 - 1) as j:
                for k in range(2):
                    for n in range(2):
                        pe_up(pe, 2 * j + 2 + k, n, k)
                        pe_down(pe, 2 * j + 1 + k, n, 1 - k)
            for n in range(2):
                pe_up(pe, NE, n, 0)
                pe_down(pe, NE - 1, n, 1)
            for n in range(2):
                pe_down(pe, NE, n, 0, end=True)


        def act_split_up(act, e, par, k):
            wait(act, w_loaded[par], 16 * 3 * (k + 1))
            wait(act, gu_full, 2 * (e - 1))
            nc.scalar.activation(w[par][:, 0, 0:UP], w_raw[par][:, 0:UP], ACT.Copy).then_inc(up_hi, 1)

        def act_split_down(act, e, par):
            wait(act, down_done, 2 * (e - 1))
            nc.scalar.activation(w[par][:, 0, UP:EW], w_raw[par][:, UP:EW], ACT.Copy).then_inc(dn_hi, 1)

        def act_silu(act, e, n):
            H = 2 * e + n
            wait(act, gu_full, H + 1)
            wait(act, scaled_done, H - 1)
            nc.scalar.activation(silu[n][:], gu[n][0], ACT.Silu).then_inc(silu_done, 1)

        def act_hidden(act, e, n):
            H = 2 * e + n
            wait(act, hidden_done, H + 1)
            wait(act, down_done, H - 1)
            nc.scalar.activation(hid[n][:, 0, :], hidden[n][:], ACT.Copy).then_inc(hid_hi, 1)

        def act_expert(act, e, par, k):
            act_silu(act, e, 0)
            act_hidden(act, e - 1, 1)
            act_split_down(act, e, par)
            if k is not None:
                act_split_up(act, e + 1, 1 - par, k)
            act_silu(act, e, 1)
            act_hidden(act, e, 0)

        @block.scalar
        def _(act):
            act.dma_start(wr_raw[:], dram["wr"].rearrange("(c p) e -> p c e", p=PART)).then_inc(wr_loaded, 16)
            act.dma_start(bias[:], dram["expert_bias"].rearrange("(o e) -> o e", o=1).to_broadcast([PART, NE])
                          ).then_inc(wr_loaded, 16)
            act.wait_ge(wr_loaded, 32)
            nc.scalar.activation(wr[:, 0, :, :], wr_raw[:], ACT.Copy).then_inc(wr_hi, 1)
            act_split_up(act, 0, 0, 0)
            act.wait_ge(routed, 1)
            nc.scalar.activation(score[:].rearrange("p t e -> p (t e)"), gu[1][1][:, 0:NT * NE],
                                 ACT.Sigmoid).then_inc(sigmoid_done, 1)
            act_split_down(act, 0, 0)
            act_split_up(act, 1, 1, 0)
            act_silu(act, 0, 0)
            act_silu(act, 0, 1)
            act.wait_ge(gate_turned, 1)
            for i in range(2):
                last = nc.scalar.activation(gate_t[:, i * half:(i + 1) * half], m.banks[0:NE, 4 + i, :],
                                            ACT.Copy)
            last.then_inc(gate_copied, 1)
            act_hidden(act, 0, 0)
            with act.Fori(0, NE // 2 - 1) as j:
                for k in range(2):
                    act_expert(act, 2 * j + 1 + k, 1 - k, j + 1)
            act_expert(act, NE - 1, 1, NE // 2)
            act_expert(act, NE, 0, None)
            act_hidden(act, NE, 1)
            final.scalar(act)


        def pool_split_up(pool, e, par):
            wait(pool, up_hi, e + 1)
            nc.gpsimd.tensor_tensor(w[par][:, 1, 0:UP], w_raw[par][:, 0:UP],
                                    w[par][:, 0, 0:UP].bitcast(F32), ALU.subtract).then_inc(up_ready, 1)

        def pool_split_down(pool, e, par):
            wait(pool, dn_hi, e + 1)
            nc.gpsimd.tensor_tensor(w[par][:, 1, UP:EW], w_raw[par][:, UP:EW],
                                    w[par][:, 0, UP:EW].bitcast(F32), ALU.subtract).then_inc(dn_ready, 1)

        def pool_scale(pool, e, n, par):
            H = 2 * e + n
            wait(pool, silu_done, H + 1)
            wait(pool, hidden_done, H - 1)
            nc.gpsimd.tensor_tensor(scaled[n][:], silu[n][:], share[par][:, n * half:(n + 1) * half],
                                    ALU.mult).then_inc(scaled_done, 1)

        def pool_expert(pool, e, par, k, more=True):
            wait(pool, share_loaded[par], 16 * k)
            pool_scale(pool, e, 0, par)
            pool_split_down(pool, e, par)
            if more:
                pool_split_up(pool, e + 1, 1 - par)
            pool_scale(pool, e, 1, par)

        @block.gpsimd
        def _(pool):
            nc.gpsimd.memset(share[0][:], 1.0).then_inc(ones_ready, 1)
            pool_split_up(pool, 0, 0)
            pool_split_down(pool, 0, 0)
            pool.wait_ge(ones_ready, 1)
            pool_scale(pool, 0, 0, 0)
            pool_split_up(pool, 1, 1)
            pool_scale(pool, 0, 1, 0)
            with pool.Fori(0, NE // 2 - 1) as j:
                for k in range(2):
                    pool_expert(pool, 2 * j + 1 + k, 1 - k, j + 1)
            pool_expert(pool, NE - 1, 1, NE // 2)
            pool_expert(pool, NE, 0, NE // 2, more=False)


        def dve_hidden(dve, e, n):
            H = 2 * e + n
            wait(dve, scaled_done, H + 1)
            wait(dve, hid_ready, H - 1)
            nc.vector.tensor_tensor(hidden[n][:], gu[n][1], scaled[n][:], ALU.mult).then_inc(hidden_done, 1)

        def dve_split(dve, e, n):
            H = 2 * e + n
            wait(dve, hid_hi, H + 1)
            nc.vector.tensor_tensor(hid[n][:, 1, :], hidden[n][:], hid[n][:, 0, :].bitcast(F32),
                                    ALU.subtract).then_inc(hid_ready, 1)

        def dve_expert(dve, e):
            dve_hidden(dve, e, 0)
            dve_split(dve, e - 1, 1)
            dve_hidden(dve, e, 1)
            dve_split(dve, e, 0)

        def dve_route(dve):
            n = [0]

            def link(instruction):
                n[0] += 1
                instruction.then_inc(route, 1)
                return n[0]

            dve.wait_ge(sigmoid_done, 1)
            rows_bias = bias[:].unsqueeze(1).to_broadcast([PART, NT, NE])
            at = link(nc.vector.tensor_tensor(biased[:], score[:], rows_bias, ALU.add))
            dve.wait_ge(route, at)
            for t in range(NT):
                at = link(nc.vector.max(best[:, t, :], biased[:, t, :]))
            for t in range(NT):
                dve.wait_ge(route, at - NT + t + 1)
                last = link(nc.vector.match_replace(struck[:, t, :], best[:, t, :], biased[:, t, :], NEG))
            dve.wait_ge(route, last)
            at = link(nc.vector.tensor_tensor(gate[:], struck[:], biased[:], ALU.not_equal))
            dve.wait_ge(route, at)
            at = link(nc.vector.tensor_tensor(gate[:], gate[:], score[:], ALU.mult))
            dve.wait_ge(route, at)
            at = link(nc.vector.reduce_sum(gsum[:], gate[:], AX))
            dve.wait_ge(route, at)
            at = link(nc.vector.reciprocal(gsum[:], gsum[:]))
            dve.wait_ge(route, at)
            nc.vector.tensor_tensor(gate[:], gate[:], gsum[:].unsqueeze(2).to_broadcast([PART, NT, NE]),
                                    ALU.mult).then_inc(gates_ready, 1)

        @block.vector
        def _(dve):
            dve.wait_ge(wr_hi, 1)
            nc.vector.tensor_tensor(wr[:, 1, :, :], wr_raw[:], wr[:, 0, :, :].bitcast(F32),
                                    ALU.subtract).then_inc(wr_ready, 1)
            dve_route(dve)
            dve_hidden(dve, 0, 0)
            dve_hidden(dve, 0, 1)
            dve_split(dve, 0, 0)
            with dve.Fori(1, NE + 1) as e:
                dve_expert(dve, e)
            dve_split(dve, NE, 1)
            dve.wait_ge(down_done, steps)
            for t in range(NT):
                nc.vector.tensor_tensor(acc[:, t, :], sums[:, t, :], acc[:, t, :], ALU.add).then_inc(ended, 1)
            final.vector(dve, lambda t: acc[:, t, :], lambda t: dve.wait_ge(ended, t + 1))
            for t in range(NT):
                final.apply(m.rows[:, t, :], acc[:, t, :], t).then_inc(ln_done, 1)
            for t in range(NT):
                dve.wait_ge(ln_done, t + 1)
                nc.vector.tensor_tensor(m.rows[:, t, :], m.rows[:, t, :], m.x[:, t, :],
                                        ALU.add).then_inc(added, 1)




def program(nc, dram):
    with ExitStack() as ctx:
        m = Machine(nc, ctx)
        m.banks = ctx.enter_context(nc.psum_tensor("banks", [PART, 8, 512], F32))
        m.s_ps = m.banks[:, 0:2, :]
        m.pt_ps = m.banks[:, 2:4, :].rearrange("p k n -> p (k n)")
        m.qt_ps, m.pj_ps, m.o_ps, m.y_ps = (m.banks[:, 4 + i, :] for i in range(4))
        m.ident = m.sb("ident", [PART, PART])
        m.ident16 = m.sb("ident16", [PART, PART], BF16)
        m.mask = m.sb("mask", [PART, PART], BF16)
        m.rope = m.sb("rope_sb", [PART, 4, NTT, DH])
        m.lnw = m.sb("lnw", [PART, 2, NC])
        m.x = m.sb("x", [PART, NT, D])
        m.acc = m.sb("acc", [PART, NT * D])
        m.act_t = m.sb("act_t", [PART, NB * SLOT], F32R)
        weights = ctx.enter_context(ExitStack())
        m.b_w = m.sb("b_w", [PART, 2 * 2 * B_W], F32R, ctx=weights)
        m.b_w_raw = m.sb("b_w_raw", [PART, B_W], ctx=weights)
        with ExitStack() as early:
            m.rows = m.sb("rows1", [PART, NT, D], ctx=early)
            m.a_wqkv = m.sb("a_wqkv", [PART, 2 * 2 * NC * A_QKV], F32R, ctx=early)
            m.a_wo = m.sb("a_wo", [PART, 2 * NC * D], F32R, ctx=early)
            prepare(m, dram)
            with ExitStack() as stage:
                AttentionA(m, stage).build(dram)
            join(m)
        with ExitStack() as stage:
            AttentionB(m, stage).build(dram)
        weights.close()
        with ExitStack() as late:
            m.tag = ""
            m.rows = m.sb("rows2", [PART, NT, D], ctx=late)
            norm_two(m)
            experts(m, dram)



_NAMES = {
    "x": "L0_attn_x", "a_wq": "L0_attn_Wq", "a_wk": "L0_attn_Wk", "a_wv": "L0_attn_Wv",
    "a_wo": "L0_attn_Wo", "ln1_w": "L0_ffn_ln1_w", "ln2_w": "L0_ffn_ln2_w", "b_wq": "L0_ffn_Wq",
    "b_wk": "L0_ffn_Wk", "b_wv": "L0_ffn_Wv", "b_wo": "L0_ffn_Wo", "wr": "L0_ffn_Wr",
    "expert_bias": "L0_ffn_expert_bias", "wg": "L0_ffn_Wg", "wu": "L0_ffn_Wu", "wd": "L0_ffn_Wd",
    "wsg": "L0_ffn_Wsg", "wsu": "L0_ffn_Wsu", "wsd": "L0_ffn_Wsd",
}


def rope_tables():
    freq = (np.float32(1.0) / np.float32(10000.0) ** (np.arange(0, DH, 2, dtype=np.float32) / np.float32(DH)))
    angle = (np.arange(SEQ, dtype=np.float32)[:, None] * freq[None, :]).astype(np.float64)
    cos, sin = np.cos(angle), np.sin(angle)
    tables = np.stack([np.concatenate([cos, cos], 1), np.concatenate([-sin, sin], 1)])
    both = np.concatenate([tables / np.sqrt(float(DH)), tables]).astype(np.float32)
    return np.ascontiguousarray(both.reshape(4, NTT, PART, DH).transpose(2, 0, 1, 3))


def kernel(**inputs):
    import concourse.bacc as bacc
    from concourse.bass_utils import run_bass_kernel_spmd

    nc = bacc.Bacc("TRN2", target_bir_lowering=False, num_devices=1)
    arrays, dram = {}, {}
    for name, source in _NAMES.items():
        a = np.ascontiguousarray(inputs[source])
        arrays["in_" + name] = a
        dram[name] = nc.dram_tensor("in_" + name, a.shape, F32, kind="ExternalInput").ap()
    arrays["rope"] = rope_tables()
    dram["rope"] = nc.dram_tensor("rope", arrays["rope"].shape, F32, kind="ExternalInput").ap()
    dram["gates"] = nc.dram_tensor("gates", (NE, NT * PART), F32, kind="Internal").ap()
    dram["out"] = nc.dram_tensor("out", (NB, SEQ, D), F32, kind="ExternalOutput").ap()
    program(nc, dram)
    result = run_bass_kernel_spmd(nc, [arrays], core_ids=[0])
    return result.results[0]["out"]
```

```python
from contextlib import ExitStack

import numpy as np
import concourse.bass as bass
from concourse import mybir

F32 = mybir.dt.float32
F32R = mybir.dt.float32r
BF16 = mybir.dt.bfloat16
ALU = mybir.AluOpType
ACT = mybir.ActivationFunctionType
AX = mybir.AxisListType.X

PART = 128
NB, SEQ, D = 4, 256, 256
NC = D // PART
NTT = SEQ // PART
NT = NB * NTT
SLOT = 2 * NC * SEQ
EPS = 1e-5
NEG = -1e30
HPI, PAIRS = 8, 4
PCOLS = PART + SEQ

A_HEADS, A_DH = 16, 16
A_ITS = NB * A_HEADS // HPI
A_QKV = 3 * HPI * A_DH
STACK = 64
KV, DH = 4, 128
B_ITS = NB * KV
B_QKV = HPI * DH + 2 * DH
B_WQ = NC * B_QKV
B_WO = HPI * D
B_W = B_WQ + B_WO
WQUART = B_W // 4

NE, TOPK, FF = 32, 8, 128
EW = 2 * NC * FF + D


def wait(eng, sem, value):
    if isinstance(value, int) and value <= 0:
        return
    eng.wait_ge(sem, value)


def three(nc, out, w_hi, w_lo, m_hi, m_lo, start, stop, skip=False):
    nc.tensor.matmul(out, w_lo, m_hi, start=start, stop=False, skip_group_check=skip)
    nc.tensor.matmul(out, w_hi, m_lo, start=False, stop=False, skip_group_check=skip)
    return nc.tensor.matmul(out, w_hi, m_hi, start=False, stop=stop, skip_group_check=skip)


class Machine:

    def __init__(self, nc, ctx):
        self.nc = nc
        self.ctx = ctx
        self.tag = ""
        self.tables = 0

    def load_table(self, act, function):
        out = self.spare[:, self.tables:self.tables + 1]
        self.tables += 1
        self.nc.scalar.activation(out, self.ident[:, 0:1], function)

    def sb(self, name, shape, dt=F32, ctx=None):
        return (ctx or self.ctx).enter_context(self.nc.sbuf_tensor(self.tag + name, shape, dt))

    def sem(self, name, ctx=None):
        return (ctx or self.ctx).enter_context(self.nc.semaphore(self.tag + name))




class Norm:

    LN = (0,)
    RMS = (2,)
    LN_AND_RMS = (0, 1)

    def __init__(self, m, ctx, name, kinds=LN):
        self.m, self.kinds = m, kinds
        K = len(kinds)
        self.stats = m.sb(name + "_stats", [PART, NT, 6], ctx=ctx)
        self.mv = m.sb(name + "_mv", [PART, NT, 2], ctx=ctx)
        self.den = m.sb(name + "_den", [PART, K, NT], ctx=ctx)
        self.factor = m.sb(name + "_factor", [PART, K, NT], ctx=ctx)
        self.shift = m.sb(name + "_shift", [PART, K, NT], ctx=ctx)
        self.step = m.sem(name + "_step", ctx=ctx)
        self.steps = 0
        self.var_ready = m.sem(name + "_var_ready", ctx=ctx)
        self.root_ready = m.sem(name + "_root_ready", ctx=ctx)
        self.ready = m.sem(name + "_ready", ctx=ctx)

    def link(self, instruction):
        self.steps += 1
        instruction.then_inc(self.step, 1)
        return self.steps

    def moments(self, dve, b, tile, arrived=None):
        nc = self.m.nc
        lo, hi = NTT * b, NTT * (b + 1)
        mean, var = self.mv[:, lo:hi, 0], self.mv[:, lo:hi, 1]
        for t in range(lo, hi):
            if arrived:
                arrived(t)
            at = self.link(nc.vector.bn_stats(self.stats[:, t, :], tile(t)))
        for t in range(lo, hi):
            dve.wait_ge(self.step, at - (hi - 1 - t))
            last = self.link(nc.vector.bn_aggr(self.mv[:, t, :], self.stats[:, t, :]))
        dve.wait_ge(self.step, last)
        for i, kind in enumerate(self.kinds):
            den = self.den[:, i, lo:hi]
            if kind == 0:
                last = nc.vector.tensor_scalar(den, var, EPS, None, ALU.add)
            elif kind == 1:
                last = nc.vector.tensor_scalar(den, var, 1.0 + EPS, EPS * EPS, ALU.mult, ALU.add)
            else:
                at = self.link(nc.vector.tensor_tensor(self.factor[:, i, lo:hi], mean, mean, ALU.mult))
                dve.wait_ge(self.step, at)
                last = nc.vector.scalar_tensor_tensor(out=den, in0=self.factor[:, i, lo:hi], scalar=EPS,
                                                      in1=var, op0=ALU.add, op1=ALU.add)
        last.then_inc(self.var_ready, 1)

    def roots(self, act, b):
        den = self.den[:, :, NTT * b:NTT * (b + 1)]
        act.wait_ge(self.var_ready, b + 1)
        self.m.nc.scalar.activation(den, den, ACT.Sqrt).then_inc(self.root_ready, 1)

    def factors(self, dve, b):
        nc = self.m.nc
        lo, hi = NTT * b, NTT * (b + 1)
        dve.wait_ge(self.root_ready, b + 1)
        at = self.link(nc.vector.reciprocal(self.factor[:, :, lo:hi], self.den[:, :, lo:hi]))
        dve.wait_ge(self.step, at)
        for i in range(len(self.kinds)):
            last = nc.vector.scalar_tensor_tensor(
                out=self.shift[:, i, lo:hi], in0=self.mv[:, lo:hi, 0], scalar=-1.0,
                in1=self.factor[:, i, lo:hi], op0=ALU.mult, op1=ALU.mult)
        last.then_inc(self.ready, 1)

    def apply(self, act, out, src, t, i=0):
        factor = self.factor[:, i, t:t + 1]
        if t % NTT == 0:
            act.wait_ge(self.ready, t // NTT + 1)
        if self.kinds[i] == 2:
            return self.m.nc.scalar.activation(out, src, ACT.Copy, scale=factor)
        return self.m.nc.scalar.activation(out, src, ACT.Identity, scale=factor,
                                           bias=self.shift[:, i, t:t + 1])


class Turn:

    def __init__(self, m, ctx, name, src, dst, first_bank=0, weight=None):
        self.m, self.src, self.dst, self.weight, self.first_bank = m, src, dst, weight, first_bank
        self.rows_ready = m.sem(name + "_rows_ready", ctx=ctx)
        self.turned = m.sem(name + "_turned", ctx=ctx)
        self.hi_done = m.sem(name + "_hi_done", ctx=ctx)
        self.lo_done = m.sem(name + "_lo_done", ctx=ctx)

    def bank(self, b):
        return self.m.banks[:, self.first_bank + b, :].rearrange("p (c t) -> p c t", c=NC)

    def slot(self, b, part, c):
        at = b * SLOT + part * NC * SEQ + c * SEQ
        return self.dst[:, at:at + SEQ]

    def tensor(self, pe, b):
        nc = self.m.nc
        pe.wait_ge(self.rows_ready, b + 1)
        for t in range(NTT):
            for c in range(NC):
                last = nc.tensor.transpose(self.bank(b)[:, c, t * PART:(t + 1) * PART],
                                           self.src[:, NTT * b + t, c * PART:(c + 1) * PART],
                                           self.m.ident[:])
        last.then_inc(self.turned, 1)

    def scalar(self, act, b):
        nc = self.m.nc
        act.wait_ge(self.turned, b + 1)
        for c in range(NC):
            scale = 1.0 if self.weight is None else self.weight[:, c:c + 1]
            last = nc.scalar.activation(self.slot(b, 0, c), self.bank(b)[:, c, :], ACT.Copy,
                                        scale=scale)
        last.then_inc(self.hi_done, 1)

    def vector(self, dve, b):
        nc = self.m.nc
        dve.wait_ge(self.hi_done, b + 1)
        for c in range(NC):
            scale = 1.0 if self.weight is None else self.weight[:, c:c + 1]
            last = nc.vector.scalar_tensor_tensor(
                out=self.slot(b, 1, c), in0=self.bank(b)[:, c, :], scalar=scale,
                in1=self.slot(b, 0, c).bitcast(F32), op0=ALU.mult, op1=ALU.subtract)
        last.then_inc(self.lo_done, 1)


def pipeline(stages, between=None):
    for s in range(NB + max(lag for lag, _ in stages)):
        for lag, stage in stages:
            if 0 <= s - lag < NB:
                stage(s - lag)
        if between:
            between(s)




def prepare(m, dram):
    nc = m.nc
    m.tag = "pre_"
    with ExitStack() as ctx:
        w_nat = m.sb("w_nat", [PART, 4, NC, D], ctx=ctx)
        norm = Norm(m, ctx, "ln_x")
        turn = Turn(m, ctx, "x", m.rows, m.act_t)
        sem = lambda name: m.sem(name, ctx=ctx)
        x_loaded = [sem(f"x_loaded{t}") for t in range(NT)]
        w_loaded = [sem(f"w_loaded{i}") for i in range(4)]
        tables_loaded = sem("tables_loaded")
        zeroed, const_ready = sem("zeroed"), sem("const_ready")
        w_turned, w_hi, w_lo = sem("w_turned"), sem("w_hi"), sem("w_lo")
        block = ctx.enter_context(nc.Block())

        def w_bank(i):
            return (m.qt_ps, m.pj_ps)[i % 2][:].rearrange("p (c n) -> p c n", c=NC)

        def w_slot(i, part):
            if i == 3:
                at = part * NC * D
                return m.a_wo[:, at:at + NC * D].rearrange("p (c n) -> p c n", c=NC)
            at = part * 2 * NC * A_QKV
            half = m.a_wqkv[:, at:at + 2 * NC * A_QKV]
            return half.rearrange("p (g c n) -> p c g n", g=2, c=NC)[:, :, :, i * PART:(i + 1) * PART]

        @block.sync
        def _(sp):
            x = dram["x"].rearrange("b (t p) d -> p (b t) d", p=PART)
            for t in range(NT):
                sp.dma_start(m.x[:, t, :], x[:, t, :]).then_inc(x_loaded[t], 16)
            sp.dma_start(m.rope[:], dram["rope"]).then_inc(tables_loaded, 16)
            for i, name in enumerate(("ln1_w", "ln2_w")):
                sp.dma_start(m.lnw[:, i, :], dram[name].rearrange("(c p) -> p c", p=PART),
                             allow_slow_non_contiguous=True).then_inc(tables_loaded, 16)
            for dst, src in group_weights(m, dram, 0):
                sp.dma_start(dst, src).then_inc(tables_loaded, 16)
            sp.wait_ge(tables_loaded, 16 * (3 + W_DMAS))

        @block.gpsimd
        def _(pool):
            for buf in (m.ident, m.ident16, m.mask):
                nc.gpsimd.memset(buf[:], 0.0).then_inc(zeroed, 1)
            pool.wait_ge(zeroed, 3)
            for buf in (m.ident, m.ident16):
                nc.gpsimd.affine_select(out=buf[:], in_=buf[:], compare_op=ALU.not_equal, fill=1.0,
                                        base=0, pattern=[[-1, PART]],
                                        channel_multiplier=1).then_inc(const_ready, 1)
            nc.gpsimd.affine_select(out=m.mask[:], in_=m.mask[:], compare_op=ALU.is_ge, fill=NEG,
                                    base=0, pattern=[[-1, PART]],
                                    channel_multiplier=1).then_inc(const_ready, 1)
            nc.gpsimd.memset(m.b_w[:, 2 * B_W:4 * B_W].bitcast(F32), 0.0)
            nc.gpsimd.memset(m.q_stack[:].bitcast(F32), 0.0)
            nc.gpsimd.memset(m.acc[:], 0.0)

        def pe_weights(pe, i):
            if i == 0:
                pe.wait_ge(const_ready, 3)
            pe.wait_ge(w_loaded[i], 16)
            wait(pe, w_lo, i - 1)
            for r in range(NC):
                for c in range(NC):
                    last = nc.tensor.transpose(w_bank(i)[:, c, r * PART:(r + 1) * PART],
                                               w_nat[:, i, r, c * PART:(c + 1) * PART], m.ident[:])
            last.then_inc(w_turned, 1)

        @block.tensor
        def _(pe):
            pipeline(((0, lambda i: pe_weights(pe, i)), (1, lambda b: turn.tensor(pe, b))))

        def w_views(i, part):
            src = w_bank(i)
            if i < 3:
                src = src.rearrange("p c (g n) -> p c g n", g=2)
            return w_slot(i, part), src

        w_scale = [float(A_DH) ** -0.5, 1.0, 1.0, 1.0]

        def act_weights(act, i):
            act.wait_ge(w_turned, i + 1)
            dst, src = w_views(i, 0)
            nc.scalar.activation(dst, src, ACT.Copy, scale=w_scale[i]).then_inc(w_hi, 1)

        def act_rows(act, b):
            for t in range(NTT * b, NTT * (b + 1)):
                last = norm.apply(act, m.rows[:, t, :], m.x[:, t, :], t)
            last.then_inc(turn.rows_ready, 1)

        @block.scalar
        def _(act):
            for i, name in enumerate(("a_wq", "a_wk", "a_wv", "a_wo")):
                act.dma_start(w_nat[:, i, :, :], dram[name].rearrange("(r p) n -> p r n", p=PART),
                              ).then_inc(w_loaded[i], 16)
            pipeline(((0, lambda b: norm.roots(act, b)), (0, lambda i: act_weights(act, i)),
                      (1, lambda b: turn.scalar(act, b)), (0, lambda b: act_rows(act, b))))

        def dve_weights(dve, i):
            dve.wait_ge(w_hi, i + 1)
            dst, src = w_views(i, 1)
            hi, _ = w_views(i, 0)
            for c in range(NC):
                last = nc.vector.scalar_tensor_tensor(
                    out=dst[:, c], in0=src[:, c], scalar=w_scale[i], in1=hi[:, c].bitcast(F32),
                    op0=ALU.mult, op1=ALU.subtract)
            last.then_inc(w_lo, 1)

        @block.vector
        def _(dve):
            arrived = lambda t: dve.wait_ge(x_loaded[t], 16)
            pipeline(((0, lambda b: norm.moments(dve, b, lambda t: m.x[:, t, :], arrived)),
                      (1, lambda b: turn.vector(dve, b)), (0, lambda b: norm.factors(dve, b)),
                      (0, lambda i: dve_weights(dve, i))))




class Attention:

    DRAIN = 5

    ITS = UNITS = 0
    UNROLL = 1
    LATE_NEXT = False
    QUERIES_LATE = None
    POOL_NORMALISES = False

    def __init__(self, m, ctx, tag):
        self.m, self.ctx = m, ctx
        m.tag = tag
        sb, sem = self.sb, self.sem
        self.src_t = sb("src_t", [PART, SLOT], F32R)
        self.qt = sb("qt", [PART, 2, 2, 2 * SEQ], F32R)
        self.prob = sb("prob", [PART, PAIRS, 2, PCOLS])
        self.prob_t = sb("prob_t", [PART, 2, 2, 2 * PCOLS], F32R)
        self.negmax = sb("negmax", [PART, 2, 2, NTT])
        self.sums = sb("sums", [PART, PAIRS, 2 * NTT])
        self.rsum = sb("rsum", [PART, PAIRS, 2 * NTT])
        self.src_loaded = sem("src_loaded")
        self.unit_full = sem("unit_full")
        self.unit_free = sem("unit_free")
        self.qt_full = sem("qt_full")
        self.qt_hi = sem("qt_hi")
        self.qt_ready = sem("qt_ready")
        self.s_full = sem("s_full")
        self.max_ready = sem("max_ready")
        self.exp_done = sem("exp_done")
        self.rsum_ready = sem("rsum_ready")
        self.prob_ready = sem("prob_ready")
        self.pt_full = sem("pt_full")
        self.pt_hi = sem("pt_hi")
        self.pt_ready = sem("pt_ready")
        self.pv_done = sem("pv_done")
        self.o_hi = sem("o_hi")
        self.o_ready = sem("o_ready")
        self.w_done = sem("w_done")
        self.y_added = sem("y_added")
        self.v_raw = sem("v_raw")
        self.v_hi = sem("v_hi")
        self.v_ready = sem("v_ready")
        self.kt_ready = sem("kt_ready")

    def sb(self, name, shape, dt=F32):
        return self.m.sb(name, shape, dt, ctx=self.ctx)

    def sem(self, name):
        return self.m.sem(name, ctx=self.ctx)


    COPIED = 3

    def src(self, it, part, c, t):
        at = part * NC * SEQ + c * SEQ + t * PART
        if isinstance(it, int) and it < self.COPIED:
            at += self.batch(it) * SLOT
            return self.m.act_t[:, at:at + PART]
        return self.src_t[:, at:at + PART]

    def wait_src(self, pe, it):
        if not (isinstance(it, int) and it < self.COPIED):
            pe.wait_ge(self.src_loaded, 16 * (it - self.COPIED + 1))

    def pe_scores(self, pe, it, p, P):
        nc, m = self.m.nc, self.m
        wait(pe, self.qt_ready, P + 1)
        self.pe_wait_keys(pe, it, p)
        for h in range(2):
            wait(pe, self.exp_done, 2 * P - 1 + h)
            for t in range(NTT):
                lo, width = t * PART, (t + 1) * PART
                out = m.s_ps[:, h, lo:lo + width]
                diagonal = m.s_ps[:, h, lo + width - PART:lo + width]
                self.pe_score(out, it, p, h, t, width)
                last = nc.tensor.matmul(diagonal, m.ident16[:], m.mask[:], start=False, stop=True)
            last.then_inc(self.s_full, 1)

    def pe_prob_t(self, pe, p, P):
        nc, m = self.m.nc, self.m
        wait(pe, self.prob_ready, P + 1)
        wait(pe, self.pt_ready, P)
        for h in range(2):
            for at, col in ((h * SEQ, 0), (h * SEQ + PART, PART), (2 * SEQ + h * PART, 2 * PART)):
                last = nc.tensor.transpose(m.pt_ps[:, at:at + PART],
                                           self.prob[:, p, h, col:col + PART], m.ident[:])
        last.then_inc(self.pt_full, 1)

    def stage(self, it, p, lag):
        P = PAIRS * it + p - lag
        if isinstance(P, int) and not 0 <= P < PAIRS * self.ITS:
            return None
        return it + (p - lag) // PAIRS, (p - lag) % PAIRS, P

    def early_unit(self, p, units):
        return self.schedule[p][0] if units and self.schedule[p] else None

    def late_unit(self, it, p, units):
        if p == 0:
            known = isinstance(it, int) and not 0 < it < self.ITS
            return None if known or len(self.schedule[-1]) < 2 else (it, self.schedule[-1][1])
        return (it + 1, self.schedule[p - 1][1]) if units and len(self.schedule[p - 1]) > 1 else None

    def slot_pe(self, pe, it, p, units=True):
        if now := self.stage(it, p, 0):
            self.pe_scores(pe, *now)
        if self.LATE_NEXT and (late := self.late_unit(it, p, units)):
            self.pe_unit(pe, *late)
        ahead = self.stage(it, p, -1)
        if ahead and p != self.QUERIES_LATE:
            self.pe_queries_t(pe, *ahead)
        if out := self.stage(it, p, 5):
            self.pe_project(pe, *out)
        if values := self.stage(it, p, 4):
            self.pe_values(pe, *values)
        u = self.early_unit(p, units)
        if u is not None and p != self.QUERIES_LATE:
            self.pe_unit(pe, it + 1, u)
        if prob := self.stage(it, p, 2):
            self.pe_prob_t(pe, *prob[1:])
        if ahead and p == self.QUERIES_LATE:
            self.pe_queries_t(pe, *ahead)
            if u is not None:
                self.pe_unit(pe, it + 1, u)
        if not self.LATE_NEXT and u is not None and len(self.schedule[p]) > 1:
            self.pe_unit(pe, it + 1, self.schedule[p][1])


    def act_exp(self, act, p, P):
        nc, m = self.m.nc, self.m
        wait(act, self.pt_full, P - PAIRS + 1)
        for h in range(2):
            wait(act, self.max_ready, 2 * P + 1 + h)
            for t in range(NTT):
                lo, width = t * PART, (t + 1) * PART
                k = 2 * h + t
                last = nc.scalar.activation(self.prob[:, p, h, lo:lo + width],
                                            m.s_ps[:, h, lo:lo + width], ACT.Exp,
                                            bias=self.negmax[:, p % 2, t, h:h + 1],
                                            accum_out=self.sums[:, p, k:k + 1])
            last.then_inc(self.exp_done, 1)

    def act_prob_t(self, act, p, P):
        wait(act, self.pt_full, P + 1)
        wait(act, self.pv_done, P - 1)
        self.m.nc.scalar.activation(self.prob_t[:, p % 2, 0, :], self.m.pt_ps[:, 0:2 * PCOLS],
                                    ACT.Copy).then_inc(self.pt_hi, 1)

    def slot_act(self, act, it, p, units=True):
        if prob := self.stage(it, p, 3):
            self.act_prob_t(act, *prob[1:])
        if late := self.late_unit(it, p, units):
            self.act_unit(act, *late)
        ahead = self.stage(it, p, -1)
        if ahead and p != self.QUERIES_LATE:
            self.act_queries(act, *ahead)
        if now := self.stage(it, p, 0):
            self.act_exp(act, *now[1:])
        if ahead and p == self.QUERIES_LATE:
            self.act_queries(act, *ahead)
        if out := self.stage(it, p, 4):
            self.act_outputs(act, *out)
        u = self.early_unit(p, units)
        if u is not None:
            self.act_unit(act, it + 1, u)
        if now and p == PAIRS - 1:
            self.act_values(act, it)
        if now and p == PAIRS - 2:
            self.act_weights(act, it)


    def dve_max(self, dve, p, P):
        nc, m = self.m.nc, self.m
        wait(dve, self.exp_done, 2 * P - 2)
        for h in range(2):
            wait(dve, self.s_full, 2 * P + 1 + h)
            for t in range(NTT):
                lo, width = t * PART, (t + 1) * PART
                last = nc.vector.tensor_reduce(self.negmax[:, p % 2, t, h:h + 1],
                                               m.s_ps[:, h, lo:lo + width], AX, ALU.max, negate=True)
            last.then_inc(self.max_ready, 1)

    def dve_normalise(self, dve, p, P):
        nc = self.m.nc
        wait(dve, self.exp_done, 2 * P + 2)
        nc.vector.reciprocal(self.rsum[:, p, :], self.sums[:, p, :]).then_inc(self.rsum_ready, 1)
        if self.POOL_NORMALISES:
            return
        wait(dve, self.rsum_ready, P + 1)
        for h in range(2):
            for t in range(NTT):
                lo, width = t * PART, (t + 1) * PART
                k = 2 * h + t
                row = self.prob[:, p, h, lo:lo + width]
                last = nc.vector.tensor_scalar(row, row, self.rsum[:, p, k:k + 1], None, ALU.mult)
        last.then_inc(self.prob_ready, 1)

    def pool_normalise(self, pool, p, P):
        wait(pool, self.rsum_ready, P + 1)
        rsum = self.rsum[:, p, :].rearrange("p (h t) -> p h t", h=2)
        for t in range(NTT):
            lo, width = t * PART, (t + 1) * PART
            rows = self.prob[:, p, :, lo:lo + width]
            last = self.m.nc.gpsimd.tensor_tensor(
                rows, rows, rsum[:, :, t:t + 1].to_broadcast([PART, 2, width]), ALU.mult)
        last.then_inc(self.prob_ready, 1)

    def dve_wait_sum(self, dve):
        pass

    def dve_prob_t(self, dve, p, P):
        wait(dve, self.pt_hi, P + 1)
        self.m.nc.vector.tensor_tensor(self.prob_t[:, p % 2, 1, :], self.m.pt_ps[:, 0:2 * PCOLS],
                                       self.prob_t[:, p % 2, 0, :].bitcast(F32),
                                       ALU.subtract).then_inc(self.pt_ready, 1)

    def dve_add(self, dve, it):
        into = self.m.acc[:, bass.ds(self.batch(it) * (NTT * D), NTT * D)]
        self.dve_wait_sum(dve)
        wait(dve, self.w_done, self.projected(it))
        wait(dve, self.y_added, it)
        self.m.nc.vector.tensor_tensor(into, self.m.y_ps[:], into, ALU.add).then_inc(self.y_added, 1)

    def slot_dve(self, dve, it, p, units=True):
        if now := self.stage(it, p, 0):
            self.dve_max(dve, *now[1:])
        if ahead := self.stage(it, p, -1):
            self.dve_queries(dve, *ahead)
        late = self.late_unit(it, p, units)
        if late and self.LATE_NEXT:
            self.dve_unit(dve, *late)
        if prob := self.stage(it, p, 3):
            self.dve_prob_t(dve, *prob[1:])
        if late and not self.LATE_NEXT:
            self.dve_unit(dve, *late)
        if before := self.stage(it, p, 1):
            self.dve_normalise(dve, *before[1:])
        if out := self.stage(it, p, 4):
            self.dve_outputs(dve, *out)
        u = self.early_unit(p, units)
        if u is not None:
            self.dve_unit(dve, it + 1, u)
        if now and p == PAIRS - 1:
            self.dve_values(dve, it)
        if p == 0 and not (isinstance(it, int) and it < 2):
            self.dve_add(dve, it - 2)


    def run(self, eng, slot, middles):
        for it in range(2):
            for p in range(PAIRS):
                slot(eng, it, p)
        for first, last in middles:
            self.splitting = last <= self.ITS - NB
            with eng.Fori(first // self.UNROLL, last // self.UNROLL) as step:
                for k in range(self.UNROLL):
                    self.parity = k
                    for p in range(PAIRS):
                        slot(eng, step * self.UNROLL + k, p)
        for it in range(middles[-1][1], self.ITS):
            for p in range(PAIRS):
                slot(eng, it, p, units=it < self.ITS - 1)
        for P in range(PAIRS * self.ITS, PAIRS * self.ITS + self.DRAIN):
            slot(eng, P // PAIRS, P % PAIRS, units=False)


class AttentionA(Attention):

    ITS, UNITS = A_ITS, 4
    LATE_NEXT = True
    UNROLL = 2
    POOL_NORMALISES = True
    schedule = ((), (0,), (1,), (2, 3))

    def __init__(self, m, ctx):
        super().__init__(m, ctx, "a_")
        sb, sem = self.sb, self.sem
        rest = m.b_w[:, 2 * B_W:4 * B_W]

        def place(n, pattern, **sizes):
            nonlocal rest
            rest, taken = rest[:, n:], rest[:, 0:n]
            return taken.rearrange(pattern, **sizes)

        self.v = place(2 * NTT * HPI * PART, "p (a t h n) -> p a t h n", a=2, t=NTT, h=HPI)
        self.k_stack = place(NTT * HPI * STACK, "p (t n) -> p t n", t=NTT)
        self.kt = place(2 * PAIRS * SEQ, "p n -> p n")
        self.v_row = sb("v_row", [PART, 2 * NTT * HPI * A_DH])
        self.ot = sb("ot", [PART, 2, SEQ], F32R)
        self.w_raw_hi = sem("w_raw_hi")
        self.stack_hi = sem("stack_hi")
        self.stack_ready = sem("stack_ready")

    def q_stack(self, it, t, at, n):
        width = HPI * PART
        return self.m.q_stack[:, bass.ds((it % 2) * (NTT * width) + (t * width + at), n)]

    def slot_pool(self, pool, it, p, units=True):
        if before := self.stage(it, p, 1):
            self.pool_normalise(pool, *before[1:])

    @staticmethod
    def batch(it):
        return it // 2

    @staticmethod
    def projected(it):
        return it + 1

    def weights(self, part, c, group):
        at = part * 2 * NC * A_QKV + c * A_QKV
        return self.m.a_wqkv[:, bass.ds(group * (NC * A_QKV) + at, A_QKV)]

    def pe_unit(self, pe, it, u):
        nc, m = self.m.nc, self.m
        n = self.UNITS * it + u
        if u < NTT:
            self.wait_src(pe, it)
            wait(pe, self.unit_free, n)
            for c in range(NC):
                last = three(nc, m.pj_ps[:, 0:A_QKV], self.src(it, 0, c, u), self.src(it, 1, c, u),
                             self.weights(0, c, it % 2), self.weights(1, c, it % 2),
                             c == 0, c == NC - 1)
        else:
            wait(pe, self.stack_ready, NTT * (it + 1))
            wait(pe, self.unit_free, n)
            for q in range(2):
                pair = 2 * (u - NTT) + q
                for t in range(NTT):
                    at = q * SEQ + t * PART
                    last = nc.tensor.transpose(
                        m.pj_ps[:, at:at + PART],
                        self.k_stack[:, t, pair * PART:(pair + 1) * PART].bitcast(F32), m.ident[:])
        last.then_inc(self.unit_full, 1)

    def pe_queries_t(self, pe, it, p, P):
        nc, m = self.m.nc, self.m
        wait(pe, self.stack_ready, NTT * (it + 1))
        wait(pe, self.qt_ready, P)
        par = it % 2 if isinstance(it, int) else (self.parity + (p == 0)) % 2
        for h in range(2):
            at = (2 * p + h) * PART - (STACK if h else 0)
            for t in range(NTT):
                last = nc.tensor.transpose(m.qt_ps[:, h * SEQ + t * PART:h * SEQ + (t + 1) * PART],
                                           self.q_stack(par, t, at, PART).bitcast(F32), m.ident[:])
        last.then_inc(self.qt_full, 1)

    def pe_wait_keys(self, pe, it, p):
        if p % 2 == 0:
            wait(pe, self.kt_ready, 2 * it + p // 2 + 1)

    def keys(self, it, p, n):
        return self.kt[:, bass.ds((it % 2) * (PAIRS * SEQ) + p * SEQ, n)]

    def pe_score(self, out, it, p, h, t, width):
        at = h * SEQ + t * PART
        self.m.nc.tensor.matmul(out, self.qt[:, p % 2, 0, at:at + PART], self.keys(it, p, width),
                                start=True, stop=False)

    def pe_values(self, pe, it, p, P):
        nc, m = self.m.nc, self.m
        wait(pe, self.pt_ready, P + 1)
        if p == 0:
            wait(pe, self.v_ready, it + 1)
            wait(pe, self.o_ready, it)
        par = p % 2
        for h in range(2):
            head = 2 * p + h
            for k in range(NTT):
                width = SEQ - k * PART
                at = h * SEQ if k == 0 else 2 * SEQ + h * PART
                last = three(nc, m.o_ps[:, k * PART:SEQ],
                             self.v[:, 0, k, head, :], self.v[:, 1, k, head, :],
                             self.prob_t[:, par, 0, at:at + width], self.prob_t[:, par, 1, at:at + width],
                             head == 0 and k == 0, head == HPI - 1 and k == NTT - 1)
        last.then_inc(self.pv_done, 1)

    def pe_project(self, pe, it, p, P):
        if p != PAIRS - 1:
            return
        nc, m = self.m.nc, self.m
        wait(pe, self.o_ready, it + 1)
        wait(pe, self.y_added, it)
        at = (it % 2) * D
        for t in range(NTT):
            last = three(nc, m.y_ps[:, t * D:(t + 1) * D],
                         self.ot[:, 0, t * PART:(t + 1) * PART], self.ot[:, 1, t * PART:(t + 1) * PART],
                         m.a_wo[:, bass.ds(at, D)], m.a_wo[:, bass.ds(at + NC * D, D)], True, True)
        last.then_inc(self.w_done, 1)

    def act_outputs(self, act, it, p, P):
        if p != PAIRS - 1:
            return
        wait(act, self.pv_done, P + 1)
        wait(act, self.w_done, it)
        self.m.nc.scalar.activation(self.ot[:, 0, :], self.m.o_ps[:, 0:SEQ],
                                    ACT.Copy).then_inc(self.o_hi, 1)

    def dve_outputs(self, dve, it, p, P):
        if p != PAIRS - 1:
            return
        wait(dve, self.o_hi, it + 1)
        self.m.nc.vector.tensor_tensor(self.ot[:, 1, :], self.m.o_ps[:, 0:SEQ],
                                       self.ot[:, 0, :].bitcast(F32),
                                       ALU.subtract).then_inc(self.o_ready, 1)

    def values(self, it, t):
        n = HPI * A_DH
        return self.v_row[:, bass.ds((it % 2) * (NTT * n) + t * n, n)]

    def v_view(self, part, t):
        base = self.v[:, part, t, 0, 0:A_DH]
        return bass.AP(tensor=base.tensor, offset=base.offset,
                       ap=[list(base.ap[0]), [PART + A_DH, HPI], [1, A_DH]])

    def act_values(self, act, it):
        nc = self.m.nc
        wait(act, self.v_raw, NTT * (it + 1))
        wait(act, self.pv_done, PAIRS * it)
        for t in range(NTT):
            row = self.values(it, t).rearrange("p (h d) -> p h d", h=HPI)
            last = nc.scalar.activation(self.v_view(0, t), row, ACT.Copy)
        last.then_inc(self.v_hi, 1)

    def dve_values(self, dve, it):
        nc = self.m.nc
        wait(dve, self.v_hi, it + 1)
        for t in range(NTT):
            row = self.values(it, t).rearrange("p (h d) -> p h d", h=HPI)
            last = nc.vector.tensor_tensor(self.v_view(1, t), row, self.v_view(0, t).bitcast(F32),
                                           ALU.subtract)
        last.then_inc(self.v_ready, 1)

    def act_queries(self, act, it, p, P):
        wait(act, self.qt_full, P + 1)
        wait(act, self.s_full, 2 * P - 2)
        self.m.nc.scalar.activation(self.qt[:, p % 2, 0, :], self.m.qt_ps[:],
                                    ACT.Copy).then_inc(self.qt_ready, 1)

    def dve_queries(self, dve, it, p, P):
        pass

    def act_weights(self, act, it):
        pass

    def stack_views(self, it, u):
        heads = lambda x, n: x.rearrange("p (h n) -> p h n", h=n)
        pj = self.m.pj_ps
        q, k, v = (pj[:, i * PART:(i + 1) * PART] for i in range(3))
        qs = heads(self.q_stack(it, u, 0, HPI * PART), HPI)[:, :, 0:STACK].rearrange("p h (s d) -> p h s d", d=A_DH)
        ks = heads(self.k_stack[:, u, :], HPI).rearrange("p h (s d) -> p h s d", d=A_DH)
        return heads(q, HPI), heads(k, HPI), v, qs, ks

    def act_unit(self, act, it, u):
        nc, m = self.m.nc, self.m
        n = self.UNITS * it + u
        wait(act, self.unit_full, n + 1)
        if u < NTT:
            wait(act, self.qt_full, PAIRS * (it - 1))
            wait(act, self.unit_free, self.UNITS * it)
            q, k, _, qs, ks = self.stack_views(it, u)
            for src, dst in ((q, qs[:, :, 0:2, :]), (k, ks[:, :, 0:3:2, :])):
                twice = src.unsqueeze(2).to_broadcast([PART, HPI, 2, A_DH])
                last = nc.scalar.activation(dst, twice, ACT.Copy)
            last.then_inc(self.stack_hi, 1)
        else:
            wait(act, self.s_full, 2 * PAIRS * (it - 1))
            nc.scalar.activation(self.keys(it, 2 * (u - NTT), 2 * SEQ), m.pj_ps[:],
                                 ACT.Copy).then_inc(self.kt_ready, 1)
            act.wait_ge(self.kt_ready, 2 * it + u - NTT + 1)
            act.sem_inc(self.unit_free, 1)

    def dve_unit(self, dve, it, u):
        if u >= NTT:
            return
        nc = self.m.nc
        wait(dve, self.stack_hi, NTT * it + u + 1)
        q, k, v, qs, ks = self.stack_views(it, u)
        nc.vector.tensor_tensor(qs[:, :, 2, :], q, qs[:, :, 0, :].bitcast(F32), ALU.subtract)
        nc.vector.tensor_tensor(ks[:, :, 1, :], k, ks[:, :, 0, :].bitcast(F32),
                                ALU.subtract).then_inc(self.stack_ready, 1)
        wait(dve, self.v_ready, it - 1)
        nc.vector.tensor_copy(self.values(it, u), v).then_inc(self.v_raw, 1)
        dve.wait_ge(self.v_raw, NTT * it + u + 1)
        dve.sem_inc(self.unit_free, 1)

    def build(self, dram):
        nc, m = self.m.nc, self.m
        middles = ((2, self.ITS - 2),)
        block = self.ctx.enter_context(nc.Block())

        @block.sync
        def _(sp):
            def load(it, b):
                if not isinstance(it, int):
                    sp.wait_ge(self.unit_full, self.UNITS * (it - 1) + NTT)
                sp.dma_start(self.src_t[:].bitcast(F32), self.m.act_t[:, bass.ds(b * SLOT, SLOT)].bitcast(F32),
                             ).then_inc(self.src_loaded, 16)
            load(self.COPIED, 1)
            with sp.Fori(2, NB) as b:
                load(2 * b, b)
                load(2 * b + 1, b)
            sp.wait_ge(self.src_loaded, 16 * (self.ITS - self.COPIED))

        @block.gpsimd
        def _(pool):
            for q in range(4):
                pool.wait_ge(self.w_raw_hi, q + 1)
                at = slice(q * WQUART, (q + 1) * WQUART)
                nc.gpsimd.tensor_tensor(m.b_w[:, B_W:2 * B_W][:, at], m.b_w_raw[:, at],
                                        m.b_w[:, at].bitcast(F32), ALU.subtract)
            self.run(pool, self.slot_pool, middles)

        @block.tensor
        def _(pe):
            for u in range(NTT):
                self.pe_unit(pe, 0, u)
            self.pe_queries_t(pe, 0, 0, 0)
            for u in range(NTT, self.UNITS):
                self.pe_unit(pe, 0, u)
            self.run(pe, self.slot_pe, middles)

        @block.scalar
        def _(act):
            def split_weights(q):
                at = slice(q * WQUART, (q + 1) * WQUART)
                nc.scalar.activation(m.b_w[:, at], m.b_w_raw[:, at], ACT.Copy).then_inc(self.w_raw_hi, 1)
            for u in range(NTT):
                split_weights(u)
                self.act_unit(act, 0, u)
            self.act_queries(act, 0, 0, 0)
            for u in range(NTT, self.UNITS):
                split_weights(u)
                self.act_unit(act, 0, u)
            m.load_table(act, ACT.Exp)
            self.run(act, self.slot_act, middles)
            m.load_table(act, ACT.Sqrt)

        @block.vector
        def _(dve):
            for u in range(self.UNITS):
                self.dve_unit(dve, 0, u)
            self.run(dve, self.slot_dve, middles)


W_DMAS = 4


def group_weights(m, dram, g):
    q = HPI * DH
    raw_in = m.b_w_raw[:, 0:B_WQ].rearrange("p (c n) -> p c n", c=NC)
    raw_out = m.b_w_raw[:, B_WQ:B_W].rearrange("p (h n) -> p h n", h=HPI)
    wq, wk, wv = (dram[n].rearrange("(c p) n -> p c n", p=PART) for n in ("b_wq", "b_wk", "b_wv"))
    wo = dram["b_wo"].rearrange("(h p) n -> p h n", p=DH)
    return [(raw_in[:, :, 0:q], wq[:, :, bass.ds(g * q, q)]),
            (raw_in[:, :, q:q + DH], wk[:, :, bass.ds(g * DH, DH)]),
            (raw_in[:, :, q + DH:q + 2 * DH], wv[:, :, bass.ds(g * DH, DH)]),
            (raw_out, wo[:, bass.ds(g * HPI, HPI), :])]


class AttentionB(Attention):

    ITS, UNITS = B_ITS, 7
    KV0, KV1, Q00, Q01, KT, Q10, Q11 = range(7)
    schedule = ((KV0, KV1), (Q00, Q01), (KT,), (Q10, Q11))
    Q_OF = {Q00: (0, 0), Q01: (0, 1), Q10: (1, 0), Q11: (1, 1)}
    KV_OF = {KV0: 0, KV1: 1}
    ROT = {KV0: 0, KV1: 1, Q00: 2, Q01: 3, Q10: 4, Q11: 5}
    NROT = len(ROT)

    def __init__(self, m, ctx):
        super().__init__(m, ctx, "b_")
        sb, sem = self.sb, self.sem
        self.w, self.w_raw = m.b_w, m.b_w_raw
        self.raw = sb("raw", [PART, 2, 4 * DH])
        self.cos_part = sb("cos_part", [PART, 2, 4 * DH])
        self.sin_part = sb("sin_part", [PART, 2, 4 * DH])
        self.q_row = sb("q_row", [PART, 2, NTT, 4 * DH])
        self.k_row = sb("k_row", [PART, NTT, DH])
        self.v_row = sb("v_row", [PART, 2 * NTT * DH])
        self.kt = sb("kt", [PART, 2 * 2 * SEQ], F32R)
        self.v = sb("v", [PART, 2, NTT, DH], F32R)
        self.ot = sb("ot", [PART, 2, 2, 2 * SEQ], F32R)
        self.w_loaded = sem("w_loaded")
        self.w_hi = sem("w_hi")
        self.w_ready = sem("w_ready")
        self.raw_ready = sem("raw_ready")
        self.cos_ready = sem("cos_ready")
        self.sin_ready = sem("sin_ready")
        self.rotated = sem("rotated")
        self.kt_hi = sem("kt_hi")
        rows = self.prob[:].rearrange("p a h n -> p (a h n)")[:, 0:NT * D]
        self.join = Join(m, ctx, rows.rearrange("p (t d) -> p t d", t=NT))

    BEHIND_STEP = {4: (KV0, KV1), 5: (Q00,), 6: (Q01, KT)}
    BEHIND_ALL = (Q10, Q11)

    @staticmethod
    def batch(it):
        return it % NB

    @staticmethod
    def projected(it):
        return PAIRS * (it + 1)

    def w_at(self, it, part, offset, n):
        group = it // NB
        return self.w[:, bass.ds((group % 2) * (2 * B_W) + (part * B_W + offset), n)]

    def unit_bank(self, it, u):
        m = self.m
        return (m.pj_ps, m.o_ps, m.y_ps)[u % 3] if isinstance(it, int) and it == 0 else m.pj_ps

    def bank_free(self, it, n):
        return n - 2 if isinstance(it, int) and it == 0 else n

    def pe_unit(self, pe, it, u):
        nc, m = self.m.nc, self.m
        n = self.UNITS * it + u
        if u == self.KT:
            wait(pe, self.rotated, self.NROT * it + self.ROT[self.KV1] + 1)
            wait(pe, self.unit_free, self.bank_free(it, n))
            for t in range(NTT):
                last = nc.tensor.transpose(self.unit_bank(it, u)[:, t * PART:(t + 1) * PART], self.k_row[:, t, :],
                                           m.ident[:])
            last.then_inc(self.unit_full, 1)
            return
        self.wait_src(pe, it)
        wait(pe, self.w_ready, 4 * (it // NB) + 3)
        wait(pe, self.unit_free, self.bank_free(it, n))
        if u in self.Q_OF:
            half, t = self.Q_OF[u]
            col, width = half * 4 * DH, 4 * DH
        else:
            t = self.KV_OF[u]
            col, width = HPI * DH, 2 * DH
        for c in range(NC):
            last = three(nc, self.unit_bank(it, u)[:, 0:width], self.src(it, 0, c, t), self.src(it, 1, c, t),
                         self.w_at(it, 0, c * B_QKV + col, width),
                         self.w_at(it, 1, c * B_QKV + col, width), c == 0, c == NC - 1)
        last.then_inc(self.unit_full, 1)

    def pe_queries_t(self, pe, it, p, P):
        nc, m = self.m.nc, self.m
        half = p // 2
        unit = self.Q01 if half == 0 else self.Q11
        wait(pe, self.rotated, self.NROT * it + self.ROT[unit] + 1)
        wait(pe, self.qt_ready, P)
        for h in range(2):
            head = 2 * (p % 2) + h
            for t in range(NTT):
                at = h * SEQ + t * PART
                last = nc.tensor.transpose(m.qt_ps[:, at:at + PART],
                                           self.q_row[:, half, t, head * DH:(head + 1) * DH], m.ident[:])
        last.then_inc(self.qt_full, 1)

    def pe_wait_keys(self, pe, it, p):
        if p == 0:
            wait(pe, self.kt_ready, it + 1)

    def keys(self, it, part, n):
        return self.kt[:, bass.ds((it % 2) * (2 * SEQ) + part * SEQ, n)]

    def pe_score(self, out, it, p, h, t, width):
        at = h * SEQ + t * PART
        q = lambda part: self.qt[:, p % 2, part, at:at + PART]
        three(self.m.nc, out, q(0), q(1), self.keys(it, 0, width), self.keys(it, 1, width), True, False)

    def pe_values(self, pe, it, p, P):
        nc, m = self.m.nc, self.m
        wait(pe, self.pt_ready, P + 1)
        if p == 0:
            wait(pe, self.v_ready, it + 1)
        wait(pe, self.o_ready, P)
        pt = lambda part: self.prob_t[:, p % 2, part, :]
        three(nc, m.o_ps[:], self.v[:, 0, 0, :], self.v[:, 1, 0, :],
              pt(0)[:, 0:2 * SEQ], pt(1)[:, 0:2 * SEQ], True, False)
        later = m.o_ps[:].rearrange("p (h q) -> p h q", h=2)[:, :, PART:SEQ]
        tail = lambda part: pt(part)[:, 2 * SEQ:2 * PCOLS].rearrange("p (h q) -> p h q", h=2)
        last = three(nc, later, self.v[:, 0, 1, :], self.v[:, 1, 1, :], tail(0), tail(1), False, True)
        last.then_inc(self.pv_done, 1)

    def pe_project(self, pe, it, p, P):
        nc, m = self.m.nc, self.m
        wait(pe, self.o_ready, P + 1)
        if p == 0:
            wait(pe, self.y_added, it)
            wait(pe, self.w_ready, 4 * (it // NB) + 4)
        for h in range(2):
            for t in range(NTT):
                at = h * SEQ + t * PART
                o = lambda part: self.ot[:, p % 2, part, at:at + PART]
                row = B_WQ + (2 * p + h) * D
                last = three(nc, m.y_ps[:, t * D:(t + 1) * D], o(0), o(1), self.w_at(it, 0, row, D),
                             self.w_at(it, 1, row, D), p == 0 and h == 0 and t == 0,
                             p == PAIRS - 1 and h == 1 and t == NTT - 1, skip=True)
        last.then_inc(self.w_done, 1)

    def dve_wait_sum(self, dve):
        dve.wait_ge(self.join.f_ready, NB)

    def act_outputs(self, act, it, p, P):
        wait(act, self.pv_done, P + 1)
        wait(act, self.w_done, P - 1)
        self.m.nc.scalar.activation(self.ot[:, p % 2, 0, :], self.m.o_ps[:],
                                    ACT.Copy).then_inc(self.o_hi, 1)

    def dve_outputs(self, dve, it, p, P):
        wait(dve, self.o_hi, P + 1)
        self.m.nc.vector.tensor_tensor(self.ot[:, p % 2, 1, :], self.m.o_ps[:],
                                       self.ot[:, p % 2, 0, :].bitcast(F32),
                                       ALU.subtract).then_inc(self.o_ready, 1)

    def act_values(self, act, it):
        wait(act, self.v_raw, NTT * (it + 1))
        wait(act, self.pv_done, PAIRS * it)
        self.m.nc.scalar.activation(self.v[:, 0, :, :].rearrange("p t n -> p (t n)"),
                                    self.values(it, 0, NTT), ACT.Copy).then_inc(self.v_hi, 1)

    def values(self, it, t, n):
        return self.v_row[:, bass.ds((it % 2) * (NTT * DH) + t * DH, n * DH)]

    def dve_values(self, dve, it):
        wait(dve, self.v_hi, it + 1)
        self.m.nc.vector.tensor_tensor(self.v[:, 1, :, :].rearrange("p t n -> p (t n)"),
                                       self.values(it, 0, NTT),
                                       self.v[:, 0, :, :].rearrange("p t n -> p (t n)").bitcast(F32),
                                       ALU.subtract).then_inc(self.v_ready, 1)

    def act_queries(self, act, it, p, P):
        wait(act, self.qt_full, P + 1)
        wait(act, self.s_full, 2 * P - 2)
        self.m.nc.scalar.activation(self.qt[:, p % 2, 0, :], self.m.qt_ps[:],
                                    ACT.Copy).then_inc(self.qt_hi, 1)

    def dve_queries(self, dve, it, p, P):
        wait(dve, self.qt_hi, P + 1)
        self.m.nc.vector.tensor_tensor(self.qt[:, p % 2, 1, :], self.m.qt_ps[:],
                                       self.qt[:, p % 2, 0, :].bitcast(F32),
                                       ALU.subtract).then_inc(self.qt_ready, 1)

    def act_unit(self, act, it, u):
        nc, m = self.m.nc, self.m
        wait(act, self.unit_full, self.UNITS * it + u + 1)
        if u == self.KT:
            wait(act, self.s_full, 2 * PAIRS * (it - 1))
            nc.scalar.activation(self.keys(it, 0, SEQ), self.unit_bank(it, u)[:, 0:SEQ],
                                 ACT.Copy).then_inc(self.kt_hi, 1)
            return
        r = self.NROT * it + self.ROT[u]
        wait(act, self.rotated, r - 1)
        n = 4 * DH if u in self.Q_OF else DH
        if u in self.KV_OF:
            wait(act, self.v_ready, it - 1)
            nc.scalar.activation(self.values(it, self.KV_OF[u], 1), self.unit_bank(it, u)[:, DH:2 * DH],
                                 ACT.Copy).then_inc(self.v_raw, 1)
        nc.scalar.activation(self.raw[:, self.ROT[u] % 2, 0:n], self.unit_bank(it, u)[:, 0:n],
                             ACT.Copy).then_inc(self.raw_ready, 1)
        act.wait_ge(self.raw_ready, r + 1)
        act.sem_inc(self.unit_free, 1)

    def dve_unit(self, dve, it, u):
        nc, m = self.m.nc, self.m
        if u == self.KT:
            wait(dve, self.kt_hi, it + 1)
            nc.vector.tensor_tensor(self.keys(it, 1, SEQ), self.unit_bank(it, u)[:, 0:SEQ],
                                    self.keys(it, 0, SEQ).bitcast(F32),
                                    ALU.subtract).then_inc(self.kt_ready, 1)
            wait(dve, self.kt_ready, it + 1)
            dve.sem_inc(self.unit_free, 1)
            return
        r = self.NROT * it + self.ROT[u]
        wait(dve, self.raw_ready, r + 1)
        wait(dve, self.rotated, r - 1)
        out, x, factor = self.rotation(u, self.cos_part, 0)
        nc.vector.tensor_tensor(out, x, factor, ALU.mult).then_inc(self.cos_ready, 1)

    def rotation(self, u, product, kind):
        par = self.ROT[u] % 2
        if u in self.Q_OF:
            (_, t), heads, table = self.Q_OF[u], 4, 0
        else:
            t, heads, table = self.KV_OF[u], 1, 2
        halves = lambda x: x[:, par, 0:heads * DH].rearrange("p (h a d) -> p h a d", h=heads, a=2)
        factor = self.m.rope[:, table + kind, t, :].rearrange("p (a d) -> p a d", a=2)
        factor = factor.unsqueeze(1).to_broadcast([PART, heads, 2, DH // 2])
        x = halves(self.raw)
        return halves(product), x[:, :, ::-1, :] if kind else x, factor

    def pool_unit(self, pool, it, u):
        if u == self.KT:
            return
        nc = self.m.nc
        r = self.NROT * it + self.ROT[u]
        par = self.ROT[u] % 2
        wait(pool, self.raw_ready, r + 1)
        wait(pool, self.rotated, r - 1)
        out, x, factor = self.rotation(u, self.sin_part, 1)
        nc.gpsimd.tensor_tensor(out, x, factor, ALU.mult).then_inc(self.sin_ready, 1)
        wait(pool, self.cos_ready, r + 1)
        wait(pool, self.sin_ready, r + 1)
        if u in self.Q_OF:
            half, t = self.Q_OF[u]
            wait(pool, self.qt_full, PAIRS * (it - 1) + 2 * half + 2)
            out, n = self.q_row[:, half, t, :], 4 * DH
        else:
            t = self.KV_OF[u]
            wait(pool, self.unit_full, self.UNITS * (it - 1) + self.KT + 1)
            out, n = self.k_row[:, t, :], DH
        nc.gpsimd.tensor_tensor(out, self.cos_part[:, par, 0:n], self.sin_part[:, par, 0:n],
                                ALU.add).then_inc(self.rotated, 1)

    def quarter(self, it, part=None):
        q = (it % NB) * WQUART
        if part is None:
            return self.w_raw[:, bass.ds(q, WQUART)]
        group = it // NB + 1
        return self.w[:, bass.ds((group % 2) * (2 * B_W) + q + part * B_W, WQUART)]

    def act_weights(self, act, it):
        if not self.more_weights(it):
            return
        wait(act, self.w_loaded, 16 * W_DMAS * (it // NB + 1))
        wait(act, self.w_done, PAIRS * (it - 2))
        self.m.nc.scalar.activation(self.quarter(it, 0), self.quarter(it), ACT.Copy).then_inc(self.w_hi, 1)

    def slot_pool(self, pool, it, p, units=True):
        if not self.stage(it, p, 0):
            return
        if units:
            for u in self.schedule[p]:
                self.pool_unit(pool, it + 1, u)
        if p == PAIRS - 2 and self.more_weights(it):
            wait(pool, self.w_hi, it + 1)
            self.m.nc.gpsimd.tensor_tensor(self.quarter(it, 1), self.quarter(it),
                                           self.quarter(it, 0).bitcast(F32),
                                           ALU.subtract).then_inc(self.w_ready, 1)

    def more_weights(self, it):
        return it < B_ITS - NB if isinstance(it, int) else self.splitting

    def build(self, dram):
        nc, m = self.m.nc, self.m
        middles = ((2, self.ITS - NB), (self.ITS - NB, self.ITS - 1))
        block = self.ctx.enter_context(nc.Block())

        @block.sync
        def _(sp):
            def load_weights(g):
                wait(sp, self.w_ready, 4 * g)
                for dst, src in group_weights(m, dram, g):
                    sp.dma_start(dst, src).then_inc(self.w_loaded, 16)

            def load_batch(it, b):
                if not (isinstance(it, int) and it == self.COPIED):
                    sp.wait_ge(self.unit_full, self.UNITS * it)
                sp.dma_start(self.src_t[:].bitcast(F32), m.act_t[:, b * SLOT:(b + 1) * SLOT].bitcast(F32),
                             ).then_inc(self.src_loaded, 16)

            load_weights(1)
            sp.wait_ge(self.join.turn.lo_done, NB)
            load_batch(3, 3)
            with sp.Fori(1, KV - 1) as g:
                load_batch(NB * g, 0)
                load_batch(NB * g + 1, 1)
                load_weights(g + 1)
                load_batch(NB * g + 2, 2)
                load_batch(NB * g + 3, 3)
            for b in range(NB):
                load_batch(NB * (KV - 1) + b, b)
            sp.wait_ge(self.src_loaded, 16 * (self.ITS - self.COPIED))

        @block.gpsimd
        def _(pool):
            pool.sem_inc(self.w_ready, 4)
            for u in range(self.UNITS):
                self.pool_unit(pool, 0, u)
            self.join.gpsimd(pool)
            self.run(pool, self.slot_pool, middles)

        def behind(eng, unit):
            def work(s):
                for u in self.BEHIND_STEP.get(s, ()):
                    unit(eng, 0, u)
            return work

        @block.tensor
        def _(pe):
            turn = self.join.turn
            turn.tensor(pe, 0)
            pe.wait_ge(turn.lo_done, 1)
            for s in (4, 5, 6):
                self.pe_unit(pe, 0, self.BEHIND_STEP[s][0])
                turn.tensor(pe, s - 3)
                for u in self.BEHIND_STEP[s][1:]:
                    self.pe_unit(pe, 0, u)
            self.pe_queries_t(pe, 0, 0, 0)
            for u in self.BEHIND_ALL:
                self.pe_unit(pe, 0, u)
            pe.wait_ge(turn.lo_done, NB)
            self.run(pe, self.slot_pe, middles)

        @block.scalar
        def _(act):
            pipeline(self.join.scalar(act), behind(act, self.act_unit))
            m.load_table(act, ACT.Exp)
            self.act_queries(act, 0, 0, 0)
            for u in self.BEHIND_ALL:
                self.act_unit(act, 0, u)
            self.run(act, self.slot_act, middles)

        @block.vector
        def _(dve):
            pipeline(self.join.vector(dve), behind(dve, self.dve_unit))
            self.dve_queries(dve, 0, 0, 0)
            for u in self.BEHIND_ALL:
                self.dve_unit(dve, 0, u)
            self.run(dve, self.slot_dve, middles)




class Join:

    def __init__(self, m, ctx, rows):
        self.m, self.rows = m, rows
        self.norm_a = Norm(m, ctx, "ln_a")
        self.norm_f = Norm(m, ctx, "ln_f", Norm.LN_AND_RMS)
        self.turn = Turn(m, ctx, "h", rows, m.act_t, weight=m.lnw[:, 0, :])
        self.acc = m.acc[:].rearrange("p (t d) -> p t d", t=NT)
        self.attn_ready = m.sem("attn_ready", ctx=ctx)
        self.x1_ready = m.sem("x1_ready", ctx=ctx)
        self.f_ready = m.sem("f_ready", ctx=ctx)

    def vector(self, dve):
        x, acc, norm_a, norm_f = self.m.x, self.acc, self.norm_a, self.norm_f

        def add(b):
            dve.wait_ge(self.attn_ready, b + 1)
            rows = slice(NTT * b, NTT * (b + 1))
            self.m.nc.vector.tensor_tensor(x[:, rows, :], x[:, rows, :], self.rows[:, rows, :],
                                           ALU.add).then_inc(self.x1_ready, 1)

        def arrived(t):
            dve.wait_ge(self.x1_ready, t // NTT + 1)

        return ((4, lambda b: self.turn.vector(dve, b)), (3, lambda b: norm_f.factors(dve, b)),
                (2, add), (2, lambda b: norm_f.moments(dve, b, lambda t: x[:, t, :], arrived)),
                (1, lambda b: norm_a.factors(dve, b)),
                (0, lambda b: norm_a.moments(dve, b, lambda t: acc[:, t, :])))

    def scalar(self, act):
        def attention(b):
            for t in range(NTT * b, NTT * (b + 1)):
                last = self.norm_a.apply(act, self.rows[:, t, :], self.acc[:, t, :], t)
            last.then_inc(self.attn_ready, 1)

        def ffn_input(b):
            for t in range(NTT * b, NTT * (b + 1)):
                last = self.norm_f.apply(act, self.rows[:, t, :], self.m.x[:, t, :], t, 1)
            last.then_inc(self.turn.rows_ready, 1)

        return ((4, lambda b: self.turn.scalar(act, b)), (3, ffn_input),
                (2, lambda b: self.norm_f.roots(act, b)), (1, attention),
                (0, lambda b: self.norm_a.roots(act, b)))

    def gpsimd(self, pool):
        m, norm = self.m, self.norm_f
        for b in range(NB):
            pool.wait_ge(norm.ready, b + 1)
            for t in range(NTT * b, NTT * (b + 1)):
                last = m.nc.gpsimd.tensor_scalar(self.acc[:, t, :], m.x[:, t, :],
                                                 norm.factor[:, 0, t:t + 1], norm.shift[:, 0, t:t + 1],
                                                 ALU.mult, ALU.add)
            last.then_inc(self.f_ready, 1)




def experts(m, dram):
    nc = m.nc
    m.tag = "moe_"
    half = NT * PART // 2
    steps = 2 * (NE + 1)
    with ExitStack() as ctx:
        sb = lambda name, shape, dt=F32: m.sb(name, shape, dt, ctx=ctx)
        sem = lambda name: m.sem(name, ctx=ctx)
        wr_raw = sb("wr_raw", [PART, NC, NE])
        wr = sb("wr", [PART, 2, NC, NE], F32R)
        bias = sb("bias", [PART, NE])
        score = sb("score", [PART, NT, NE])
        biased = sb("biased", [PART, NT, NE])
        best = sb("best", [PART, NT, TOPK])
        struck = sb("struck", [PART, NT, NE])
        gate = sb("gate", [PART, NT, NE])
        gsum = sb("gsum", [PART, NT])
        gate_t = sb("gate_t", [NE, NT * PART])
        w_raw = [sb(f"w_raw{i}", [PART, EW]) for i in range(2)]
        w = [sb(f"w{i}", [PART, 2, EW], F32R) for i in range(2)]
        share = [sb(f"share{i}", [PART, NT * PART]) for i in range(2)]
        silu = [sb(f"silu{i}", [PART, half]) for i in range(2)]
        scaled = [sb(f"scaled{i}", [PART, half]) for i in range(2)]
        hidden = [sb(f"hidden{i}", [PART, half]) for i in range(2)]
        hid = [sb(f"hid{i}", [PART, 2, half], F32R) for i in range(2)]
        norm = Norm(m, ctx, "rms", Norm.RMS)
        turn = Turn(m, ctx, "h", m.rows, m.act_t, first_bank=4, weight=m.lnw[:, 1, :])
        final = Norm(m, ctx, "ln_o")

        wr_loaded, wr_hi, wr_ready = sem("wr_loaded"), sem("wr_hi"), sem("wr_ready")
        routed, sigmoid_done, route = sem("routed"), sem("sigmoid_done"), sem("route")
        gates_ready = sem("gates_ready")
        gate_turned, gate_copied, gate_out = sem("gate_turned"), sem("gate_copied"), sem("gate_out")
        w_loaded = [sem(f"w_loaded{i}") for i in range(2)]
        share_loaded = [sem(f"share_loaded{i}") for i in range(2)]
        ones_ready = sem("ones_ready")
        up_hi, up_ready = sem("up_hi"), sem("up_ready")
        dn_hi, dn_ready = sem("dn_hi"), sem("dn_ready")
        gu_full = sem("gu_full")
        silu_done = sem("silu_done")
        scaled_done = sem("scaled_done")
        hidden_done = sem("hidden_done")
        hid_hi = sem("hid_hi")
        hid_ready = sem("hid_ready")
        down_done = sem("down_done")
        ended = sem("ended")
        ln_done = sem("ln_done")
        added, last_added = sem("added"), sem("last_added")
        out_done = sem("out_done")

        acc = m.acc[:].rearrange("p (t d) -> p t d", t=NT)
        gu = [[m.banks[:, 2 * i + j, :] for j in range(2)] for i in range(2)]
        sums = m.banks[:, 4:8, :].rearrange("p k (a d) -> p (k a) d", a=2)
        act_b = m.act_t[:].rearrange("p (b n) -> p b n", b=NB)
        UP = 2 * NC * FF

        def tokens(part, c, t):
            at = part * NC * SEQ + c * SEQ + (t % NTT) * PART
            return act_b[:, t // NTT, at:at + PART]

        def half_tokens(part, c, n):
            at = part * NC * SEQ + c * SEQ
            return act_b[:, NB // 2 * n:NB // 2 * (n + 1), at:at + SEQ]

        def loads(e, par):
            raw = w_raw[par][:]
            gu_view = raw[:, 0:UP].rearrange("p (j c i) -> p j c i", j=2, c=NC)
            if isinstance(e, int) and e == 0:
                src = [dram[n].rearrange("(c p) i -> p c i", p=PART) for n in ("wsg", "wsu")]
                down = dram["wsd"]
            else:
                src = [dram[n][bass.ds(e - 1, 1), :, :].rearrange("e (c p) i -> p (e c) i", p=PART)
                       for n in ("wg", "wu")]
                down = dram["wd"][bass.ds(e - 1, 1), :, :].rearrange("e p d -> p (e d)")
            return [(gu_view[:, 0, :, :], src[0]), (gu_view[:, 1, :, :], src[1]), (raw[:, UP:EW], down)]

        block = ctx.enter_context(nc.Block())

        @block.sync
        def _(sp):
            def load(e, par):
                wait(sp, dn_ready, e - 1)
                for dst, src in loads(e, par):
                    sp.dma_start(dst, src).then_inc(w_loaded[par], 16)

            def load_share(e, par):
                wait(sp, scaled_done, 2 * (e - 1))
                row = dram["gates"][bass.ds(e - 1, 1), :].to_broadcast([PART, NT * PART])
                sp.dma_start(share[par][:], row).then_inc(share_loaded[par], 16)

            load(0, 0)
            load(1, 1)
            sp.wait_ge(gate_copied, 1)
            sp.dma_start(dram["gates"], gate_t[:]).then_inc(gate_out, 16)
            sp.wait_ge(gate_out, 16)
            load_share(1, 1)
            load(2, 0)
            with sp.Fori(0, NE // 2 - 1) as j:
                for k in range(2):
                    load_share(2 * j + 2 + k, k)
                    load(2 * j + 3 + k, 1 - k)
            load_share(NE, 0)
            sp.wait_ge(share_loaded[0], 16 * (NE // 2))
            for b in range(NB):
                if b < NB - 1:
                    sp.wait_ge(added, b + 1)
                else:
                    sp.wait_ge(last_added, 1)
                sp.dma_start(dram["out"].rearrange("b (t p) d -> b p t d", p=PART)[b],
                             m.rows[:, NTT * b:NTT * (b + 1), :]).then_inc(out_done, 16)
            sp.wait_ge(out_done, 16 * NB)


        def pe_up(pe, e, n, par):
            H = 2 * e + n
            if n == 0:
                wait(pe, up_ready, e + 1)
            wait(pe, hidden_done, H - 1)
            for j in range(2):
                for c in range(NC):
                    at = (j * NC + c) * FF
                    last = three(nc, gu[n][j], w[par][:, 0, at:at + FF], w[par][:, 1, at:at + FF],
                                 half_tokens(0, c, n), half_tokens(1, c, n), c == 0, c == NC - 1)
            last.then_inc(gu_full, 1)

        def pe_down(pe, e, n, par, first=False, end=False):
            H = 2 * e + n
            wait(pe, dn_ready, e + 1)
            wait(pe, hid_ready, H + 1)
            for t in range(NT // 2):
                last = three(nc, sums[:, n * (NT // 2) + t, :],
                             hid[n][:, 0, t * PART:(t + 1) * PART], hid[n][:, 1, t * PART:(t + 1) * PART],
                             w[par][:, 0, UP:EW], w[par][:, 1, UP:EW],
                             first and t % 2 == 0, end and t % 2 == 1, skip=True)
            last.then_inc(down_done, 1)

        @block.tensor
        def _(pe):
            def router(b):
                if b == 0:
                    pe.wait_ge(wr_ready, 1)
                pe.wait_ge(turn.lo_done, b + 1)
                for t in range(NTT * b, NTT * (b + 1)):
                    for c in range(NC):
                        last = three(nc, gu[1][1][:, t * NE:(t + 1) * NE], tokens(0, c, t),
                                     tokens(1, c, t), wr[:, 0, c, :], wr[:, 1, c, :],
                                     c == 0, c == NC - 1)
                last.then_inc(routed, 1)

            pipeline(((0, lambda b: turn.tensor(pe, b)), (1, router)))
            pe_up(pe, 0, 0, 0)
            pe.wait_ge(sigmoid_done, 1)
            pe_up(pe, 0, 1, 0)
            pe.wait_ge(gates_ready, 1)
            for t in range(NT):
                last = nc.tensor.transpose(m.banks[0:NE, 4 + t // 4, (t % 4) * PART:(t % 4 + 1) * PART],
                                           gate[:, t, :], m.ident[:])
            last.then_inc(gate_turned, 1)
            for n in range(2):
                pe_up(pe, 1, n, 1)
                pe.wait_ge(gate_copied, 1)
                pe_down(pe, 0, n, 0, first=True)
            with pe.Fori(0, NE // 2 - 1) as j:
                for k in range(2):
                    for n in range(2):
                        pe_up(pe, 2 * j + 2 + k, n, k)
                        pe_down(pe, 2 * j + 1 + k, n, 1 - k)
            for n in range(2):
                pe_up(pe, NE, n, 0)
                pe_down(pe, NE - 1, n, 1)
            for n in range(2):
                pe_down(pe, NE, n, 0, end=True)


        def act_split_up(act, e, par, k):
            wait(act, w_loaded[par], 16 * 3 * (k + 1))
            wait(act, gu_full, 2 * (e - 1))
            nc.scalar.activation(w[par][:, 0, 0:UP], w_raw[par][:, 0:UP], ACT.Copy).then_inc(up_hi, 1)

        def act_split_down(act, e, par):
            wait(act, down_done, 2 * (e - 1))
            nc.scalar.activation(w[par][:, 0, UP:EW], w_raw[par][:, UP:EW], ACT.Copy).then_inc(dn_hi, 1)

        def act_silu(act, e, n):
            H = 2 * e + n
            wait(act, gu_full, H + 1)
            wait(act, scaled_done, H - 1)
            nc.scalar.activation(silu[n][:], gu[n][0], ACT.Silu).then_inc(silu_done, 1)

        def act_hidden(act, e, n):
            H = 2 * e + n
            wait(act, hidden_done, H + 1)
            wait(act, down_done, H - 1)
            nc.scalar.activation(hid[n][:, 0, :], hidden[n][:], ACT.Copy).then_inc(hid_hi, 1)

        def act_expert(act, e, par, k):
            act_silu(act, e, 0)
            act_hidden(act, e - 1, 1)
            act_split_down(act, e, par)
            if k is not None:
                act_split_up(act, e + 1, 1 - par, k)
            act_silu(act, e, 1)
            act_hidden(act, e, 0)

        @block.scalar
        def _(act):
            act.dma_start(wr_raw[:], dram["wr"].rearrange("(c p) e -> p c e", p=PART)).then_inc(wr_loaded, 16)
            act.dma_start(bias[:], dram["expert_bias"].rearrange("(o e) -> o e", o=1).to_broadcast([PART, NE])
                          ).then_inc(wr_loaded, 16)
            norm.roots(act, 0)
            act.wait_ge(wr_loaded, 32)
            nc.scalar.activation(wr[:, 0, :, :], wr_raw[:], ACT.Copy).then_inc(wr_hi, 1)

            def rows(b):
                for t in range(NTT * b, NTT * (b + 1)):
                    last = norm.apply(act, m.rows[:, t, :], acc[:, t, :], t)
                last.then_inc(turn.rows_ready, 1)

            pipeline(((0, lambda b: b and norm.roots(act, b)), (1, lambda b: turn.scalar(act, b)),
                      (0, rows)))
            act_split_up(act, 0, 0, 0)
            act.wait_ge(routed, NB)
            nc.scalar.activation(score[:].rearrange("p t e -> p (t e)"), gu[1][1][:, 0:NT * NE],
                                 ACT.Sigmoid).then_inc(sigmoid_done, 1)
            act_split_down(act, 0, 0)
            act_split_up(act, 1, 1, 0)
            act_silu(act, 0, 0)
            act_silu(act, 0, 1)
            act.wait_ge(gate_turned, 1)
            for i in range(2):
                last = nc.scalar.activation(gate_t[:, i * half:(i + 1) * half], m.banks[0:NE, 4 + i, :],
                                            ACT.Copy)
            last.then_inc(gate_copied, 1)
            act_hidden(act, 0, 0)
            with act.Fori(0, NE // 2 - 1) as j:
                for k in range(2):
                    act_expert(act, 2 * j + 1 + k, 1 - k, j + 1)
            act_expert(act, NE - 1, 1, NE // 2)
            act_expert(act, NE, 0, None)
            act_hidden(act, NE, 1)

            def output(b):
                for t in range(NTT * b, NTT * (b + 1)):
                    last = final.apply(act, m.rows[:, t, :], acc[:, t, :], t)
                last.then_inc(ln_done, 1)

            pipeline(((1, output), (0, lambda b: final.roots(act, b))))


        def pool_split_up(pool, e, par):
            wait(pool, up_hi, e + 1)
            nc.gpsimd.tensor_tensor(w[par][:, 1, 0:UP], w_raw[par][:, 0:UP],
                                    w[par][:, 0, 0:UP].bitcast(F32), ALU.subtract).then_inc(up_ready, 1)

        def pool_split_down(pool, e, par):
            wait(pool, dn_hi, e + 1)
            nc.gpsimd.tensor_tensor(w[par][:, 1, UP:EW], w_raw[par][:, UP:EW],
                                    w[par][:, 0, UP:EW].bitcast(F32), ALU.subtract).then_inc(dn_ready, 1)

        def pool_scale(pool, e, n, par):
            H = 2 * e + n
            wait(pool, silu_done, H + 1)
            wait(pool, hidden_done, H - 1)
            nc.gpsimd.tensor_tensor(scaled[n][:], silu[n][:], share[par][:, n * half:(n + 1) * half],
                                    ALU.mult).then_inc(scaled_done, 1)

        def pool_expert(pool, e, par, k, more=True):
            wait(pool, share_loaded[par], 16 * k)
            pool_scale(pool, e, 0, par)
            pool_split_down(pool, e, par)
            if more:
                pool_split_up(pool, e + 1, 1 - par)
            pool_scale(pool, e, 1, par)

        @block.gpsimd
        def _(pool):
            nc.gpsimd.memset(share[0][:], 1.0).then_inc(ones_ready, 1)
            pool_split_up(pool, 0, 0)
            pool_split_down(pool, 0, 0)
            pool.wait_ge(ones_ready, 1)
            pool_scale(pool, 0, 0, 0)
            pool_split_up(pool, 1, 1)
            pool_scale(pool, 0, 1, 0)
            with pool.Fori(0, NE // 2 - 1) as j:
                for k in range(2):
                    pool_expert(pool, 2 * j + 1 + k, 1 - k, j + 1)
            pool_expert(pool, NE - 1, 1, NE // 2)
            pool_expert(pool, NE, 0, NE // 2, more=False)
            for b in range(NB - 1):
                pool.wait_ge(ln_done, b + 1)
                rows = slice(NTT * b, NTT * (b + 1))
                nc.gpsimd.tensor_tensor(m.rows[:, rows, :], m.rows[:, rows, :], m.x[:, rows, :],
                                        ALU.add).then_inc(added, 1)


        def dve_hidden(dve, e, n):
            H = 2 * e + n
            wait(dve, scaled_done, H + 1)
            wait(dve, hid_ready, H - 1)
            nc.vector.tensor_tensor(hidden[n][:], gu[n][1], scaled[n][:], ALU.mult).then_inc(hidden_done, 1)

        def dve_split(dve, e, n):
            H = 2 * e + n
            wait(dve, hid_hi, H + 1)
            nc.vector.tensor_tensor(hid[n][:, 1, :], hidden[n][:], hid[n][:, 0, :].bitcast(F32),
                                    ALU.subtract).then_inc(hid_ready, 1)

        def dve_expert(dve, e):
            dve_hidden(dve, e, 0)
            dve_split(dve, e - 1, 1)
            dve_hidden(dve, e, 1)
            dve_split(dve, e, 0)

        def dve_route(dve):
            n = [0]

            def link(instruction):
                n[0] += 1
                instruction.then_inc(route, 1)
                return n[0]

            dve.wait_ge(sigmoid_done, 1)
            rows_bias = bias[:].unsqueeze(1).to_broadcast([PART, NT, NE])
            at = link(nc.vector.tensor_tensor(biased[:], score[:], rows_bias, ALU.add))
            dve.wait_ge(route, at)
            for t in range(NT):
                at = link(nc.vector.max(best[:, t, :], biased[:, t, :]))
            for t in range(NT):
                dve.wait_ge(route, at - NT + t + 1)
                last = link(nc.vector.match_replace(struck[:, t, :], best[:, t, :], biased[:, t, :], NEG))
            dve.wait_ge(route, last)
            at = link(nc.vector.tensor_tensor(gate[:], struck[:], biased[:], ALU.not_equal))
            dve.wait_ge(route, at)
            at = link(nc.vector.tensor_tensor(gate[:], gate[:], score[:], ALU.mult))
            dve.wait_ge(route, at)
            at = link(nc.vector.reduce_sum(gsum[:], gate[:], AX))
            dve.wait_ge(route, at)
            at = link(nc.vector.reciprocal(gsum[:], gsum[:]))
            dve.wait_ge(route, at)
            nc.vector.tensor_tensor(gate[:], gate[:], gsum[:].unsqueeze(2).to_broadcast([PART, NT, NE]),
                                    ALU.mult).then_inc(gates_ready, 1)

        @block.vector
        def _(dve):
            norm.moments(dve, 0, lambda t: acc[:, t, :])
            dve.wait_ge(wr_hi, 1)
            nc.vector.tensor_tensor(wr[:, 1, :, :], wr_raw[:], wr[:, 0, :, :].bitcast(F32),
                                    ALU.subtract).then_inc(wr_ready, 1)
            pipeline(((0, lambda b: b and norm.moments(dve, b, lambda t: acc[:, t, :])),
                      (1, lambda b: turn.vector(dve, b)), (0, lambda b: norm.factors(dve, b))))
            dve_route(dve)
            dve_hidden(dve, 0, 0)
            dve_hidden(dve, 0, 1)
            dve_split(dve, 0, 0)
            with dve.Fori(1, NE + 1) as e:
                dve_expert(dve, e)
            dve_split(dve, NE, 1)

            def total(b):
                dve.wait_ge(down_done, steps - 1 if b < NB // 2 else steps)
                rows = slice(NTT * b, NTT * (b + 1))
                nc.vector.tensor_tensor(acc[:, rows, :], sums[:, rows, :], acc[:, rows, :],
                                        ALU.add).then_inc(ended, 1)

            def arrived(t):
                dve.wait_ge(ended, t // NTT + 1)

            pipeline(((0, total), (1, lambda b: final.factors(dve, b)),
                      (0, lambda b: final.moments(dve, b, lambda t: acc[:, t, :], arrived))))
            dve.wait_ge(ln_done, NB)
            rows = slice(NTT * (NB - 1), NT)
            nc.vector.tensor_tensor(m.rows[:, rows, :], m.rows[:, rows, :], m.x[:, rows, :],
                                    ALU.add).then_inc(last_added, 1)




def program(nc, dram):
    with ExitStack() as ctx:
        m = Machine(nc, ctx)
        m.banks = ctx.enter_context(nc.psum_tensor("banks", [PART, 8, 512], F32))
        m.s_ps = m.banks[:, 0:2, :]
        m.pt_ps = m.banks[:, 2:4, :].rearrange("p k n -> p (k n)")
        m.qt_ps, m.pj_ps, m.o_ps, m.y_ps = (m.banks[:, 4 + i, :] for i in range(4))
        m.ident = m.sb("ident", [PART, PART])
        m.ident16 = m.sb("ident16", [PART, PART], BF16)
        m.mask = m.sb("mask", [PART, PART], BF16)
        m.rope = m.sb("rope_sb", [PART, 4, NTT, DH])
        m.lnw = m.sb("lnw", [PART, 2, NC])
        m.spare = m.sb("spare", [PART, 8])
        m.x = m.sb("x", [PART, NT, D])
        m.acc = m.sb("acc", [PART, NT * D])
        m.act_t = m.sb("act_t", [PART, NB * SLOT], F32R)
        weights = ctx.enter_context(ExitStack())
        m.b_w = m.sb("b_w", [PART, 2 * 2 * B_W], F32R, ctx=weights)
        m.b_w_raw = m.sb("b_w_raw", [PART, B_W], ctx=weights)
        with ExitStack() as early:
            m.rows = m.sb("rows1", [PART, NT, D], ctx=early)
            m.a_wqkv = m.sb("a_wqkv", [PART, 2 * 2 * NC * A_QKV], F32R, ctx=early)
            m.a_wo = m.sb("a_wo", [PART, 2 * NC * D], F32R, ctx=early)
            m.q_stack = m.sb("a_q_stack", [PART, 2 * NTT * HPI * PART], F32R, ctx=early)
            prepare(m, dram)
            with ExitStack() as stage:
                AttentionA(m, stage).build(dram)
        with ExitStack() as stage:
            AttentionB(m, stage).build(dram)
        weights.close()
        with ExitStack() as late:
            m.tag = ""
            m.rows = m.sb("rows2", [PART, NT, D], ctx=late)
            experts(m, dram)



_NAMES = {
    "x": "L0_attn_x", "a_wq": "L0_attn_Wq", "a_wk": "L0_attn_Wk", "a_wv": "L0_attn_Wv",
    "a_wo": "L0_attn_Wo", "ln1_w": "L0_ffn_ln1_w", "ln2_w": "L0_ffn_ln2_w", "b_wq": "L0_ffn_Wq",
    "b_wk": "L0_ffn_Wk", "b_wv": "L0_ffn_Wv", "b_wo": "L0_ffn_Wo", "wr": "L0_ffn_Wr",
    "expert_bias": "L0_ffn_expert_bias", "wg": "L0_ffn_Wg", "wu": "L0_ffn_Wu", "wd": "L0_ffn_Wd",
    "wsg": "L0_ffn_Wsg", "wsu": "L0_ffn_Wsu", "wsd": "L0_ffn_Wsd",
}


def rope_tables():
    freq = (np.float32(1.0) / np.float32(10000.0) ** (np.arange(0, DH, 2, dtype=np.float32) / np.float32(DH)))
    angle = (np.arange(SEQ, dtype=np.float32)[:, None] * freq[None, :]).astype(np.float64)
    cos, sin = np.cos(angle), np.sin(angle)
    tables = np.stack([np.concatenate([cos, cos], 1), np.concatenate([-sin, sin], 1)])
    both = np.concatenate([tables / np.sqrt(float(DH)), tables]).astype(np.float32)
    return np.ascontiguousarray(both.reshape(4, NTT, PART, DH).transpose(2, 0, 1, 3))


def kernel(**inputs):
    import concourse.bacc as bacc
    from concourse.bass_utils import run_bass_kernel_spmd

    nc = bacc.Bacc("TRN2", target_bir_lowering=False, num_devices=1)
    arrays, dram = {}, {}
    for name, source in _NAMES.items():
        a = np.ascontiguousarray(inputs[source])
        arrays["in_" + name] = a
        dram[name] = nc.dram_tensor("in_" + name, a.shape, F32, kind="ExternalInput").ap()
    arrays["rope"] = rope_tables()
    dram["rope"] = nc.dram_tensor("rope", arrays["rope"].shape, F32, kind="ExternalInput").ap()
    dram["gates"] = nc.dram_tensor("gates", (NE, NT * PART), F32, kind="Internal").ap()
    dram["out"] = nc.dram_tensor("out", (NB, SEQ, D), F32, kind="ExternalOutput").ap()
    program(nc, dram)
    result = run_bass_kernel_spmd(nc, [arrays], core_ids=[0])
    return result.results[0]["out"]
```

```python
from contextlib import ExitStack

import numpy as np
import concourse.bass as bass
from concourse import mybir

F32 = mybir.dt.float32
F32R = mybir.dt.float32r
BF16 = mybir.dt.bfloat16
ALU = mybir.AluOpType
ACT = mybir.ActivationFunctionType
AX = mybir.AxisListType.X

PART = 128
NB, SEQ, D = 4, 256, 256
NC = D // PART
NTT = SEQ // PART
NT = NB * NTT
SLOT = 2 * NC * SEQ
EPS = 1e-5
NEG = -1e30
HPI, PAIRS = 8, 4
PCOLS = PART + SEQ

A_HEADS, A_DH = 16, 16
A_ITS = NB * A_HEADS // HPI
A_QKV = 3 * HPI * A_DH
STACK = 64
KV, DH = 4, 128
B_ITS = NB * KV
B_QKV = HPI * DH + 2 * DH
B_WQ = NC * B_QKV
B_WO = HPI * D
B_W = B_WQ + B_WO
WQUART = B_W // 4

NE, TOPK, FF = 32, 8, 128
EW = 2 * NC * FF + D


def wait(eng, sem, value):
    if isinstance(value, int) and value <= 0:
        return
    eng.wait_ge(sem, value)


def three(nc, out, w_hi, w_lo, m_hi, m_lo, start, stop, skip=False):
    nc.tensor.matmul(out, w_lo, m_hi, start=start, stop=False, skip_group_check=skip)
    nc.tensor.matmul(out, w_hi, m_lo, start=False, stop=False, skip_group_check=skip)
    return nc.tensor.matmul(out, w_hi, m_hi, start=False, stop=stop, skip_group_check=skip)


class Machine:

    def __init__(self, nc, ctx):
        self.nc = nc
        self.ctx = ctx
        self.tag = ""
        self.tables = 0

    def load_table(self, act, function):
        out = self.spare[:, self.tables:self.tables + 1]
        self.tables += 1
        self.nc.scalar.activation(out, self.ident[:, 0:1], function)

    def sb(self, name, shape, dt=F32, ctx=None):
        return (ctx or self.ctx).enter_context(self.nc.sbuf_tensor(self.tag + name, shape, dt))

    def sem(self, name, ctx=None):
        return (ctx or self.ctx).enter_context(self.nc.semaphore(self.tag + name))




class Norm:

    LN = (0,)
    RMS = (2,)
    LN_AND_RMS = (0, 1)

    def __init__(self, m, ctx, name, kinds=LN):
        self.m, self.kinds = m, kinds
        K = len(kinds)
        self.stats = m.sb(name + "_stats", [PART, NT, 6], ctx=ctx)
        self.mv = m.sb(name + "_mv", [PART, NT, 2], ctx=ctx)
        self.den = m.sb(name + "_den", [PART, K, NT], ctx=ctx)
        self.factor = m.sb(name + "_factor", [PART, K, NT], ctx=ctx)
        self.shift = m.sb(name + "_shift", [PART, K, NT], ctx=ctx)
        self.step = m.sem(name + "_step", ctx=ctx)
        self.steps = 0
        self.var_ready = m.sem(name + "_var_ready", ctx=ctx)
        self.root_ready = m.sem(name + "_root_ready", ctx=ctx)
        self.ready = m.sem(name + "_ready", ctx=ctx)

    def link(self, instruction):
        self.steps += 1
        instruction.then_inc(self.step, 1)
        return self.steps

    def moments(self, dve, b, tile, arrived=None):
        nc = self.m.nc
        lo, hi = NTT * b, NTT * (b + 1)
        mean, var = self.mv[:, lo:hi, 0], self.mv[:, lo:hi, 1]
        for t in range(lo, hi):
            if arrived:
                arrived(t)
            at = self.link(nc.vector.bn_stats(self.stats[:, t, :], tile(t)))
        for t in range(lo, hi):
            dve.wait_ge(self.step, at - (hi - 1 - t))
            last = self.link(nc.vector.bn_aggr(self.mv[:, t, :], self.stats[:, t, :]))
        dve.wait_ge(self.step, last)
        for i, kind in enumerate(self.kinds):
            den = self.den[:, i, lo:hi]
            if kind == 0:
                last = nc.vector.tensor_scalar(den, var, EPS, None, ALU.add)
            elif kind == 1:
                last = nc.vector.tensor_scalar(den, var, 1.0 + EPS, EPS * EPS, ALU.mult, ALU.add)
            else:
                at = self.link(nc.vector.tensor_tensor(self.factor[:, i, lo:hi], mean, mean, ALU.mult))
                dve.wait_ge(self.step, at)
                last = nc.vector.scalar_tensor_tensor(out=den, in0=self.factor[:, i, lo:hi], scalar=EPS,
                                                      in1=var, op0=ALU.add, op1=ALU.add)
        last.then_inc(self.var_ready, 1)

    def roots(self, act, b):
        den = self.den[:, :, NTT * b:NTT * (b + 1)]
        act.wait_ge(self.var_ready, b + 1)
        self.m.nc.scalar.activation(den, den, ACT.Sqrt).then_inc(self.root_ready, 1)

    def factors(self, dve, b):
        nc = self.m.nc
        lo, hi = NTT * b, NTT * (b + 1)
        dve.wait_ge(self.root_ready, b + 1)
        at = self.link(nc.vector.reciprocal(self.factor[:, :, lo:hi], self.den[:, :, lo:hi]))
        dve.wait_ge(self.step, at)
        for i in range(len(self.kinds)):
            last = nc.vector.scalar_tensor_tensor(
                out=self.shift[:, i, lo:hi], in0=self.mv[:, lo:hi, 0], scalar=-1.0,
                in1=self.factor[:, i, lo:hi], op0=ALU.mult, op1=ALU.mult)
        last.then_inc(self.ready, 1)

    def apply(self, act, out, src, t, i=0):
        factor = self.factor[:, i, t:t + 1]
        if t % NTT == 0:
            act.wait_ge(self.ready, t // NTT + 1)
        if self.kinds[i] == 2:
            return self.m.nc.scalar.activation(out, src, ACT.Copy, scale=factor)
        return self.m.nc.scalar.activation(out, src, ACT.Identity, scale=factor,
                                           bias=self.shift[:, i, t:t + 1])


class Turn:

    def __init__(self, m, ctx, name, src, dst, banks=(0, 1, 2, 3), weight=None):
        self.m, self.src, self.dst, self.weight, self.banks = m, src, dst, weight, banks
        self.rows_ready = m.sem(name + "_rows_ready", ctx=ctx)
        self.turned = m.sem(name + "_turned", ctx=ctx)
        self.hi_done = m.sem(name + "_hi_done", ctx=ctx)
        self.lo_done = m.sem(name + "_lo_done", ctx=ctx)

    def bank(self, b):
        return self.m.banks[:, self.banks[b], :].rearrange("p (c t) -> p c t", c=NC)

    def slot(self, b, part, c):
        at = b * SLOT + part * NC * SEQ + c * SEQ
        return self.dst[:, at:at + SEQ]

    def tensor(self, pe, b):
        nc = self.m.nc
        pe.wait_ge(self.rows_ready, b + 1)
        for t in range(NTT):
            for c in range(NC):
                last = nc.tensor.transpose(self.bank(b)[:, c, t * PART:(t + 1) * PART],
                                           self.src[:, NTT * b + t, c * PART:(c + 1) * PART],
                                           self.m.ident[:])
        last.then_inc(self.turned, 1)

    def scalar(self, act, b):
        nc = self.m.nc
        act.wait_ge(self.turned, b + 1)
        for c in range(NC):
            scale = 1.0 if self.weight is None else self.weight[:, c:c + 1]
            last = nc.scalar.activation(self.slot(b, 0, c), self.bank(b)[:, c, :], ACT.Copy,
                                        scale=scale)
        last.then_inc(self.hi_done, 1)

    def vector(self, dve, b):
        nc = self.m.nc
        dve.wait_ge(self.hi_done, b + 1)
        for c in range(NC):
            scale = 1.0 if self.weight is None else self.weight[:, c:c + 1]
            last = nc.vector.scalar_tensor_tensor(
                out=self.slot(b, 1, c), in0=self.bank(b)[:, c, :], scalar=scale,
                in1=self.slot(b, 0, c).bitcast(F32), op0=ALU.mult, op1=ALU.subtract)
        last.then_inc(self.lo_done, 1)


def pipeline(stages, between=None):
    for s in range(NB + max(lag for lag, _ in stages)):
        for lag, stage in stages:
            if 0 <= s - lag < NB:
                stage(s - lag)
        if between:
            between(s)




def prepare(m, dram):
    nc = m.nc
    m.tag = "pre_"
    with ExitStack() as ctx:
        w_nat = m.sb("w_nat", [PART, 4, NC, D], ctx=ctx)
        norm = Norm(m, ctx, "ln_x")
        turn = Turn(m, ctx, "x", m.rows, m.act_t)
        sem = lambda name: m.sem(name, ctx=ctx)
        x_loaded = [sem(f"x_loaded{t}") for t in range(NT)]
        w_loaded = [sem(f"w_loaded{i}") for i in range(4)]
        tables_loaded = sem("tables_loaded")
        wr_loaded, wr_hi = sem("wr_loaded"), sem("wr_hi")
        zeroed, const_ready = sem("zeroed"), sem("const_ready")
        w_turned, w_hi = sem("w_turned"), sem("w_hi")
        block = ctx.enter_context(nc.Block())

        def w_bank(i):
            return m.banks[:, 4 + i, :].rearrange("p (c n) -> p c n", c=NC)

        def w_slot(i, part):
            if i == 3:
                at = part * NC * D
                return m.a_wo[:, at:at + NC * D].rearrange("p (c n) -> p c n", c=NC)
            at = part * 2 * NC * A_QKV
            half = m.a_wqkv[:, at:at + 2 * NC * A_QKV]
            return half.rearrange("p (g c n) -> p c g n", g=2, c=NC)[:, :, :, i * PART:(i + 1) * PART]

        @block.sync
        def _(sp):
            x = dram["x"].rearrange("b (t p) d -> p (b t) d", p=PART)
            for t in range(NT):
                sp.dma_start(m.x[:, t, :], x[:, t, :]).then_inc(x_loaded[t], 16)
            sp.dma_start(m.rope[:], dram["rope"]).then_inc(tables_loaded, 16)
            for i, name in enumerate(("ln1_w", "ln2_w")):
                sp.dma_start(m.lnw[:, i, :], dram[name].rearrange("(c p) -> p c", p=PART),
                             allow_slow_non_contiguous=True).then_inc(tables_loaded, 16)
            sp.dma_start(m.wr_raw[:], dram["wr"].rearrange("(c p) e -> p c e", p=PART)).then_inc(wr_loaded, 16)
            sp.dma_start(m.bias[:], dram["expert_bias"].rearrange("(o e) -> o e", o=1)
                         .to_broadcast([PART, NE])).then_inc(tables_loaded, 16)
            for dst, src in group_weights(m, dram, 0):
                sp.dma_start(dst, src).then_inc(tables_loaded, 16)
            sp.wait_ge(tables_loaded, 16 * (4 + W_DMAS))

        @block.gpsimd
        def _(pool):
            for buf in (m.ident, m.ident16, m.mask):
                nc.gpsimd.memset(buf[:], 0.0).then_inc(zeroed, 1)
            pool.wait_ge(zeroed, 3)
            for buf in (m.ident, m.ident16):
                nc.gpsimd.affine_select(out=buf[:], in_=buf[:], compare_op=ALU.not_equal, fill=1.0,
                                        base=0, pattern=[[-1, PART]],
                                        channel_multiplier=1).then_inc(const_ready, 1)
            nc.gpsimd.affine_select(out=m.mask[:], in_=m.mask[:], compare_op=ALU.is_ge, fill=NEG,
                                    base=0, pattern=[[-1, PART]],
                                    channel_multiplier=1).then_inc(const_ready, 1)
            nc.gpsimd.memset(m.b_w[:, 2 * B_W:4 * B_W].bitcast(F32), 0.0)
            nc.gpsimd.memset(m.q_stack[:].bitcast(F32), 0.0)

        def pe_weights(pe, i):
            if i == 0:
                pe.wait_ge(const_ready, 3)
            pe.wait_ge(w_loaded[i], 16)
            for r in range(NC):
                for c in range(NC):
                    last = nc.tensor.transpose(w_bank(i)[:, c, r * PART:(r + 1) * PART],
                                               w_nat[:, i, r, c * PART:(c + 1) * PART], m.ident[:])
            last.then_inc(w_turned, 1)

        @block.tensor
        def _(pe):
            for i in range(4):
                pe_weights(pe, i)
            for b in range(NB):
                turn.tensor(pe, b)

        def w_views(i, part):
            src = w_bank(i)
            if i < 3:
                src = src.rearrange("p c (g n) -> p c g n", g=2)
            return w_slot(i, part), src

        w_scale = [float(A_DH) ** -0.5, 1.0, 1.0, 1.0]

        def act_weights(act, i):
            act.wait_ge(w_turned, i + 1)
            dst, src = w_views(i, 0)
            nc.scalar.activation(dst, src, ACT.Copy, scale=w_scale[i]).then_inc(w_hi, 1)

        def act_rows(act, b):
            for t in range(NTT * b, NTT * (b + 1)):
                last = norm.apply(act, m.rows[:, t, :], m.x[:, t, :], t)
            last.then_inc(turn.rows_ready, 1)

        @block.scalar
        def _(act):
            for i, name in enumerate(("a_wq", "a_wk", "a_wv", "a_wo")):
                act.dma_start(w_nat[:, i, :, :], dram[name].rearrange("(r p) n -> p r n", p=PART),
                              ).then_inc(w_loaded[i], 16)
            roots, rows = (lambda b: norm.roots(act, b)), (lambda b: act_rows(act, b))
            weights, turns = (lambda i: act_weights(act, i)), (lambda b: turn.scalar(act, b))
            act.wait_ge(const_ready, 3)
            m.load_table(act, ACT.Sqrt)
            for stage, n in ((weights, 0), (roots, 0), (weights, 1), (rows, 0), (roots, 1), (rows, 1),
                             (roots, 2), (turns, 0), (rows, 2), (roots, 3), (weights, 2), (turns, 1),
                             (rows, 3), (weights, 3), (turns, 2), (turns, 3)):
                stage(n)
            act.wait_ge(wr_loaded, 16)
            nc.scalar.activation(m.wr[:, 0, :, :], m.wr_raw[:], ACT.Copy).then_inc(wr_hi, 1)

        def dve_weights(dve, i):
            dve.wait_ge(w_hi, i + 1)
            dst, src = w_views(i, 1)
            hi, _ = w_views(i, 0)
            for c in range(NC):
                nc.vector.scalar_tensor_tensor(
                    out=dst[:, c], in0=src[:, c], scalar=w_scale[i], in1=hi[:, c].bitcast(F32),
                    op0=ALU.mult, op1=ALU.subtract)

        @block.vector
        def _(dve):
            arrived = lambda t: dve.wait_ge(x_loaded[t], 16)
            moments = lambda b: norm.moments(dve, b, lambda t: m.x[:, t, :], arrived)
            factors, turns = (lambda b: norm.factors(dve, b)), (lambda b: turn.vector(dve, b))
            weights = lambda i: dve_weights(dve, i)
            for stage, n in ((moments, 0), (moments, 1), (factors, 0), (moments, 2), (factors, 1),
                             (moments, 3), (factors, 2), (factors, 3), (weights, 0), (turns, 0),
                             (weights, 1), (turns, 1), (weights, 2), (turns, 2), (weights, 3), (turns, 3)):
                stage(n)
            dve.wait_ge(wr_hi, 1)
            nc.vector.tensor_tensor(m.wr[:, 1, :, :], m.wr_raw[:], m.wr[:, 0, :, :].bitcast(F32),
                                    ALU.subtract)




class Attention:

    DRAIN = 5

    ITS = UNITS = 0
    UNROLL = 1
    LATE_NEXT = False
    POOL_NORMALISES = False

    def __init__(self, m, ctx, tag):
        self.m, self.ctx = m, ctx
        m.tag = tag
        sb, sem = self.sb, self.sem
        self.src_t = sb("src_t", [PART, SLOT], F32R)
        self.qt = sb("qt", [PART, 2, 2, 2 * SEQ], F32R)
        self.prob = sb("prob", [PART, PAIRS, 2, PCOLS])
        self.prob_t = sb("prob_t", [PART, 2, 2, 2 * PCOLS], F32R)
        self.negmax = sb("negmax", [PART, 2, 2, NTT])
        self.sums = sb("sums", [PART, PAIRS, 2 * NTT])
        self.rsum = sb("rsum", [PART, PAIRS, 2 * NTT])
        self.src_loaded = sem("src_loaded")
        self.unit_full = sem("unit_full")
        self.unit_free = sem("unit_free")
        self.qt_full = sem("qt_full")
        self.qt_hi = sem("qt_hi")
        self.qt_ready = sem("qt_ready")
        self.s_full = sem("s_full")
        self.max_ready = sem("max_ready")
        self.exp_done = sem("exp_done")
        self.rsum_ready = sem("rsum_ready")
        self.prob_ready = sem("prob_ready")
        self.pt_full = sem("pt_full")
        self.pt_hi = sem("pt_hi")
        self.pt_ready = sem("pt_ready")
        self.pv_done = sem("pv_done")
        self.o_hi = sem("o_hi")
        self.o_ready = sem("o_ready")
        self.w_done = sem("w_done")
        self.y_added = sem("y_added")
        self.v_raw = sem("v_raw")
        self.v_hi = sem("v_hi")
        self.v_ready = sem("v_ready")
        self.kt_ready = sem("kt_ready")

    def sb(self, name, shape, dt=F32):
        return self.m.sb(name, shape, dt, ctx=self.ctx)

    def sem(self, name):
        return self.m.sem(name, ctx=self.ctx)


    COPIED = 3

    def src(self, it, part, c, t):
        at = part * NC * SEQ + c * SEQ + t * PART
        if isinstance(it, int) and it < self.COPIED:
            at += self.batch(it) * SLOT
            return self.m.act_t[:, at:at + PART]
        return self.src_t[:, at:at + PART]

    def wait_src(self, pe, it):
        if not (isinstance(it, int) and it < self.COPIED):
            pe.wait_ge(self.src_loaded, 16 * (it - self.COPIED + 1))

    def unit_bank(self, it, u):
        m = self.m
        return (m.pj_ps, m.o_ps, m.y_ps)[u % 3] if isinstance(it, int) and it == 0 else m.pj_ps

    def bank_free(self, it, n):
        return n - 2 if isinstance(it, int) and it == 0 else n

    def pe_scores(self, pe, it, p, P):
        nc, m = self.m.nc, self.m
        wait(pe, self.qt_ready, P + 1)
        self.pe_wait_keys(pe, it, p)
        for h in range(2):
            wait(pe, self.exp_done, 2 * P - 1 + h)
            for t in range(NTT):
                lo, width = t * PART, (t + 1) * PART
                out = m.s_ps[:, h, lo:lo + width]
                diagonal = m.s_ps[:, h, lo + width - PART:lo + width]
                self.pe_score(out, it, p, h, t, width)
                last = nc.tensor.matmul(diagonal, m.ident16[:], m.mask[:], start=False, stop=True)
            last.then_inc(self.s_full, 1)

    def pe_prob_t(self, pe, p, P):
        nc, m = self.m.nc, self.m
        wait(pe, self.prob_ready, P + 1)
        wait(pe, self.pt_ready, P)
        for h in range(2):
            for at, col in ((h * SEQ, 0), (h * SEQ + PART, PART), (2 * SEQ + h * PART, 2 * PART)):
                last = nc.tensor.transpose(m.pt_ps[:, at:at + PART],
                                           self.prob[:, p, h, col:col + PART], m.ident[:])
        last.then_inc(self.pt_full, 1)

    def stage(self, it, p, lag):
        P = PAIRS * it + p - lag
        if isinstance(P, int) and not 0 <= P < PAIRS * self.ITS:
            return None
        return it + (p - lag) // PAIRS, (p - lag) % PAIRS, P

    def early_unit(self, p, units):
        return self.schedule[p][0] if units and self.schedule[p] else None

    def late_unit(self, it, p, units):
        if p == 0:
            known = isinstance(it, int) and not 0 < it < self.ITS
            return None if known or len(self.schedule[-1]) < 2 else (it, self.schedule[-1][1])
        return (it + 1, self.schedule[p - 1][1]) if units and len(self.schedule[p - 1]) > 1 else None

    def slot_pe(self, pe, it, p, units=True):
        if now := self.stage(it, p, 0):
            self.pe_scores(pe, *now)
        if self.LATE_NEXT and (late := self.late_unit(it, p, units)):
            self.pe_unit(pe, *late)
        if ahead := self.stage(it, p, -1):
            self.pe_queries_t(pe, *ahead)
        if out := self.stage(it, p, 5):
            self.pe_project(pe, *out)
        if values := self.stage(it, p, 4):
            self.pe_values(pe, *values)
        u = self.early_unit(p, units)
        if u is not None:
            self.pe_unit(pe, it + 1, u)
        if prob := self.stage(it, p, 2):
            self.pe_prob_t(pe, *prob[1:])
        if not self.LATE_NEXT and u is not None and len(self.schedule[p]) > 1:
            self.pe_unit(pe, it + 1, self.schedule[p][1])


    def act_exp(self, act, p, P):
        nc, m = self.m.nc, self.m
        wait(act, self.pt_full, P - PAIRS + 1)
        for h in range(2):
            wait(act, self.max_ready, 2 * P + 1 + h)
            for t in range(NTT):
                lo, width = t * PART, (t + 1) * PART
                k = 2 * h + t
                last = nc.scalar.activation(self.prob[:, p, h, lo:lo + width],
                                            m.s_ps[:, h, lo:lo + width], ACT.Exp,
                                            bias=self.negmax[:, p % 2, t, h:h + 1],
                                            accum_out=self.sums[:, p, k:k + 1])
            last.then_inc(self.exp_done, 1)

    def act_prob_t(self, act, p, P):
        wait(act, self.pt_full, P + 1)
        wait(act, self.pv_done, P - 1)
        self.m.nc.scalar.activation(self.prob_t[:, p % 2, 0, :], self.m.pt_ps[:, 0:2 * PCOLS],
                                    ACT.Copy).then_inc(self.pt_hi, 1)

    def slot_act(self, act, it, p, units=True):
        if prob := self.stage(it, p, 3):
            self.act_prob_t(act, *prob[1:])
        if late := self.late_unit(it, p, units):
            self.act_unit(act, *late)
        if ahead := self.stage(it, p, -1):
            self.act_queries(act, *ahead)
        if now := self.stage(it, p, 0):
            self.act_exp(act, *now[1:])
        if out := self.stage(it, p, 4):
            self.act_outputs(act, *out)
        u = self.early_unit(p, units)
        if u is not None:
            self.act_unit(act, it + 1, u)
        if now and p == PAIRS - 1:
            self.act_values(act, it)
        if now and p == PAIRS - 2:
            self.act_weights(act, it)


    def dve_max(self, dve, p, P):
        nc, m = self.m.nc, self.m
        wait(dve, self.exp_done, 2 * P - 2)
        for h in range(2):
            wait(dve, self.s_full, 2 * P + 1 + h)
            for t in range(NTT):
                lo, width = t * PART, (t + 1) * PART
                last = nc.vector.tensor_reduce(self.negmax[:, p % 2, t, h:h + 1],
                                               m.s_ps[:, h, lo:lo + width], AX, ALU.max, negate=True)
            last.then_inc(self.max_ready, 1)

    def dve_normalise(self, dve, p, P):
        nc = self.m.nc
        wait(dve, self.exp_done, 2 * P + 2)
        nc.vector.reciprocal(self.rsum[:, p, :], self.sums[:, p, :]).then_inc(self.rsum_ready, 1)
        if self.POOL_NORMALISES:
            return
        wait(dve, self.rsum_ready, P + 1)
        for h in range(2):
            for t in range(NTT):
                lo, width = t * PART, (t + 1) * PART
                k = 2 * h + t
                row = self.prob[:, p, h, lo:lo + width]
                last = nc.vector.tensor_scalar(row, row, self.rsum[:, p, k:k + 1], None, ALU.mult)
        last.then_inc(self.prob_ready, 1)

    def pool_normalise(self, pool, p, P):
        wait(pool, self.rsum_ready, P + 1)
        rsum = self.rsum[:, p, :].rearrange("p (h t) -> p h t", h=2)
        for t in range(NTT):
            lo, width = t * PART, (t + 1) * PART
            rows = self.prob[:, p, :, lo:lo + width]
            last = self.m.nc.gpsimd.tensor_tensor(
                rows, rows, rsum[:, :, t:t + 1].to_broadcast([PART, 2, width]), ALU.mult)
        last.then_inc(self.prob_ready, 1)

    def dve_prob_t(self, dve, p, P):
        wait(dve, self.pt_hi, P + 1)
        self.m.nc.vector.tensor_tensor(self.prob_t[:, p % 2, 1, :], self.m.pt_ps[:, 0:2 * PCOLS],
                                       self.prob_t[:, p % 2, 0, :].bitcast(F32),
                                       ALU.subtract).then_inc(self.pt_ready, 1)

    def dve_add(self, dve, it):
        into = self.m.acc[:, bass.ds(self.batch(it) * (NTT * D), NTT * D)]
        wait(dve, self.w_done, self.projected(it))
        wait(dve, self.y_added, it + 1)
        self.m.nc.vector.tensor_tensor(into, self.m.y_ps[:], into, ALU.add).then_inc(self.y_added, 1)

    def slot_dve(self, dve, it, p, units=True):
        if now := self.stage(it, p, 0):
            self.dve_max(dve, *now[1:])
        if ahead := self.stage(it, p, -1):
            self.dve_queries(dve, *ahead)
        late = self.late_unit(it, p, units)
        if late and self.LATE_NEXT:
            self.dve_unit(dve, *late)
        if prob := self.stage(it, p, 3):
            self.dve_prob_t(dve, *prob[1:])
        if late and not self.LATE_NEXT:
            self.dve_unit(dve, *late)
        if before := self.stage(it, p, 1):
            self.dve_normalise(dve, *before[1:])
        if out := self.stage(it, p, 4):
            self.dve_outputs(dve, *out)
        u = self.early_unit(p, units)
        if u is not None:
            self.dve_unit(dve, it + 1, u)
        if now and p == PAIRS - 1:
            self.dve_values(dve, it)
        if p == 0 and not (isinstance(it, int) and it < 2):
            self.dve_add(dve, it - 2)


    def run(self, eng, slot, middles, after=None):
        for it in range(2):
            for p in range(PAIRS):
                slot(eng, it, p)
        for first, last in middles:
            self.splitting = last <= self.ITS - NB
            with eng.Fori(first // self.UNROLL, last // self.UNROLL) as step:
                for k in range(self.UNROLL):
                    self.parity = k
                    for p in range(PAIRS):
                        slot(eng, step * self.UNROLL + k, p)
        for it in range(middles[-1][1], self.ITS):
            for p in range(PAIRS):
                slot(eng, it, p, units=it < self.ITS - 1)
        for k in range(self.DRAIN):
            P = PAIRS * self.ITS + k
            slot(eng, P // PAIRS, P % PAIRS, units=False)
            if after:
                after(k)


class AttentionA(Attention):

    ITS, UNITS = A_ITS, 4
    LATE_NEXT = True
    UNROLL = 2
    POOL_NORMALISES = True
    schedule = ((), (0,), (1,), (2, 3))

    def __init__(self, m, ctx):
        super().__init__(m, ctx, "a_")
        sb, sem = self.sb, self.sem
        rest = m.b_w[:, 2 * B_W:4 * B_W]

        def place(n, pattern, **sizes):
            nonlocal rest
            rest, taken = rest[:, n:], rest[:, 0:n]
            return taken.rearrange(pattern, **sizes)

        self.v = place(2 * NTT * HPI * PART, "p (a t h n) -> p a t h n", a=2, t=NTT, h=HPI)
        self.k_stack = place(NTT * HPI * STACK, "p (t n) -> p t n", t=NTT)
        self.kt = place(2 * PAIRS * SEQ, "p n -> p n")
        self.v_row = sb("v_row", [PART, 2 * NTT * HPI * A_DH])
        self.ot = sb("ot", [PART, 2, SEQ], F32R)
        self.w_raw_hi = sem("w_raw_hi")
        self.stack_hi = sem("stack_hi")
        self.stack_ready = sem("stack_ready")

    def q_stack(self, it, t, at, n):
        width = HPI * PART
        return self.m.q_stack[:, bass.ds((it % 2) * (NTT * width) + (t * width + at), n)]

    def slot_pool(self, pool, it, p, units=True):
        if before := self.stage(it, p, 1):
            self.pool_normalise(pool, *before[1:])

    @staticmethod
    def batch(it):
        return it // 2

    @staticmethod
    def projected(it):
        return it + 1

    def weights(self, part, c, group):
        at = part * 2 * NC * A_QKV + c * A_QKV
        return self.m.a_wqkv[:, bass.ds(group * (NC * A_QKV) + at, A_QKV)]

    def pe_unit(self, pe, it, u):
        nc, m = self.m.nc, self.m
        n = self.UNITS * it + u
        if u < NTT:
            self.wait_src(pe, it)
            wait(pe, self.unit_free, self.bank_free(it, n))
            for c in range(NC):
                last = three(nc, self.unit_bank(it, u)[:, 0:A_QKV], self.src(it, 0, c, u), self.src(it, 1, c, u),
                             self.weights(0, c, it % 2), self.weights(1, c, it % 2),
                             c == 0, c == NC - 1)
        else:
            wait(pe, self.stack_ready, NTT * (it + 1))
            wait(pe, self.unit_free, self.bank_free(it, n))
            for q in range(2):
                pair = 2 * (u - NTT) + q
                for t in range(NTT):
                    at = q * SEQ + t * PART
                    last = nc.tensor.transpose(
                        self.unit_bank(it, u)[:, at:at + PART],
                        self.k_stack[:, t, pair * PART:(pair + 1) * PART].bitcast(F32), m.ident[:])
        last.then_inc(self.unit_full, 1)

    def pe_queries_t(self, pe, it, p, P):
        nc, m = self.m.nc, self.m
        wait(pe, self.stack_ready, NTT * (it + 1))
        wait(pe, self.qt_ready, P)
        par = it % 2 if isinstance(it, int) else (self.parity + (p == 0)) % 2
        for h in range(2):
            at = (2 * p + h) * PART - (STACK if h else 0)
            for t in range(NTT):
                last = nc.tensor.transpose(m.qt_ps[:, h * SEQ + t * PART:h * SEQ + (t + 1) * PART],
                                           self.q_stack(par, t, at, PART).bitcast(F32), m.ident[:])
        last.then_inc(self.qt_full, 1)

    def pe_wait_keys(self, pe, it, p):
        if p % 2 == 0:
            wait(pe, self.kt_ready, 2 * it + p // 2 + 1)

    def keys(self, it, p, n):
        return self.kt[:, bass.ds((it % 2) * (PAIRS * SEQ) + p * SEQ, n)]

    def pe_score(self, out, it, p, h, t, width):
        at = h * SEQ + t * PART
        self.m.nc.tensor.matmul(out, self.qt[:, p % 2, 0, at:at + PART], self.keys(it, p, width),
                                start=True, stop=False)

    def pe_values(self, pe, it, p, P):
        nc, m = self.m.nc, self.m
        wait(pe, self.pt_ready, P + 1)
        if p == 0:
            wait(pe, self.v_ready, it + 1)
            wait(pe, self.o_ready, it)
        par = p % 2
        for h in range(2):
            head = 2 * p + h
            for k in range(NTT):
                width = SEQ - k * PART
                at = h * SEQ if k == 0 else 2 * SEQ + h * PART
                last = three(nc, m.o_ps[:, k * PART:SEQ],
                             self.v[:, 0, k, head, :], self.v[:, 1, k, head, :],
                             self.prob_t[:, par, 0, at:at + width], self.prob_t[:, par, 1, at:at + width],
                             head == 0 and k == 0, head == HPI - 1 and k == NTT - 1)
        last.then_inc(self.pv_done, 1)

    def pe_project(self, pe, it, p, P):
        if p != PAIRS - 1:
            return
        nc, m = self.m.nc, self.m
        wait(pe, self.o_ready, it + 1)
        wait(pe, self.y_added, it + 1)
        at = (it % 2) * D
        for t in range(NTT):
            last = three(nc, m.y_ps[:, t * D:(t + 1) * D],
                         self.ot[:, 0, t * PART:(t + 1) * PART], self.ot[:, 1, t * PART:(t + 1) * PART],
                         m.a_wo[:, bass.ds(at, D)], m.a_wo[:, bass.ds(at + NC * D, D)], True, True)
        last.then_inc(self.w_done, 1)

    def act_outputs(self, act, it, p, P):
        if p != PAIRS - 1:
            return
        wait(act, self.pv_done, P + 1)
        wait(act, self.w_done, it)
        self.m.nc.scalar.activation(self.ot[:, 0, :], self.m.o_ps[:, 0:SEQ],
                                    ACT.Copy).then_inc(self.o_hi, 1)

    def dve_outputs(self, dve, it, p, P):
        if p != PAIRS - 1:
            return
        wait(dve, self.o_hi, it + 1)
        self.m.nc.vector.tensor_tensor(self.ot[:, 1, :], self.m.o_ps[:, 0:SEQ],
                                       self.ot[:, 0, :].bitcast(F32),
                                       ALU.subtract).then_inc(self.o_ready, 1)

    def values(self, it, t):
        n = HPI * A_DH
        return self.v_row[:, bass.ds((it % 2) * (NTT * n) + t * n, n)]

    def v_view(self, part, t):
        base = self.v[:, part, t, 0, 0:A_DH]
        return bass.AP(tensor=base.tensor, offset=base.offset,
                       ap=[list(base.ap[0]), [PART + A_DH, HPI], [1, A_DH]])

    def act_values(self, act, it):
        nc = self.m.nc
        wait(act, self.v_raw, NTT * (it + 1))
        wait(act, self.pv_done, PAIRS * it)
        for t in range(NTT):
            row = self.values(it, t).rearrange("p (h d) -> p h d", h=HPI)
            last = nc.scalar.activation(self.v_view(0, t), row, ACT.Copy)
        last.then_inc(self.v_hi, 1)

    def dve_values(self, dve, it):
        nc = self.m.nc
        wait(dve, self.v_hi, it + 1)
        for t in range(NTT):
            row = self.values(it, t).rearrange("p (h d) -> p h d", h=HPI)
            last = nc.vector.tensor_tensor(self.v_view(1, t), row, self.v_view(0, t).bitcast(F32),
                                           ALU.subtract)
        last.then_inc(self.v_ready, 1)

    def act_queries(self, act, it, p, P):
        wait(act, self.qt_full, P + 1)
        wait(act, self.s_full, 2 * P - 2)
        self.m.nc.scalar.activation(self.qt[:, p % 2, 0, :], self.m.qt_ps[:],
                                    ACT.Copy).then_inc(self.qt_ready, 1)

    def dve_queries(self, dve, it, p, P):
        pass

    def act_weights(self, act, it):
        pass

    def stack_views(self, it, u):
        heads = lambda x, n: x.rearrange("p (h n) -> p h n", h=n)
        pj = self.unit_bank(it, u)
        q, k, v = (pj[:, i * PART:(i + 1) * PART] for i in range(3))
        qs = heads(self.q_stack(it, u, 0, HPI * PART), HPI)[:, :, 0:STACK].rearrange("p h (s d) -> p h s d", d=A_DH)
        ks = heads(self.k_stack[:, u, :], HPI).rearrange("p h (s d) -> p h s d", d=A_DH)
        return heads(q, HPI), heads(k, HPI), v, qs, ks

    def act_unit(self, act, it, u):
        nc, m = self.m.nc, self.m
        n = self.UNITS * it + u
        wait(act, self.unit_full, n + 1)
        if u < NTT:
            wait(act, self.qt_full, PAIRS * (it - 1))
            wait(act, self.unit_free, self.UNITS * it)
            q, k, _, qs, ks = self.stack_views(it, u)
            for src, dst in ((q, qs[:, :, 0:2, :]), (k, ks[:, :, 0:3:2, :])):
                twice = src.unsqueeze(2).to_broadcast([PART, HPI, 2, A_DH])
                last = nc.scalar.activation(dst, twice, ACT.Copy)
            last.then_inc(self.stack_hi, 1)
        else:
            wait(act, self.s_full, 2 * PAIRS * (it - 1))
            nc.scalar.activation(self.keys(it, 2 * (u - NTT), 2 * SEQ), self.unit_bank(it, u)[:],
                                 ACT.Copy).then_inc(self.kt_ready, 1)
            act.wait_ge(self.kt_ready, 2 * it + u - NTT + 1)
            act.sem_inc(self.unit_free, 1)

    def dve_unit(self, dve, it, u):
        if u >= NTT:
            return
        nc = self.m.nc
        wait(dve, self.stack_hi, NTT * it + u + 1)
        q, k, v, qs, ks = self.stack_views(it, u)
        nc.vector.tensor_tensor(qs[:, :, 2, :], q, qs[:, :, 0, :].bitcast(F32), ALU.subtract)
        nc.vector.tensor_tensor(ks[:, :, 1, :], k, ks[:, :, 0, :].bitcast(F32),
                                ALU.subtract).then_inc(self.stack_ready, 1)
        wait(dve, self.v_ready, it - 1)
        nc.vector.tensor_copy(self.values(it, u), v).then_inc(self.v_raw, 1)
        dve.wait_ge(self.v_raw, NTT * it + u + 1)
        dve.sem_inc(self.unit_free, 1)

    def build(self, dram):
        nc, m = self.m.nc, self.m
        middles = ((2, self.ITS - 2),)
        block = self.ctx.enter_context(nc.Block())

        @block.sync
        def _(sp):
            def load(it, b):
                if not isinstance(it, int):
                    sp.wait_ge(self.unit_full, self.UNITS * (it - 1) + NTT)
                sp.dma_start(self.src_t[:].bitcast(F32), self.m.act_t[:, bass.ds(b * SLOT, SLOT)].bitcast(F32),
                             ).then_inc(self.src_loaded, 16)
            load(self.COPIED, 1)
            with sp.Fori(2, NB) as b:
                load(2 * b, b)
                load(2 * b + 1, b)
            sp.wait_ge(self.src_loaded, 16 * (self.ITS - self.COPIED))

        @block.gpsimd
        def _(pool):
            nc.gpsimd.memset(m.acc[:], 0.0).then_inc(self.y_added, 1)
            for q in range(4):
                pool.wait_ge(self.w_raw_hi, q + 1)
                at = slice(q * WQUART, (q + 1) * WQUART)
                nc.gpsimd.tensor_tensor(m.b_w[:, B_W:2 * B_W][:, at], m.b_w_raw[:, at],
                                        m.b_w[:, at].bitcast(F32), ALU.subtract)
            self.run(pool, self.slot_pool, middles)

        @block.tensor
        def _(pe):
            for u in range(NTT):
                self.pe_unit(pe, 0, u)
            self.pe_queries_t(pe, 0, 0, 0)
            for u in range(NTT, self.UNITS):
                self.pe_unit(pe, 0, u)
            self.run(pe, self.slot_pe, middles)

        @block.scalar
        def _(act):
            def split_weights(q):
                at = slice(q * WQUART, (q + 1) * WQUART)
                nc.scalar.activation(m.b_w[:, at], m.b_w_raw[:, at], ACT.Copy).then_inc(self.w_raw_hi, 1)
            m.load_table(act, ACT.Exp)
            split_weights(0)
            self.act_unit(act, 0, 0)
            split_weights(1)
            self.act_unit(act, 0, 1)
            self.act_queries(act, 0, 0, 0)
            for u in range(NTT, self.UNITS):
                self.act_unit(act, 0, u)
            split_weights(2)
            split_weights(3)
            self.run(act, self.slot_act, middles)
            for b in range(NB - 1):
                m.norm_a.roots(act, b)

        @block.vector
        def _(dve):
            for u in range(self.UNITS):
                self.dve_unit(dve, 0, u)
            acc = m.acc[:].rearrange("p (t d) -> p t d", t=NT)

            def arrived(t):
                dve.wait_ge(self.y_added, 2 * (t // NTT + 1) + 1)

            def moments(k):
                if k < NB - 1:
                    m.norm_a.moments(dve, k, lambda t: acc[:, t, :], arrived)

            self.run(dve, self.slot_dve, middles, moments)
            for b in range(NB - 1):
                m.norm_a.factors(dve, b)


W_DMAS = 4


def group_weights(m, dram, g):
    q = HPI * DH
    raw_in = m.b_w_raw[:, 0:B_WQ].rearrange("p (c n) -> p c n", c=NC)
    raw_out = m.b_w_raw[:, B_WQ:B_W].rearrange("p (h n) -> p h n", h=HPI)
    wq, wk, wv = (dram[n].rearrange("(c p) n -> p c n", p=PART) for n in ("b_wq", "b_wk", "b_wv"))
    wo = dram["b_wo"].rearrange("(h p) n -> p h n", p=DH)
    return [(raw_in[:, :, 0:q], wq[:, :, bass.ds(g * q, q)]),
            (raw_in[:, :, q:q + DH], wk[:, :, bass.ds(g * DH, DH)]),
            (raw_in[:, :, q + DH:q + 2 * DH], wv[:, :, bass.ds(g * DH, DH)]),
            (raw_out, wo[:, bass.ds(g * HPI, HPI), :])]


class AttentionB(Attention):

    ITS, UNITS = B_ITS, 7
    KV0, KV1, Q00, Q01, KT, Q10, Q11 = range(7)
    schedule = ((KV0, KV1), (Q00, Q01), (KT,), (Q10, Q11))
    Q_OF = {Q00: (0, 0), Q01: (0, 1), Q10: (1, 0), Q11: (1, 1)}
    KV_OF = {KV0: 0, KV1: 1}
    ROT = {KV0: 0, KV1: 1, Q00: 2, Q01: 3, Q10: 4, Q11: 5}
    NROT = len(ROT)

    def __init__(self, m, ctx):
        super().__init__(m, ctx, "b_")
        sb, sem = self.sb, self.sem
        self.w, self.w_raw = m.b_w, m.b_w_raw
        self.raw = sb("raw", [PART, 2, 4 * DH])
        self.cos_part = sb("cos_part", [PART, 2, 4 * DH])
        self.sin_part = sb("sin_part", [PART, 2, 4 * DH])
        self.q_row = sb("q_row", [PART, 2, NTT, 4 * DH])
        self.k_row = sb("k_row", [PART, NTT, DH])
        self.v_row = sb("v_row", [PART, 2 * NTT * DH])
        self.kt = sb("kt", [PART, 2 * 2 * SEQ], F32R)
        self.v = sb("v", [PART, 2, NTT, DH], F32R)
        self.ot = sb("ot", [PART, 2, 2, 2 * SEQ], F32R)
        self.w_loaded = sem("w_loaded")
        self.w_hi = sem("w_hi")
        self.w_ready = sem("w_ready")
        self.raw_ready = sem("raw_ready")
        self.cos_ready = sem("cos_ready")
        self.sin_ready = sem("sin_ready")
        self.rotated = sem("rotated")
        self.kt_hi = sem("kt_hi")
        rows = self.prob[:].rearrange("p a h n -> p (a h n)")[:, 0:NT * D]
        self.join = Join(m, ctx, rows.rearrange("p (t d) -> p t d", t=NT))
        rows = self.q_row[:].rearrange("p a t n -> p (a t n)").rearrange("p (t d) -> p t d", t=NT)
        self.norm2 = Norm(m, ctx, "rms", Norm.RMS)
        self.turn2 = Turn(m, ctx, "h2", rows, m.act_t, banks=(0, 1, 4, 5), weight=m.lnw[:, 1, :])
        self.e_loaded, self.e_hi = sem("e_loaded"), sem("e_hi")

    BEHIND_STEP = {3: (KV0, KV1), 4: (Q00,), 5: (Q01, KT)}
    BEHIND_ALL = (Q10, Q11)

    @staticmethod
    def batch(it):
        return it % NB

    @staticmethod
    def projected(it):
        return PAIRS * (it + 1)

    def w_at(self, it, part, offset, n):
        group = it // NB
        return self.w[:, bass.ds((group % 2) * (2 * B_W) + (part * B_W + offset), n)]

    def pe_unit(self, pe, it, u):
        nc, m = self.m.nc, self.m
        n = self.UNITS * it + u
        if u == self.KT:
            wait(pe, self.rotated, self.NROT * it + self.ROT[self.KV1] + 1)
            wait(pe, self.unit_free, self.bank_free(it, n))
            for t in range(NTT):
                last = nc.tensor.transpose(self.unit_bank(it, u)[:, t * PART:(t + 1) * PART], self.k_row[:, t, :],
                                           m.ident[:])
            last.then_inc(self.unit_full, 1)
            return
        self.wait_src(pe, it)
        wait(pe, self.w_ready, 4 * (it // NB) + 3)
        wait(pe, self.unit_free, self.bank_free(it, n))
        if u in self.Q_OF:
            half, t = self.Q_OF[u]
            col, width = half * 4 * DH, 4 * DH
        else:
            t = self.KV_OF[u]
            col, width = HPI * DH, 2 * DH
        for c in range(NC):
            last = three(nc, self.unit_bank(it, u)[:, 0:width], self.src(it, 0, c, t), self.src(it, 1, c, t),
                         self.w_at(it, 0, c * B_QKV + col, width),
                         self.w_at(it, 1, c * B_QKV + col, width), c == 0, c == NC - 1)
        last.then_inc(self.unit_full, 1)

    def pe_queries_t(self, pe, it, p, P):
        nc, m = self.m.nc, self.m
        half = p // 2
        unit = self.Q01 if half == 0 else self.Q11
        wait(pe, self.rotated, self.NROT * it + self.ROT[unit] + 1)
        wait(pe, self.qt_ready, P)
        for h in range(2):
            head = 2 * (p % 2) + h
            for t in range(NTT):
                at = h * SEQ + t * PART
                last = nc.tensor.transpose(m.qt_ps[:, at:at + PART],
                                           self.q_row[:, half, t, head * DH:(head + 1) * DH], m.ident[:])
        last.then_inc(self.qt_full, 1)

    def pe_wait_keys(self, pe, it, p):
        if p == 0:
            wait(pe, self.kt_ready, it + 1)

    def keys(self, it, part, n):
        return self.kt[:, bass.ds((it % 2) * (2 * SEQ) + part * SEQ, n)]

    def pe_score(self, out, it, p, h, t, width):
        at = h * SEQ + t * PART
        q = lambda part: self.qt[:, p % 2, part, at:at + PART]
        three(self.m.nc, out, q(0), q(1), self.keys(it, 0, width), self.keys(it, 1, width), True, False)

    def pe_values(self, pe, it, p, P):
        nc, m = self.m.nc, self.m
        wait(pe, self.pt_ready, P + 1)
        if p == 0:
            wait(pe, self.v_ready, it + 1)
        wait(pe, self.o_ready, P)
        pt = lambda part: self.prob_t[:, p % 2, part, :]
        three(nc, m.o_ps[:], self.v[:, 0, 0, :], self.v[:, 1, 0, :],
              pt(0)[:, 0:2 * SEQ], pt(1)[:, 0:2 * SEQ], True, False)
        later = m.o_ps[:].rearrange("p (h q) -> p h q", h=2)[:, :, PART:SEQ]
        tail = lambda part: pt(part)[:, 2 * SEQ:2 * PCOLS].rearrange("p (h q) -> p h q", h=2)
        last = three(nc, later, self.v[:, 0, 1, :], self.v[:, 1, 1, :], tail(0), tail(1), False, True)
        last.then_inc(self.pv_done, 1)

    def pe_project(self, pe, it, p, P):
        nc, m = self.m.nc, self.m
        wait(pe, self.o_ready, P + 1)
        if p == 0:
            wait(pe, self.y_added, it + 1)
            wait(pe, self.w_ready, 4 * (it // NB) + 4)
        for h in range(2):
            for t in range(NTT):
                at = h * SEQ + t * PART
                o = lambda part: self.ot[:, p % 2, part, at:at + PART]
                row = B_WQ + (2 * p + h) * D
                last = three(nc, m.y_ps[:, t * D:(t + 1) * D], o(0), o(1), self.w_at(it, 0, row, D),
                             self.w_at(it, 1, row, D), p == 0 and h == 0 and t == 0,
                             p == PAIRS - 1 and h == 1 and t == NTT - 1, skip=True)
        last.then_inc(self.w_done, 1)

    def act_outputs(self, act, it, p, P):
        wait(act, self.pv_done, P + 1)
        wait(act, self.w_done, P - 1)
        self.m.nc.scalar.activation(self.ot[:, p % 2, 0, :], self.m.o_ps[:],
                                    ACT.Copy).then_inc(self.o_hi, 1)

    def dve_outputs(self, dve, it, p, P):
        wait(dve, self.o_hi, P + 1)
        self.m.nc.vector.tensor_tensor(self.ot[:, p % 2, 1, :], self.m.o_ps[:],
                                       self.ot[:, p % 2, 0, :].bitcast(F32),
                                       ALU.subtract).then_inc(self.o_ready, 1)

    def act_values(self, act, it):
        wait(act, self.v_raw, NTT * (it + 1))
        wait(act, self.pv_done, PAIRS * it)
        self.m.nc.scalar.activation(self.v[:, 0, :, :].rearrange("p t n -> p (t n)"),
                                    self.values(it, 0, NTT), ACT.Copy).then_inc(self.v_hi, 1)

    def values(self, it, t, n):
        return self.v_row[:, bass.ds((it % 2) * (NTT * DH) + t * DH, n * DH)]

    def dve_values(self, dve, it):
        wait(dve, self.v_hi, it + 1)
        self.m.nc.vector.tensor_tensor(self.v[:, 1, :, :].rearrange("p t n -> p (t n)"),
                                       self.values(it, 0, NTT),
                                       self.v[:, 0, :, :].rearrange("p t n -> p (t n)").bitcast(F32),
                                       ALU.subtract).then_inc(self.v_ready, 1)

    def act_queries(self, act, it, p, P):
        wait(act, self.qt_full, P + 1)
        wait(act, self.s_full, 2 * P - 2)
        self.m.nc.scalar.activation(self.qt[:, p % 2, 0, :], self.m.qt_ps[:],
                                    ACT.Copy).then_inc(self.qt_hi, 1)

    def dve_queries(self, dve, it, p, P):
        wait(dve, self.qt_hi, P + 1)
        self.m.nc.vector.tensor_tensor(self.qt[:, p % 2, 1, :], self.m.qt_ps[:],
                                       self.qt[:, p % 2, 0, :].bitcast(F32),
                                       ALU.subtract).then_inc(self.qt_ready, 1)

    def act_unit(self, act, it, u):
        nc, m = self.m.nc, self.m
        wait(act, self.unit_full, self.UNITS * it + u + 1)
        if u == self.KT:
            wait(act, self.s_full, 2 * PAIRS * (it - 1))
            nc.scalar.activation(self.keys(it, 0, SEQ), self.unit_bank(it, u)[:, 0:SEQ],
                                 ACT.Copy).then_inc(self.kt_hi, 1)
            return
        r = self.NROT * it + self.ROT[u]
        wait(act, self.rotated, r - 1)
        n = 4 * DH if u in self.Q_OF else DH
        if u in self.KV_OF:
            wait(act, self.v_ready, it - 1)
            nc.scalar.activation(self.values(it, self.KV_OF[u], 1), self.unit_bank(it, u)[:, DH:2 * DH],
                                 ACT.Copy).then_inc(self.v_raw, 1)
        nc.scalar.activation(self.raw[:, self.ROT[u] % 2, 0:n], self.unit_bank(it, u)[:, 0:n],
                             ACT.Copy).then_inc(self.raw_ready, 1)
        act.wait_ge(self.raw_ready, r + 1)
        act.sem_inc(self.unit_free, 1)

    def dve_unit(self, dve, it, u):
        nc, m = self.m.nc, self.m
        if u == self.KT:
            wait(dve, self.kt_hi, it + 1)
            nc.vector.tensor_tensor(self.keys(it, 1, SEQ), self.unit_bank(it, u)[:, 0:SEQ],
                                    self.keys(it, 0, SEQ).bitcast(F32),
                                    ALU.subtract).then_inc(self.kt_ready, 1)
            wait(dve, self.kt_ready, it + 1)
            dve.sem_inc(self.unit_free, 1)
            return
        r = self.NROT * it + self.ROT[u]
        wait(dve, self.raw_ready, r + 1)
        wait(dve, self.rotated, r - 1)
        out, x, factor = self.rotation(u, self.cos_part, 0)
        nc.vector.tensor_tensor(out, x, factor, ALU.mult).then_inc(self.cos_ready, 1)

    def rotation(self, u, product, kind):
        par = self.ROT[u] % 2
        if u in self.Q_OF:
            (_, t), heads, table = self.Q_OF[u], 4, 0
        else:
            t, heads, table = self.KV_OF[u], 1, 2
        halves = lambda x: x[:, par, 0:heads * DH].rearrange("p (h a d) -> p h a d", h=heads, a=2)
        factor = self.m.rope[:, table + kind, t, :].rearrange("p (a d) -> p a d", a=2)
        factor = factor.unsqueeze(1).to_broadcast([PART, heads, 2, DH // 2])
        x = halves(self.raw)
        return halves(product), x[:, :, ::-1, :] if kind else x, factor

    def pool_unit(self, pool, it, u):
        if u == self.KT:
            return
        nc = self.m.nc
        r = self.NROT * it + self.ROT[u]
        par = self.ROT[u] % 2
        wait(pool, self.raw_ready, r + 1)
        wait(pool, self.rotated, r - 1)
        out, x, factor = self.rotation(u, self.sin_part, 1)
        nc.gpsimd.tensor_tensor(out, x, factor, ALU.mult).then_inc(self.sin_ready, 1)
        wait(pool, self.cos_ready, r + 1)
        wait(pool, self.sin_ready, r + 1)
        if u in self.Q_OF:
            half, t = self.Q_OF[u]
            wait(pool, self.qt_full, PAIRS * (it - 1) + 2 * half + 2)
            out, n = self.q_row[:, half, t, :], 4 * DH
        else:
            t = self.KV_OF[u]
            wait(pool, self.unit_full, self.UNITS * (it - 1) + self.KT + 1)
            out, n = self.k_row[:, t, :], DH
        nc.gpsimd.tensor_tensor(out, self.cos_part[:, par, 0:n], self.sin_part[:, par, 0:n],
                                ALU.add).then_inc(self.rotated, 1)

    def quarter(self, it, part=None):
        q = (it % NB) * WQUART
        if part is None:
            return self.w_raw[:, bass.ds(q, WQUART)]
        group = it // NB + 1
        return self.w[:, bass.ds((group % 2) * (2 * B_W) + q + part * B_W, WQUART)]

    def act_weights(self, act, it):
        if not self.more_weights(it):
            return
        wait(act, self.w_loaded, 16 * W_DMAS * (it // NB + 1))
        wait(act, self.w_done, PAIRS * (it - 2) + 1)
        self.m.nc.scalar.activation(self.quarter(it, 0), self.quarter(it), ACT.Copy).then_inc(self.w_hi, 1)

    def slot_pool(self, pool, it, p, units=True):
        if not self.stage(it, p, 0):
            return
        if units:
            for u in self.schedule[p]:
                self.pool_unit(pool, it + 1, u)
        if p == PAIRS - 2 and self.more_weights(it):
            wait(pool, self.w_hi, it + 1)
            self.m.nc.gpsimd.tensor_tensor(self.quarter(it, 1), self.quarter(it),
                                           self.quarter(it, 0).bitcast(F32),
                                           ALU.subtract).then_inc(self.w_ready, 1)

    TAIL = 7

    @staticmethod
    def tail(plan, k):
        for stage, b in plan.get(k, ()):
            stage(b)

    def more_weights(self, it):
        return it < B_ITS - NB if isinstance(it, int) else self.splitting

    def build(self, dram):
        nc, m = self.m.nc, self.m
        middles = ((2, self.ITS - NB), (self.ITS - NB, self.ITS - 1))
        block = self.ctx.enter_context(nc.Block())

        @block.sync
        def _(sp):
            def load_weights(g):
                wait(sp, self.w_ready, 4 * g)
                for dst, src in group_weights(m, dram, g):
                    sp.dma_start(dst, src).then_inc(self.w_loaded, 16)

            def load_batch(it, b):
                if not (isinstance(it, int) and it == self.COPIED):
                    sp.wait_ge(self.unit_full, self.UNITS * it)
                sp.dma_start(self.src_t[:].bitcast(F32), m.act_t[:, b * SLOT:(b + 1) * SLOT].bitcast(F32),
                             ).then_inc(self.src_loaded, 16)

            load_weights(1)
            sp.wait_ge(self.join.turn.lo_done, NB)
            load_batch(3, 3)
            with sp.Fori(1, KV - 1) as g:
                load_batch(NB * g, 0)
                load_batch(NB * g + 1, 1)
                load_weights(g + 1)
                load_batch(NB * g + 2, 2)
                load_batch(NB * g + 3, 3)
            for b in range(NB):
                load_batch(NB * (KV - 1) + b, b)
            sp.wait_ge(self.w_ready, 4 * KV)
            for dst, src in expert_weights(m.e_w_raw, dram, 0):
                sp.dma_start(dst, src).then_inc(self.e_loaded, 16)
            sp.wait_ge(self.src_loaded, 16 * (self.ITS - self.COPIED))

        @block.gpsimd
        def _(pool):
            pool.sem_inc(self.w_ready, 4)
            f_before = {self.KV0: (0, 1), self.Q00: (2,), self.Q10: (3,)}
            for u in range(self.UNITS):
                for b in f_before.get(u, ()):
                    self.join.gpsimd(pool, b)
                self.pool_unit(pool, 0, u)
            self.run(pool, self.slot_pool, middles)
            pool.wait_ge(self.e_hi, 1)
            nc.gpsimd.tensor_tensor(m.e_w[:, 1, :], m.e_w_raw, m.e_w[:, 0, :].bitcast(F32), ALU.subtract)

        def behind(eng, unit):
            def work(s):
                for u in self.BEHIND_STEP.get(s, ()):
                    unit(eng, 0, u)
            return work

        @block.tensor
        def _(pe):
            turn = self.join.turn
            turn.tensor(pe, 0)
            pe.wait_ge(turn.lo_done, 1)
            for s in (3, 4, 5):
                self.pe_unit(pe, 0, self.BEHIND_STEP[s][0])
                turn.tensor(pe, s - 2)
                for u in self.BEHIND_STEP[s][1:]:
                    self.pe_unit(pe, 0, u)
            self.pe_queries_t(pe, 0, 0, 0)
            for u in self.BEHIND_ALL:
                self.pe_unit(pe, 0, u)
            pe.wait_ge(turn.lo_done, NB)

            def turn_h2(b):
                pe.wait_ge(*{0: (self.exp_done, 2 * PAIRS * self.ITS),
                             1: (self.exp_done, 2 * PAIRS * self.ITS),
                             2: (self.qt_ready, PAIRS * self.ITS),
                             3: (self.unit_free, self.UNITS * self.ITS)}[b])
                self.turn2.tensor(pe, b)

            def route(b):
                pe.wait_ge(self.pt_ready, PAIRS * self.ITS)
                pe.wait_ge(self.turn2.lo_done, b + 1)
                router_scores(m, b)

            plan = {4: ((turn_h2, 0), (turn_h2, 1), (turn_h2, 2), (route, 0)),
                    5: ((turn_h2, 3), (route, 1)), 6: ((route, 2),)}
            self.run(pe, self.slot_pe, middles, lambda k: self.tail(plan, k))
            for k in range(self.DRAIN, self.TAIL):
                self.tail(plan, k)

        @block.scalar
        def _(act):
            def work(s, units=behind(act, self.act_unit)):
                units(s)
                if s == 4:
                    m.load_table(act, ACT.Exp)

            pipeline(self.join.scalar(act), work)
            self.act_queries(act, 0, 0, 0)
            for u in self.BEHIND_ALL:
                self.act_unit(act, 0, u)
            acc = m.acc[:].rearrange("p (t d) -> p t d", t=NT)

            roots = lambda b: self.norm2.roots(act, b)

            def rows(b):
                for t in range(NTT * b, NTT * (b + 1)):
                    last = self.norm2.apply(act, self.turn2.src[:, t, :], acc[:, t, :], t)
                last.then_inc(self.turn2.rows_ready, 1)

            def turn(b):
                if b == NB - 1:
                    m.load_table(act, ACT.Sigmoid)
                self.turn2.scalar(act, b)

            plan = {1: ((roots, 0), (roots, 1), (roots, 2)), 3: ((rows, 0), (rows, 1), (rows, 2)),
                    4: ((turn, 0), (turn, 1), (roots, 3)), 5: ((rows, 3), (turn, 2)), 6: ((turn, 3),)}

            def after(k):
                self.tail(plan, k)
                if k == 1:
                    act.wait_ge(self.e_loaded, 16 * len(expert_weights(m.e_w_raw, dram, 0)))
                    act.wait_ge(self.w_done, PAIRS * (self.ITS - NB))
                    nc.scalar.activation(m.e_w[:, 0, :], m.e_w_raw, ACT.Copy).then_inc(self.e_hi, 1)

            self.run(act, self.slot_act, middles, after)
            for k in range(self.DRAIN, self.TAIL):
                self.tail(plan, k)

        @block.vector
        def _(dve):
            pipeline(self.join.vector(dve), behind(dve, self.dve_unit))
            self.dve_queries(dve, 0, 0, 0)
            for u in self.BEHIND_ALL:
                self.dve_unit(dve, 0, u)
            acc = m.acc[:].rearrange("p (t d) -> p t d", t=NT)

            def arrived(t):
                dve.wait_ge(self.y_added, self.ITS - NB + t // NTT + 2)

            moments = lambda b: self.norm2.moments(dve, b, lambda t: acc[:, t, :], arrived)
            factors = lambda b: self.norm2.factors(dve, b)
            turn = lambda b: self.turn2.vector(dve, b)
            plan = {0: ((moments, 0), (moments, 1)), 1: ((moments, 2),),
                    2: ((factors, 0), (factors, 1), (factors, 2)), 4: ((moments, 3), (turn, 0)),
                    5: ((factors, 3), (turn, 1)), 6: ((turn, 2), (turn, 3))}
            dve.wait_ge(self.join.f_ready, NB)
            dve.sem_inc(self.y_added, 1)
            self.run(dve, self.slot_dve, middles, lambda k: self.tail(plan, k))
            for k in range(self.DRAIN, self.TAIL):
                self.tail(plan, k)




class Join:

    def __init__(self, m, ctx, rows):
        self.m, self.rows = m, rows
        self.norm_a = m.norm_a
        self.norm_f = Norm(m, ctx, "ln_f", Norm.LN_AND_RMS)
        self.turn = Turn(m, ctx, "h", rows, m.act_t, weight=m.lnw[:, 0, :])
        self.acc = m.acc[:].rearrange("p (t d) -> p t d", t=NT)
        self.attn_ready = m.sem("attn_ready", ctx=ctx)
        self.x1_ready = m.sem("x1_ready", ctx=ctx)
        self.f_ready = m.sem("f_ready", ctx=ctx)

    def vector(self, dve):
        x, acc, norm_a, norm_f = self.m.x, self.acc, self.norm_a, self.norm_f

        def add(b):
            dve.wait_ge(self.attn_ready, b + 1)
            rows = slice(NTT * b, NTT * (b + 1))
            self.m.nc.vector.tensor_tensor(x[:, rows, :], x[:, rows, :], self.rows[:, rows, :],
                                           ALU.add).then_inc(self.x1_ready, 1)

        def arrived(t):
            dve.wait_ge(self.x1_ready, t // NTT + 1)

        def last_attention(s):
            if s == 0:
                norm_a.moments(dve, NB - 1, lambda t: acc[:, t, :])
            elif s == 1:
                norm_a.factors(dve, NB - 1)

        return ((3, lambda b: self.turn.vector(dve, b)), (2, lambda b: norm_f.factors(dve, b)),
                (1, add), (1, lambda b: norm_f.moments(dve, b, lambda t: x[:, t, :], arrived)),
                (0, last_attention))

    def scalar(self, act):
        def attention(b):
            for t in range(NTT * b, NTT * (b + 1)):
                last = self.norm_a.apply(act, self.rows[:, t, :], self.acc[:, t, :], t)
            last.then_inc(self.attn_ready, 1)

        def ffn_input(b):
            for t in range(NTT * b, NTT * (b + 1)):
                last = self.norm_f.apply(act, self.rows[:, t, :], self.m.x[:, t, :], t, 1)
            last.then_inc(self.turn.rows_ready, 1)

        def last_attention(s):
            if s == 0:
                self.norm_a.roots(act, NB - 1)

        return ((3, lambda b: self.turn.scalar(act, b)), (2, ffn_input),
                (1, lambda b: self.norm_f.roots(act, b)), (0, attention), (0, last_attention))

    def gpsimd(self, pool, b):
        m, norm = self.m, self.norm_f
        pool.wait_ge(norm.ready, b + 1)
        for t in range(NTT * b, NTT * (b + 1)):
            last = m.nc.gpsimd.tensor_scalar(self.acc[:, t, :], m.x[:, t, :],
                                             norm.factor[:, 0, t:t + 1], norm.shift[:, 0, t:t + 1],
                                             ALU.mult, ALU.add)
        last.then_inc(self.f_ready, 1)




def router_scores(m, b):
    act_b = m.act_t[:].rearrange("p (b n) -> p b n", b=NB)
    for t in range(NTT):
        out = m.banks[:, 3, (NTT * b + t) * NE:(NTT * b + t + 1) * NE]
        for c in range(NC):
            tokens = lambda part: act_b[:, b, part * NC * SEQ + c * SEQ + t * PART:][:, 0:PART]
            last = three(m.nc, out, tokens(0), tokens(1), m.wr[:, 0, c, :], m.wr[:, 1, c, :],
                         c == 0, c == NC - 1)
    return last


UP = 2 * NC * FF


def expert_weights(raw, dram, e):
    gu_view = raw[:, 0:UP].rearrange("p (j c i) -> p j c i", j=2, c=NC)
    if isinstance(e, int) and e == 0:
        src = [dram[n].rearrange("(c p) i -> p c i", p=PART) for n in ("wsg", "wsu")]
        down = dram["wsd"]
    else:
        src = [dram[n][bass.ds(e - 1, 1), :, :].rearrange("e (c p) i -> p (e c) i", p=PART)
               for n in ("wg", "wu")]
        down = dram["wd"][bass.ds(e - 1, 1), :, :].rearrange("e p d -> p (e d)")
    return [(gu_view[:, 0, :, :], src[0]), (gu_view[:, 1, :, :], src[1]), (raw[:, UP:EW], down)]


def experts(m, dram):
    nc = m.nc
    m.tag = "moe_"
    half = NT * PART // 2
    steps = 2 * (NE + 1)
    with ExitStack() as ctx:
        sb = lambda name, shape, dt=F32: m.sb(name, shape, dt, ctx=ctx)
        sem = lambda name: m.sem(name, ctx=ctx)
        score = sb("score", [PART, NT, NE])
        biased = sb("biased", [PART, NT, NE])
        best = sb("best", [PART, NT, TOPK])
        struck = sb("struck", [PART, NT, NE])
        gate = sb("gate", [PART, NT, NE])
        gsum = sb("gsum", [PART, NT])
        gate_t = sb("gate_t", [NE, NT * PART])
        w_raw = [m.e_w_raw, sb("w_raw1", [PART, EW])[:]]
        w = [m.e_w, sb("w1", [PART, 2, EW], F32R)[:]]
        share = [sb(f"share{i}", [PART, NT * PART]) for i in range(2)]
        silu = [sb(f"silu{i}", [PART, half]) for i in range(2)]
        scaled = [sb(f"scaled{i}", [PART, half]) for i in range(2)]
        hidden = [sb(f"hidden{i}", [PART, half]) for i in range(2)]
        hid = [sb(f"hid{i}", [PART, 2, half], F32R) for i in range(2)]
        final = Norm(m, ctx, "ln_o")

        routed, sigmoid_done, route = sem("routed"), sem("sigmoid_done"), sem("route")
        gates_ready = sem("gates_ready")
        gate_turned, gate_copied, gate_out = sem("gate_turned"), sem("gate_copied"), sem("gate_out")
        w_loaded = [sem(f"w_loaded{i}") for i in range(2)]
        share_loaded = [sem(f"share_loaded{i}") for i in range(2)]
        ones_ready = sem("ones_ready")
        up_hi, up_ready = sem("up_hi"), sem("up_ready")
        dn_hi, dn_ready = sem("dn_hi"), sem("dn_ready")
        gu_full = sem("gu_full")
        silu_done = sem("silu_done")
        scaled_done = sem("scaled_done")
        hidden_done = sem("hidden_done")
        hid_hi = sem("hid_hi")
        hid_ready = sem("hid_ready")
        down_done = sem("down_done")
        ended = sem("ended")
        ln_done = sem("ln_done")
        added, last_added = sem("added"), sem("last_added")
        out_done = sem("out_done")

        acc = m.acc[:].rearrange("p (t d) -> p t d", t=NT)
        gu = [[m.banks[:, 2 * i + j, :] for j in range(2)] for i in range(2)]
        sums = m.banks[:, 4:8, :].rearrange("p k (a d) -> p (k a) d", a=2)
        act_b = m.act_t[:].rearrange("p (b n) -> p b n", b=NB)
        UP = 2 * NC * FF

        def half_tokens(part, c, n):
            at = part * NC * SEQ + c * SEQ
            return act_b[:, NB // 2 * n:NB // 2 * (n + 1), at:at + SEQ]

        block = ctx.enter_context(nc.Block())

        @block.sync
        def _(sp):
            def load(e, par):
                wait(sp, dn_ready, e - 1)
                for dst, src in expert_weights(w_raw[par], dram, e):
                    sp.dma_start(dst, src).then_inc(w_loaded[par], 16)

            def load_share(e, par):
                wait(sp, scaled_done, 2 * (e - 1))
                row = dram["gates"][bass.ds(e - 1, 1), :].to_broadcast([PART, NT * PART])
                sp.dma_start(share[par][:], row).then_inc(share_loaded[par], 16)

            sp.sem_inc(w_loaded[0], 16 * 3)
            load(1, 1)
            sp.wait_ge(gate_copied, 1)
            sp.dma_start(dram["gates"], gate_t[:]).then_inc(gate_out, 16)
            sp.wait_ge(gate_out, 16)
            load_share(1, 1)
            load(2, 0)
            with sp.Fori(0, NE // 2 - 1) as j:
                for k in range(2):
                    load_share(2 * j + 2 + k, k)
                    load(2 * j + 3 + k, 1 - k)
            load_share(NE, 0)
            sp.wait_ge(share_loaded[0], 16 * (NE // 2))
            for b in range(NB):
                if b < NB - 1:
                    sp.wait_ge(added, b + 1)
                else:
                    sp.wait_ge(last_added, 1)
                sp.dma_start(dram["out"].rearrange("b (t p) d -> b p t d", p=PART)[b],
                             m.rows[:, NTT * b:NTT * (b + 1), :]).then_inc(out_done, 16)
            sp.wait_ge(out_done, 16 * NB)


        def pe_up(pe, e, n, par, between=None):
            H = 2 * e + n
            if n == 0:
                wait(pe, up_ready, e + 1)
            wait(pe, hidden_done, H - 1)
            for j in range(2):
                for c in range(NC):
                    at = (j * NC + c) * FF
                    last = three(nc, gu[n][j], w[par][:, 0, at:at + FF], w[par][:, 1, at:at + FF],
                                 half_tokens(0, c, n), half_tokens(1, c, n), c == 0, c == NC - 1)
                if between and j == 0:
                    between()
            last.then_inc(gu_full, 1)

        def pe_down(pe, e, n, par, first=False, end=False):
            H = 2 * e + n
            wait(pe, dn_ready, e + 1)
            wait(pe, hid_ready, H + 1)
            for t in range(NT // 2):
                last = three(nc, sums[:, n * (NT // 2) + t, :],
                             hid[n][:, 0, t * PART:(t + 1) * PART], hid[n][:, 1, t * PART:(t + 1) * PART],
                             w[par][:, 0, UP:EW], w[par][:, 1, UP:EW],
                             first and t % 2 == 0, end and t % 2 == 1, skip=True)
            last.then_inc(down_done, 1)

        @block.tensor
        def _(pe):
            pe.sem_inc(down_done, 1)
            router_scores(m, NB - 1).then_inc(routed, 1)
            pe_up(pe, 0, 0, 0)
            pe.wait_ge(sigmoid_done, 1)

            def turn_gates():
                pe.wait_ge(gates_ready, 1)
                for t in range(NT):
                    last = nc.tensor.transpose(
                        m.banks[0:NE, 4 + t // 4, (t % 4) * PART:(t % 4 + 1) * PART], gate[:, t, :],
                        m.ident[:])
                last.then_inc(gate_turned, 1)

            pe_up(pe, 0, 1, 0, turn_gates)
            for n in range(2):
                pe_up(pe, 1, n, 1)
                pe.wait_ge(gate_copied, 1)
                pe_down(pe, 0, n, 0, first=True)
            with pe.Fori(0, NE // 2 - 1) as j:
                for k in range(2):
                    for n in range(2):
                        pe_up(pe, 2 * j + 2 + k, n, k)
                        pe_down(pe, 2 * j + 1 + k, n, 1 - k)
            for n in range(2):
                pe_up(pe, NE, n, 0)
                pe_down(pe, NE - 1, n, 1)
            for n in range(2):
                pe_down(pe, NE, n, 0, end=True)


        def act_split_up(act, e, par, k):
            wait(act, w_loaded[par], 16 * 3 * (k + 1))
            wait(act, gu_full, 2 * (e - 1))
            nc.scalar.activation(w[par][:, 0, 0:UP], w_raw[par][:, 0:UP], ACT.Copy).then_inc(up_hi, 1)

        def act_split_down(act, e, par):
            wait(act, down_done, 2 * (e - 1) + 1)
            nc.scalar.activation(w[par][:, 0, UP:EW], w_raw[par][:, UP:EW], ACT.Copy).then_inc(dn_hi, 1)

        def act_silu(act, e, n):
            H = 2 * e + n
            wait(act, gu_full, H + 1)
            wait(act, scaled_done, H - 1)
            nc.scalar.activation(silu[n][:], gu[n][0], ACT.Silu).then_inc(silu_done, 1)

        def act_hidden(act, e, n):
            H = 2 * e + n
            wait(act, hidden_done, H + 1)
            wait(act, down_done, H)
            nc.scalar.activation(hid[n][:, 0, :], hidden[n][:], ACT.Copy).then_inc(hid_hi, 1)

        def act_expert(act, e, par, k):
            act_silu(act, e, 0)
            act_hidden(act, e - 1, 1)
            act_split_down(act, e, par)
            if k is not None:
                act_split_up(act, e + 1, 1 - par, k)
            act_silu(act, e, 1)
            act_hidden(act, e, 0)

        @block.scalar
        def _(act):
            act.sem_inc(up_hi, 1)
            act.sem_inc(dn_hi, 1)
            act.wait_ge(routed, 1)
            nc.scalar.activation(score[:].rearrange("p t e -> p (t e)"), gu[1][1][:, 0:NT * NE],
                                 ACT.Sigmoid).then_inc(sigmoid_done, 1)
            act_split_up(act, 1, 1, 0)
            act_silu(act, 0, 0)
            act.wait_ge(gate_turned, 1)
            for i in range(2):
                last = nc.scalar.activation(gate_t[:, i * half:(i + 1) * half], m.banks[0:NE, 4 + i, :],
                                            ACT.Copy)
            last.then_inc(gate_copied, 1)
            act_silu(act, 0, 1)
            act_hidden(act, 0, 0)
            with act.Fori(0, NE // 2 - 1) as j:
                for k in range(2):
                    act_expert(act, 2 * j + 1 + k, 1 - k, j + 1)
            act_expert(act, NE - 1, 1, NE // 2)
            act_expert(act, NE, 0, None)
            act_hidden(act, NE, 1)

            def output(b):
                for t in range(NTT * b, NTT * (b + 1)):
                    last = final.apply(act, m.rows[:, t, :], acc[:, t, :], t)
                last.then_inc(ln_done, 1)

            pipeline(((1, lambda b: b < NB - 1 and output(b)), (0, lambda b: final.roots(act, b))))


        def pool_split_up(pool, e, par):
            wait(pool, up_hi, e + 1)
            nc.gpsimd.tensor_tensor(w[par][:, 1, 0:UP], w_raw[par][:, 0:UP],
                                    w[par][:, 0, 0:UP].bitcast(F32), ALU.subtract).then_inc(up_ready, 1)

        def pool_split_down(pool, e, par):
            wait(pool, dn_hi, e + 1)
            nc.gpsimd.tensor_tensor(w[par][:, 1, UP:EW], w_raw[par][:, UP:EW],
                                    w[par][:, 0, UP:EW].bitcast(F32), ALU.subtract).then_inc(dn_ready, 1)

        def pool_scale(pool, e, n, par):
            H = 2 * e + n
            wait(pool, silu_done, H + 1)
            wait(pool, hidden_done, H - 1)
            nc.gpsimd.tensor_tensor(scaled[n][:], silu[n][:], share[par][:, n * half:(n + 1) * half],
                                    ALU.mult).then_inc(scaled_done, 1)

        def pool_expert(pool, e, par, k, more=True):
            wait(pool, share_loaded[par], 16 * k)
            pool_scale(pool, e, 0, par)
            pool_split_down(pool, e, par)
            if more:
                pool_split_up(pool, e + 1, 1 - par)
            pool_scale(pool, e, 1, par)

        @block.gpsimd
        def _(pool):
            nc.gpsimd.memset(share[0][:], 1.0).then_inc(ones_ready, 1)
            pool.sem_inc(up_ready, 1)
            pool.sem_inc(dn_ready, 1)
            pool.wait_ge(ones_ready, 1)
            pool_scale(pool, 0, 0, 0)
            pool_split_up(pool, 1, 1)
            pool_scale(pool, 0, 1, 0)
            with pool.Fori(0, NE // 2 - 1) as j:
                for k in range(2):
                    pool_expert(pool, 2 * j + 1 + k, 1 - k, j + 1)
            pool_expert(pool, NE - 1, 1, NE // 2)
            pool_expert(pool, NE, 0, NE // 2, more=False)
            for b in range(NB - 1):
                pool.wait_ge(ln_done, b + 1)
                rows = slice(NTT * b, NTT * (b + 1))
                nc.gpsimd.tensor_tensor(m.rows[:, rows, :], m.rows[:, rows, :], m.x[:, rows, :],
                                        ALU.add).then_inc(added, 1)


        def dve_hidden(dve, e, n):
            H = 2 * e + n
            wait(dve, scaled_done, H + 1)
            wait(dve, hid_ready, H - 1)
            nc.vector.tensor_tensor(hidden[n][:], gu[n][1], scaled[n][:], ALU.mult).then_inc(hidden_done, 1)

        def dve_split(dve, e, n):
            H = 2 * e + n
            wait(dve, hid_hi, H + 1)
            nc.vector.tensor_tensor(hid[n][:, 1, :], hidden[n][:], hid[n][:, 0, :].bitcast(F32),
                                    ALU.subtract).then_inc(hid_ready, 1)

        def dve_expert(dve, e):
            dve_hidden(dve, e, 0)
            dve_split(dve, e - 1, 1)
            dve_hidden(dve, e, 1)
            dve_split(dve, e, 0)

        def dve_route(dve):
            n = [0]

            def link(instruction):
                n[0] += 1
                instruction.then_inc(route, 1)
                return n[0]

            dve.wait_ge(sigmoid_done, 1)
            rows_bias = m.bias[:].unsqueeze(1).to_broadcast([PART, NT, NE])
            at = link(nc.vector.tensor_tensor(biased[:], score[:], rows_bias, ALU.add))
            dve.wait_ge(route, at)
            for t in range(NT):
                at = link(nc.vector.max(best[:, t, :], biased[:, t, :]))
            for t in range(NT):
                dve.wait_ge(route, at - NT + t + 1)
                last = link(nc.vector.match_replace(struck[:, t, :], best[:, t, :], biased[:, t, :], NEG))
            dve.wait_ge(route, last)
            at = link(nc.vector.tensor_tensor(gate[:], struck[:], biased[:], ALU.not_equal))
            dve.wait_ge(route, at)
            at = link(nc.vector.tensor_tensor(gate[:], gate[:], score[:], ALU.mult))
            dve.wait_ge(route, at)
            at = link(nc.vector.reduce_sum(gsum[:], gate[:], AX))
            dve.wait_ge(route, at)
            at = link(nc.vector.reciprocal(gsum[:], gsum[:]))
            dve.wait_ge(route, at)
            nc.vector.tensor_tensor(gate[:], gate[:], gsum[:].unsqueeze(2).to_broadcast([PART, NT, NE]),
                                    ALU.mult).then_inc(gates_ready, 1)

        @block.vector
        def _(dve):
            dve_route(dve)
            dve_hidden(dve, 0, 0)
            dve_hidden(dve, 0, 1)
            dve_split(dve, 0, 0)
            with dve.Fori(1, NE + 1) as e:
                dve_expert(dve, e)
            dve_split(dve, NE, 1)

            def total(b):
                dve.wait_ge(down_done, steps if b < NB // 2 else steps + 1)
                rows = slice(NTT * b, NTT * (b + 1))
                nc.vector.tensor_tensor(acc[:, rows, :], sums[:, rows, :], acc[:, rows, :],
                                        ALU.add).then_inc(ended, 1)

            def arrived(t):
                dve.wait_ge(ended, t // NTT + 1)

            pipeline(((0, total), (1, lambda b: final.factors(dve, b)),
                      (0, lambda b: final.moments(dve, b, lambda t: acc[:, t, :], arrived))))
            dve.wait_ge(final.ready, NB)
            for t in range(NTT * (NB - 1), NT):
                at = final.link(nc.vector.tensor_scalar(m.rows[:, t, :], acc[:, t, :],
                                                        final.factor[:, 0, t:t + 1],
                                                        final.shift[:, 0, t:t + 1], ALU.mult, ALU.add))
            dve.wait_ge(final.step, at)
            rows = slice(NTT * (NB - 1), NT)
            nc.vector.tensor_tensor(m.rows[:, rows, :], m.rows[:, rows, :], m.x[:, rows, :],
                                    ALU.add).then_inc(last_added, 1)




def program(nc, dram):
    with ExitStack() as ctx:
        m = Machine(nc, ctx)
        m.banks = ctx.enter_context(nc.psum_tensor("banks", [PART, 8, 512], F32))
        m.s_ps = m.banks[:, 0:2, :]
        m.pt_ps = m.banks[:, 2:4, :].rearrange("p k n -> p (k n)")
        m.qt_ps, m.pj_ps, m.o_ps, m.y_ps = (m.banks[:, 4 + i, :] for i in range(4))
        m.ident = m.sb("ident", [PART, PART])
        m.ident16 = m.sb("ident16", [PART, PART], BF16)
        m.mask = m.sb("mask", [PART, PART], BF16)
        m.rope = m.sb("rope_sb", [PART, 4, NTT, DH])
        m.lnw = m.sb("lnw", [PART, 2, NC])
        m.spare = m.sb("spare", [PART, 8])
        m.x = m.sb("x", [PART, NT, D])
        m.acc = m.sb("acc", [PART, NT * D])
        m.act_t = m.sb("act_t", [PART, NB * SLOT], F32R)
        m.wr_raw = m.sb("wr_raw", [PART, NC, NE])
        m.wr = m.sb("wr", [PART, 2, NC, NE], F32R)
        m.bias = m.sb("bias", [PART, NE])
        m.b_w = m.sb("b_w", [PART, 2 * 2 * B_W], F32R)
        m.b_w_raw = m.sb("b_w_raw", [PART, B_W])[:]
        m.e_w_raw = m.b_w_raw[:, 0:EW]
        m.e_w = m.b_w[:, 0:2 * EW].rearrange("p (s n) -> p s n", s=2)
        m.norm_a = Norm(m, ctx, "ln_a")
        with ExitStack() as early:
            m.rows = m.acc[:].rearrange("p (t d) -> p t d", t=NT)
            m.a_wqkv = m.sb("a_wqkv", [PART, 2 * 2 * NC * A_QKV], F32R, ctx=early)
            m.a_wo = m.sb("a_wo", [PART, 2 * NC * D], F32R, ctx=early)
            m.q_stack = m.sb("a_q_stack", [PART, 2 * NTT * HPI * PART], F32R, ctx=early)
            prepare(m, dram)
            with ExitStack() as stage:
                AttentionA(m, stage).build(dram)
        with ExitStack() as stage:
            AttentionB(m, stage).build(dram)
        with ExitStack() as late:
            m.tag = ""
            m.rows = m.sb("rows2", [PART, NT, D], ctx=late)
            experts(m, dram)



_NAMES = {
    "x": "L0_attn_x", "a_wq": "L0_attn_Wq", "a_wk": "L0_attn_Wk", "a_wv": "L0_attn_Wv",
    "a_wo": "L0_attn_Wo", "ln1_w": "L0_ffn_ln1_w", "ln2_w": "L0_ffn_ln2_w", "b_wq": "L0_ffn_Wq",
    "b_wk": "L0_ffn_Wk", "b_wv": "L0_ffn_Wv", "b_wo": "L0_ffn_Wo", "wr": "L0_ffn_Wr",
    "expert_bias": "L0_ffn_expert_bias", "wg": "L0_ffn_Wg", "wu": "L0_ffn_Wu", "wd": "L0_ffn_Wd",
    "wsg": "L0_ffn_Wsg", "wsu": "L0_ffn_Wsu", "wsd": "L0_ffn_Wsd",
}


def rope_tables():
    freq = (np.float32(1.0) / np.float32(10000.0) ** (np.arange(0, DH, 2, dtype=np.float32) / np.float32(DH)))
    angle = (np.arange(SEQ, dtype=np.float32)[:, None] * freq[None, :]).astype(np.float64)
    cos, sin = np.cos(angle), np.sin(angle)
    tables = np.stack([np.concatenate([cos, cos], 1), np.concatenate([-sin, sin], 1)])
    both = np.concatenate([tables / np.sqrt(float(DH)), tables]).astype(np.float32)
    return np.ascontiguousarray(both.reshape(4, NTT, PART, DH).transpose(2, 0, 1, 3))


def kernel(**inputs):
    import concourse.bacc as bacc
    from concourse.bass_utils import run_bass_kernel_spmd

    nc = bacc.Bacc("TRN2", target_bir_lowering=False, num_devices=1)
    arrays, dram = {}, {}
    for name, source in _NAMES.items():
        a = np.ascontiguousarray(inputs[source])
        arrays["in_" + name] = a
        dram[name] = nc.dram_tensor("in_" + name, a.shape, F32, kind="ExternalInput").ap()
    arrays["rope"] = rope_tables()
    dram["rope"] = nc.dram_tensor("rope", arrays["rope"].shape, F32, kind="ExternalInput").ap()
    dram["gates"] = nc.dram_tensor("gates", (NE, NT * PART), F32, kind="Internal").ap()
    dram["out"] = nc.dram_tensor("out", (NB, SEQ, D), F32, kind="ExternalOutput").ap()
    program(nc, dram)
    result = run_bass_kernel_spmd(nc, [arrays], core_ids=[0])
    return result.results[0]["out"]
```
